# Optimizing a Trainium2 kernel written in Bass

```python
import numpy as np
import jax
import jax.numpy as jnp

def _softmax(x, axis=-1):
    return jax.nn.softmax(x, axis=axis)

def _gelu(x):
    return jax.nn.gelu(x, approximate=True)

def _silu(x):
    return jax.nn.silu(x)

def _sigmoid(x):
    return jax.nn.sigmoid(x)

def _layernorm(x, axis=-1, eps=1e-05):
    m = jnp.mean(x, axis=axis, keepdims=True)
    v = jnp.var(x, axis=axis, keepdims=True)
    return (x - m) / jnp.sqrt(v + eps)

def _scatter_add(tgt, idx, src, axis=0):
    return tgt.at[idx].add(src)

def _segment_sum(src, seg, n):
    return jax.ops.segment_sum(src, seg, n)
kernel_name = 'mk_perceiver_d1_seqx_r8_2a6f53'

def setup_inputs(seed: int=0):
    np.random.seed(seed)
    _w = jnp.asarray

    def _rec_inputs():
        import jax
        import jax.numpy as jnp
        _rk = jax.random.key(seed)
        x = -0.000125 + 0.9999 * jax.random.normal(jax.random.fold_in(_rk, 1), (32, 64, 256), jnp.float32)
        _lenS = 64 - jax.random.randint(jax.random.fold_in(_rk, 7), (32,), 0, max(1, 64 // 4) + 1, jnp.int32)
        _lenS2 = 1601 - jax.random.randint(jax.random.fold_in(_rk, 8), (32,), 0, max(1, 1601 // 4) + 1, jnp.int32)
        _ctx_2048P = jax.random.normal(jax.random.fold_in(_rk, 11), (32, 16, 256), jnp.float32)
        _ctx_2048c = jax.random.dirichlet(jax.random.fold_in(_rk, 511), 0.3 * jnp.ones((16,), jnp.float32), (32, 1601))
        _ctx_2048t = jnp.einsum('bsk,bkd->bsd', _ctx_2048c, _ctx_2048P)
        _ctx_2048t = _ctx_2048t * jax.lax.rsqrt(jnp.mean(jnp.square(_ctx_2048t)) + 1e-12) * 0.953939
        ctx_2048 = -0.000514642 + 1.00011 * (_ctx_2048t + 0.3 * jax.random.normal(jax.random.fold_in(_rk, 611), (32, 1601, 256), jnp.float32))
        _validS = jnp.arange(64)[None, :] < _lenS[:, None]
        _validS2 = jnp.arange(1601)[None, :] < _lenS2[:, None]
        _causal = jnp.tril(jnp.ones((64, 64), dtype=bool))
        mask_BxS2_bk0 = jnp.logical_not(jnp.broadcast_to(_validS2[:, :], (32, 1601)))
        return (x, ctx_2048, mask_BxS2_bk0)
    x, ctx_2048, mask_BxS2_bk0 = _rec_inputs()

    def _L0_xattn_setup():
        import jax, jax.numpy as jnp
        import numpy as np
        key = jax.random.key(seed)
        k1, k2, k3 = jax.random.split(key, 3)
        B, S, D, M = (8, 256, 256, 128)
        hidden_states = jax.random.normal(k1, (B, S, D), dtype=jnp.float32)
        memory_tokens = jax.random.normal(k2, (B, M, D), dtype=jnp.float32)
        memory_mask = jax.random.randint(k3, (B, M), 0, 2).astype(jnp.bool_)
        return {'hidden_states': hidden_states, 'memory_tokens': memory_tokens, 'memory_mask': memory_mask}
    _L0_xattn_all = _L0_xattn_setup()
    _L0_xattn_in = {k: v for k, v in _L0_xattn_all.items() if k in ()}
    del _L0_xattn_all

    def _L0_attn_setup():
        import jax, jax.numpy as jnp
        import numpy as np
        from jax import lax
        HIDDEN = 256
        INTER = 512
        NHEADS = 64
        HEADDIM = INTER // NHEADS
        STATE = 128
        NGROUPS = 1
        CONVK = 4
        CHUNK = 32
        CONV_DIM = INTER + 2 * NGROUPS * STATE
        EPS = 1e-05
        DT_MIN, DT_MAX = (0.0, 100.0)

        def _segsum(x):
            l = x.shape[-1]
            xx = jnp.broadcast_to(x[..., None], x.shape + (l,))
            m1 = jnp.tril(jnp.ones((l, l), bool), -1)
            s = jnp.cumsum(jnp.where(m1, xx, 0.0), axis=-2)
            m2 = jnp.tril(jnp.ones((l, l), bool), 0)
            return jnp.where(m2, s, -jnp.inf)
        key = jax.random.key(seed)
        ks = jax.random.split(key, 4)
        B, S = (1, 512)
        std = 0.02
        return {'hidden_states': jax.random.normal(ks[0], (B, S, HIDDEN), jnp.float32), 'in_proj_w': jax.random.normal(ks[1], (INTER + CONV_DIM + NHEADS, HIDDEN), jnp.float32) * std, 'conv_w': jax.random.normal(ks[2], (CONV_DIM, 1, CONVK), jnp.float32) * std, 'conv_b': jnp.zeros((CONV_DIM,), jnp.float32), 'dt_bias': jnp.ones((NHEADS,), jnp.float32), 'A_log': jnp.log(jnp.arange(1, NHEADS + 1, dtype=jnp.float32)), 'D': jnp.ones((NHEADS,), jnp.float32), 'norm_w': jnp.ones((INTER,), jnp.float32), 'out_proj_w': jax.random.normal(ks[3], (HIDDEN, INTER), jnp.float32) * std}
    _L0_attn_all = _L0_attn_setup()
    _L0_attn_in = {k: v for k, v in _L0_attn_all.items() if k in ('in_proj_w', 'conv_w', 'conv_b', 'dt_bias', 'A_log', 'D', 'norm_w', 'out_proj_w')}
    del _L0_attn_all

    def _L0_ffn_setup():
        import jax, jax.numpy as jnp
        import numpy as np
        NUM_EXPERTS = 32
        TOP_K = 8
        THRESHOLD = 0.8
        HIDDEN = 256
        INTER = 96
        key = jax.random.key(seed)
        k1, k2, k3, k4 = jax.random.split(key, 4)
        hidden_states = jax.random.normal(k1, (2, 128, HIDDEN), jnp.float32)
        gate_weight = jax.random.normal(k2, (NUM_EXPERTS, HIDDEN), jnp.float32) * 0.02
        gate_up_proj = jax.random.normal(k3, (NUM_EXPERTS, 2 * INTER, HIDDEN), jnp.float32) * 0.02
        down_proj = jax.random.normal(k4, (NUM_EXPERTS, HIDDEN, INTER), jnp.float32) * 0.02
        return {'hidden_states': hidden_states, 'gate_weight': gate_weight, 'gate_up_proj': gate_up_proj, 'down_proj': down_proj}
    _L0_ffn_all = _L0_ffn_setup()
    _L0_ffn_in = {k: v for k, v in _L0_ffn_all.items() if k in ('gate_weight', 'gate_up_proj', 'down_proj')}
    del _L0_ffn_all
    return {'x': x, 'ctx_2048': ctx_2048, 'mask_BxS2_bk0': mask_BxS2_bk0, 'L0_attn_in_proj_w': _L0_attn_in['in_proj_w'], 'L0_attn_conv_w': _L0_attn_in['conv_w'], 'L0_attn_conv_b': _L0_attn_in['conv_b'], 'L0_attn_dt_bias': _L0_attn_in['dt_bias'], 'L0_attn_A_log': _L0_attn_in['A_log'], 'L0_attn_D': _L0_attn_in['D'], 'L0_attn_norm_w': _L0_attn_in['norm_w'], 'L0_attn_out_proj_w': _L0_attn_in['out_proj_w'], 'L0_ffn_gate_weight': _L0_ffn_in['gate_weight'], 'L0_ffn_gate_up_proj': _L0_ffn_in['gate_up_proj'], 'L0_ffn_down_proj': _L0_ffn_in['down_proj']}

def reference(x, ctx_2048, mask_BxS2_bk0, L0_attn_in_proj_w, L0_attn_conv_w, L0_attn_conv_b, L0_attn_dt_bias, L0_attn_A_log, L0_attn_D, L0_attn_norm_w, L0_attn_out_proj_w, L0_ffn_gate_weight, L0_ffn_gate_up_proj, L0_ffn_down_proj):
    import jax
    import jax.numpy as jnp

    def _L0_xattn_ref(hidden_states, memory_tokens, memory_mask):
        import jax, jax.numpy as jnp
        import numpy as np
        B, S, D = hidden_states.shape
        scale = 1.0 / jnp.sqrt(jnp.asarray(D, hidden_states.dtype))
        scores = jnp.einsum('bsd,bmd->bsm', hidden_states, memory_tokens) * scale
        neg_inf = jnp.asarray(-1e+30, scores.dtype)
        scores = jnp.where(memory_mask[:, None, :], scores, neg_inf)
        attn = jax.nn.softmax(scores, axis=-1)
        readout = jnp.einsum('bsm,bmd->bsd', attn, memory_tokens)
        valid_b = jnp.any(memory_mask, axis=-1)
        out = jnp.where(valid_b[:, None, None], readout, jnp.zeros_like(readout))
        return out

    def _L0_attn_ref(hidden_states, in_proj_w, conv_w, conv_b, dt_bias, A_log, D, norm_w, out_proj_w):
        import jax, jax.numpy as jnp
        import numpy as np
        from jax import lax
        HIDDEN = 256
        INTER = 512
        NHEADS = 64
        HEADDIM = INTER // NHEADS
        STATE = 128
        NGROUPS = 1
        CONVK = 4
        CHUNK = 32
        CONV_DIM = INTER + 2 * NGROUPS * STATE
        EPS = 1e-05
        DT_MIN, DT_MAX = (0.0, 100.0)

        def _segsum(x):
            l = x.shape[-1]
            xx = jnp.broadcast_to(x[..., None], x.shape + (l,))
            m1 = jnp.tril(jnp.ones((l, l), bool), -1)
            s = jnp.cumsum(jnp.where(m1, xx, 0.0), axis=-2)
            m2 = jnp.tril(jnp.ones((l, l), bool), 0)
            return jnp.where(m2, s, -jnp.inf)
        Bsz, S, _ = hidden_states.shape
        proj = hidden_states @ in_proj_w.T
        gate, xBC, dt = jnp.split(proj, [INTER, INTER + CONV_DIM], axis=-1)
        xBC_t = xBC.transpose(0, 2, 1)
        xBC_t = lax.conv_general_dilated(xBC_t, conv_w, (1,), [(CONVK - 1, 0)], dimension_numbers=('NCH', 'OIH', 'NCH'), feature_group_count=CONV_DIM)
        xBC = jax.nn.silu((xBC_t + conv_b[None, :, None]).transpose(0, 2, 1))
        x, Bmat, Cmat = jnp.split(xBC, [INTER, INTER + NGROUPS * STATE], axis=-1)
        A = -jnp.exp(A_log.astype(jnp.float32))
        dt = jnp.clip(jax.nn.softplus(dt + dt_bias), DT_MIN, DT_MAX)
        x = x.reshape(Bsz, S, NHEADS, HEADDIM).astype(jnp.float32)
        Bmat = jnp.tile(Bmat.reshape(Bsz, S, NGROUPS, STATE).astype(jnp.float32), (1, 1, NHEADS // NGROUPS, 1))
        Cmat = jnp.tile(Cmat.reshape(Bsz, S, NGROUPS, STATE).astype(jnp.float32), (1, 1, NHEADS // NGROUPS, 1))
        pad = (CHUNK - S % CHUNK) % CHUNK
        D_res = D[..., None] * jnp.pad(x, ((0, 0), (0, pad), (0, 0), (0, 0)))
        x = x * dt[..., None]
        Adt = A * dt

        def chunk(t):
            t = jnp.pad(t, ((0, 0), (0, pad)) + ((0, 0),) * (t.ndim - 2))
            return t.reshape(t.shape[0], -1, CHUNK, *t.shape[2:])
        x_c, A_c, B_c, C_c = (chunk(x), chunk(Adt), chunk(Bmat), chunk(Cmat))
        A_c = A_c.transpose(0, 3, 1, 2)
        A_cum = jnp.cumsum(A_c, axis=-1)
        L = jnp.exp(_segsum(A_c))
        G = jnp.einsum('bclhn,bcshn->bclsh', C_c, B_c)
        M = G * L.transpose(0, 2, 3, 4, 1)
        Y_diag = jnp.einsum('bclsh,bcshp->bclhp', M, x_c)
        decay_states = jnp.exp(A_cum[..., -1:] - A_cum)
        B_decay = B_c * decay_states.transpose(0, 2, 3, 1)[..., None]
        states = jnp.einsum('bclhn,bclhp->bchpn', B_decay, x_c)
        states = jnp.concatenate([jnp.zeros_like(states[:, :1]), states], axis=1)
        decay_chunk = jnp.exp(_segsum(jnp.pad(A_cum[..., -1], ((0, 0), (0, 0), (1, 0)))))
        new_states = jnp.einsum('bhzj,bjhpn->bzhpn', decay_chunk, states)
        states = new_states[:, :-1]
        state_decay_out = jnp.exp(A_cum).transpose(0, 2, 3, 1)
        Y_off = jnp.einsum('bclhn,bchpn->bclhp', C_c, states) * state_decay_out[..., None]
        y = (Y_diag + Y_off).reshape(Bsz, -1, NHEADS, HEADDIM) + D_res
        y = y[:, :S].reshape(Bsz, S, INTER)
        y = y * jax.nn.silu(gate)
        var = jnp.mean(jnp.square(y), axis=-1, keepdims=True)
        y = y * lax.rsqrt(var + EPS) * norm_w
        return y @ out_proj_w.T

    def _L0_ffn_ref(hidden_states, gate_weight, gate_up_proj, down_proj):
        import jax, jax.numpy as jnp
        import numpy as np
        NUM_EXPERTS = 32
        TOP_K = 8
        THRESHOLD = 0.8
        HIDDEN = 256
        INTER = 96
        B, S, H = hidden_states.shape
        x = hidden_states.reshape(-1, H)
        logits = x @ gate_weight.T
        probs = jax.nn.softmax(logits.astype(jnp.float32), axis=-1).astype(logits.dtype)
        top_vals, top_idx = jax.lax.top_k(probs, TOP_K)
        renorm = top_vals / jnp.clip(jnp.sum(top_vals, axis=-1, keepdims=True), 1e-12)
        cum = jnp.cumsum(renorm, axis=-1)
        num_keep = jnp.minimum(jnp.sum((cum < THRESHOLD).astype(jnp.int32), axis=-1) + 1, TOP_K)
        active = jnp.arange(TOP_K)[None, :] < num_keep[:, None]
        rw = top_vals * active.astype(top_vals.dtype)
        rw = rw / jnp.clip(jnp.sum(rw, axis=-1, keepdims=True), 1e-12)
        combine = jnp.sum(jax.nn.one_hot(top_idx, NUM_EXPERTS, dtype=rw.dtype) * rw[..., None], axis=1)

        def body(acc, params):
            w_gu, w_d, ce = params
            gu = x @ w_gu.T
            g, u = jnp.split(gu, 2, axis=-1)
            h = jax.nn.silu(g) * u
            return (acc + h @ w_d.T * ce[:, None], None)
        out, _ = jax.lax.scan(body, jnp.zeros_like(x), (gate_up_proj, down_proj, combine.T))
        return out.reshape(B, S, H)
    x = x + _L0_xattn_ref(_layernorm(x, axis=-1), ctx_2048, mask_BxS2_bk0)
    x = x + _L0_attn_ref(_layernorm(x, axis=-1), L0_attn_in_proj_w, L0_attn_conv_w, L0_attn_conv_b, L0_attn_dt_bias, L0_attn_A_log, L0_attn_D, L0_attn_norm_w, L0_attn_out_proj_w)
    x = x + _L0_ffn_ref(_layernorm(x, axis=-1), L0_ffn_gate_weight, L0_ffn_gate_up_proj, L0_ffn_down_proj)
    return x

_drawn_inputs = setup_inputs


def setup_inputs(seed=0):
    import zlib

    import numpy as np

    out = dict(_drawn_inputs(seed))
    spreads = {'L0_attn_conv_b': (0.0, 0.1),
     'L0_attn_dt_bias': (1.0, 0.6),
     'L0_attn_D': (1.0, 0.2),
     'L0_attn_norm_w': (1.0, 0.2)}
    factors = {'L0_attn_A_log': 8.0,
     'L0_ffn_gate_weight': 8.0,
     'L0_ffn_gate_up_proj': 8.0,
     'L0_ffn_down_proj': 8.0}
    for name, (base, spread) in spreads.items():
        noise = np.random.default_rng([zlib.crc32(name.encode()), seed]).standard_normal(out[name].shape)
        drawn = base * np.exp(spread * noise) if base else spread * noise
        out[name] = jnp.asarray(drawn.astype(out[name].dtype))
    for name, factor in factors.items():
        out[name] = (out[name] * factor).astype(out[name].dtype)
    return out
```

```python
from contextlib import ExitStack

import concourse.bass as bass
from concourse import mybir

F32 = mybir.dt.float32
I32 = mybir.dt.int32
U32 = mybir.dt.uint32
U8 = mybir.dt.uint8
ALU = mybir.AluOpType
ACT = mybir.ActivationFunctionType
AX = mybir.AxisListType

P = 128
D = 256
KD = D // P
B, SEQ, CTX = 32, 64, 1601
TOK = B * SEQ
TILES = TOK // P
TB = P // SEQ
CHUNKS = -(-CTX // P)
LAST = CHUNKS - 1
LAST_ROWS = CTX - LAST * P
INTER, STATE, HEADS, HD, TAPS = 512, 128, 64, 8, 4
CONV = INTER + 2 * STATE
CB = CONV // P
IB = INTER // P
PROJ = INTER + CONV + HEADS
LEVELS = (32, 16, 8, 4, 2, 1)
NL = len(LEVELS)
EXPERTS, TOP, EI, KEEP = 32, 8, 96, 0.8
GE = 4
GROUPS = EXPERTS // GE
GW = GE * EI
HB = GW // P
EPS = 1e-5
MASKED = 1e30


def build(nc, x, ctx, ctx_t, mask_t, w_in, conv_w, conv_b, dt_bias, a_log, skip_d, norm_w, w_out,
          w_router, w_gu, w_down, c_ident, c_sum, c_mask, c_expert, out):
    with ExitStack() as stack:
        def sb(name, shape, dt=F32):
            return stack.enter_context(nc.sbuf_tensor(name, shape, dt))

        def sem(name):
            return stack.enter_context(nc.semaphore(name))

        fresh = []

        def loop_sem(name):
            fresh.append(sem(name))
            return fresh[-1]

        def start_loop_sems(eng):
            for s in fresh:
                eng.sem_inc(s, 1)
            fresh.clear()

        bank = [stack.enter_context(nc.psum_tensor(f"bank{n}", [P, 512], F32)) for n in range(8)]

        ident = sb("ident", [P, P])
        ones = sb("ones", [P, P])
        level_sum = sb("level_sum", [P, NL, P])
        level_mask = sb("level_mask", [P, NL, P])
        expert_no = sb("expert_no", [P, EXPERTS, TOP])
        minus_half = sb("minus_half", [P, TILES])
        w_in_sb = sb("w_in_sb", [P, KD, PROJ])
        w_out_sb = sb("w_out_sb", [P, IB, D])
        w_router_sb = sb("w_router_sb", [P, KD, EXPERTS])
        conv_w_sb = sb("conv_w_sb", [P, CB, TAPS])
        conv_b_sb = sb("conv_b_sb", [P, CB])
        dt_bias_sb = sb("dt_bias_sb", [P, HEADS])
        neg_a = sb("neg_a", [P, HEADS])
        half_d = sb("half_d", [P, HEADS])
        norm_sb = sb("norm_sb", [P, IB])

        x_all = sb("x_all", [P, TILES, D])
        xt_all = sb("xt_all", [P, TILES, D])
        dt_all = sb("dt_all", [P, TILES, HEADS])
        adt_all = sb("adt_all", [P, TILES, HEADS])
        comb_all = sb("comb_all", [P, TILES, EXPERTS])
        xn = sb("xn", [P, D])
        xt = sb("xt", [P, KD, P])
        stats = sb("stats", [P, 6])
        moments = sb("moments", [P, 2])
        var_eps = sb("var_eps", [P, 1])
        rstd = sb("rstd", [P, 1])

        phase = stack.enter_context(ExitStack())

        def tmp(name, shape, dt=F32):
            return phase.enter_context(nc.sbuf_tensor(name, shape, dt))

        CW = TB * D + TB * (D + 1)
        chunks = tmp("chunks", [P, 2, CHUNKS, CW])
        ctx_t_sb = [[chunks[:, p, c, 0:TB * D].rearrange("p (b k m) -> p b k m", b=TB, k=KD)
                     for c in range(CHUNKS)] for p in range(2)]
        ctx_sb = [[chunks[:, p, c, TB * D:CW].rearrange("p (b d) -> p b d", b=TB)
                   for c in range(CHUNKS)] for p in range(2)]
        mask_u8 = tmp("mask_u8", [P, CHUNKS, B], U8)
        mask_f = tmp("mask_f", [P, CHUNKS * B])
        mask_bias = tmp("mask_bias", [P, CHUNKS, B])
        count = tmp("count", [1, CHUNKS * TILES])
        flags = tmp("flags", [1, CHUNKS * TILES], I32)
        stats1 = tmp("stats1", [P, TILES, 6])
        moments1 = tmp("moments1", [P, TILES, 2])
        var1 = tmp("var1", [P, TILES])
        rstd1 = tmp("rstd1", [P, TILES])
        col_max = tmp("col_max", [P, P])
        q_max = tmp("q_max", [P, 1])
        max_diag = tmp("max_diag", [P, P])
        max_rows = tmp("max_rows", [P, P])
        probs = tmp("probs", [P, CHUNKS, P])
        valid = tmp("valid", [P, 1])
        denom = tmp("denom", [P, 1])
        weight = tmp("weight", [P, 1])

        ps_qt = bank[0][:, 0:D].rearrange("p (k m) -> p k m", k=KD)
        ps_xt = bank[0][:, D:2 * D].rearrange("p (k m) -> p k m", k=KD)
        ps_s = [bank[1 + c // 4][:, (c % 4) * P:(c % 4 + 1) * P] for c in range(CHUNKS)]
        ps_o = bank[5]
        ps_max = bank[6][:, 0:P]
        ps_rows = bank[6][:, P:2 * P]
        ps_dt = bank[6][:, 2 * P:2 * P + HEADS]
        ps_fence = bank[5][:, 510:512]
        ps_count = bank[7][0:1, 0:CHUNKS * B]

        x_loaded = sem("x_loaded")
        mask_cleared = sem("mask_cleared")
        mask_loaded = sem("mask_loaded")
        const_loaded = sem("const_loaded")
        ones_set = sem("ones_set")
        half_set = sem("half_set")
        mask_ready = sem("mask_ready")
        counted = sem("counted")
        flags_ready = sem("flags_ready")
        ln1_step = sem("ln1_step")
        ln1_rstd = sem("ln1_rstd")
        ones_col = sem("ones_col")
        ctx_loaded = [sem("ctx_loaded0"), sem("ctx_loaded1")]
        gathered = loop_sem("gathered")
        q_normed = loop_sem("q_normed")
        q_turned = loop_sem("q_turned")
        q_ready = loop_sem("q_ready")
        scored = loop_sem("scored")
        max_cleared = loop_sem("max_cleared")
        chunk_maxed = loop_sem("chunk_maxed")
        max_turned = loop_sem("max_turned")
        q_maxed = loop_sem("q_maxed")
        diag_ready = loop_sem("diag_ready")
        rows_ready = loop_sem("rows_ready")
        rows_copied = loop_sem("rows_copied")
        shifted = loop_sem("shifted")
        exped = loop_sem("exped")
        denom_ready = loop_sem("denom_ready")
        weight_ready = loop_sem("weight_ready")
        x2_ready = loop_sem("x2_ready")
        ln2_stats = loop_sem("ln2_stats")
        ln2_moments = loop_sem("ln2_moments")
        ln2_var = loop_sem("ln2_var")
        ln2_rstd = loop_sem("ln2_rstd")
        ln2_normed = loop_sem("ln2_normed")
        ln2_turned = loop_sem("ln2_turned")
        ln2_ready = loop_sem("ln2_ready")
        xt_kept = loop_sem("xt_kept")
        dt_projected = loop_sem("dt_projected")
        dt_biased = sem("dt_biased")

        def active(eng, c, t):
            return eng.value_load(flags[0:1, bass.ds(t + c * TILES, 1)], min_val=0, max_val=1)

        wait_taken = sem("wait_taken")

        def waited(eng):
            eng.sem_inc(wait_taken, 1)

        with nc.Block() as block:
            @block.sync
            def _(sp):
                start_loop_sems(sp)

        with nc.Block() as block:
            @block.sync
            def _(sp):
                sp.dma_start(x_all[:], x.rearrange("(t p) d -> p t d", p=P)).then_inc(x_loaded, 16)
                sp.wait_ge(mask_cleared, 1)
                sp.dma_start(mask_u8[:, 0:LAST, :],
                             mask_t[0:LAST * P, :].rearrange("(c p) b -> p c b", p=P)).then_inc(mask_loaded, 16)
                sp.dma_start(mask_u8[0:LAST_ROWS, LAST, :], mask_t[LAST * P:CTX, :]).then_inc(mask_loaded, 16)
                sp.wait_ge(flags_ready, 1)
                sp.wait_ge(ones_col, 1)
                with sp.Fori(0, TILES // 2) as j:
                    for p in range(2):
                        t = j * 2 + p

                        def load(c):
                            n = P if c < LAST else LAST_ROWS
                            sp.dma_start(ctx_t_sb[p][c][:, :, :, 0:n],
                                         ctx_t[t].rearrange("b (k p) m -> p b k m", p=P)[:, :, :, c * P:c * P + n]
                                         ).then_inc(ctx_loaded[p], 16)
                            sp.dma_start(ctx_sb[p][c][0:n, :, 0:D],
                                         ctx[t, :, c * P:c * P + n, :].rearrange("b m d -> m b d")
                                         ).then_inc(ctx_loaded[p], 16)

                        sp.wait_ge(gathered, after(t))
                        load(LAST)
                        for c in range(LAST):
                            with sp.If(active(sp, c, t) > 0):
                                load(c)

            @block.gpsimd
            def _(pool):
                pool.memset(mask_u8[:], 0).then_inc(mask_cleared, 1)
                pool.memset(ones[:], 1.0).then_inc(ones_set, 1)
                pool.memset(minus_half[:], -0.5).then_inc(half_set, 1)
                for p in range(2):
                    for c in range(CHUNKS):
                        last = pool.memset(ctx_sb[p][c][:, :, D:D + 1], 1.0)
                last.then_inc(ones_col, 1)
                pool.wait_ge(half_set, 1)
                pool.wait_ge(ln1_step, 3)
                pool.tensor_tensor(rstd1[:], var1[:], minus_half[:], ALU.pow).then_inc(ln1_rstd, 1)
                with pool.Fori(0, TILES) as t:
                    pool.wait_ge(ln2_var, after(t + 1))
                    pool.tensor_tensor(rstd[:], var_eps[:], minus_half[:, 0:1], ALU.pow).then_inc(ln2_rstd, 1)
                    pool.wait_ge(ln2_ready, after(t + 1))
                    pool.tensor_copy(xt_all[:, t, :], xt[:].rearrange("p k m -> p (k m)")).then_inc(xt_kept, 1)

            @block.vector
            def _(dve):
                dve.wait_ge(mask_loaded, 32)
                dve.tensor_copy(mask_f[:], mask_u8[:].rearrange("p c b -> p (c b)")).then_inc(mask_ready, 1)
                dve.wait_ge(mask_ready, 1)
                dve.tensor_scalar(mask_bias[:].rearrange("p c b -> p (c b)"), mask_f[:], MASKED, MASKED,
                                  ALU.mult, ALU.subtract).then_inc(mask_ready, 1)
                dve.wait_ge(counted, 1)
                dve.tensor_reduce(count[:], ps_count.rearrange("p (n b) -> p n b", b=TB), AX.X, ALU.add
                                  ).then_inc(mask_ready, 1)
                dve.wait_ge(mask_ready, 3)
                dve.tensor_scalar(flags[:], count[:], 1.0, None, ALU.min).then_inc(flags_ready, 1)
                dve.wait_ge(x_loaded, 16)
                for t in range(TILES):
                    last = dve.bn_stats(stats1[:, t, :], x_all[:, t, :])
                last.then_inc(ln1_step, 1)
                dve.wait_ge(ln1_step, 1)
                for t in range(TILES):
                    last = dve.bn_aggr(moments1[:, t, :], stats1[:, t, :])
                last.then_inc(ln1_step, 1)
                dve.wait_ge(ln1_step, 2)
                dve.tensor_scalar(var1[:], moments1[:, :, 1], EPS, None, ALU.add).then_inc(ln1_step, 1)
                dve.wait_ge(ln1_rstd, 1)
                dve.wait_ge(const_loaded, 13 * 16)
                n_max = dve.alloc_register("dve_chunks_maxed")
                n_sub = dve.alloc_register("dve_chunks_shifted")
                dve.reg_mov(n_max, 0)
                dve.reg_mov(n_sub, 0)
                total = TILES * CHUNKS
                with dve.Fori(0, TILES) as t:
                    dve.wait_ge(q_turned, after(t))
                    dve.tensor_scalar(xn[:], x_all[:, t, :], moments1[:, t, 0:1], rstd1[:, bass.ds(t, 1)],
                                      ALU.subtract, ALU.mult).then_inc(q_normed, 1)
                    dve.memset(col_max[:], -MASKED).then_inc(max_cleared, 1)
                    dve.wait_ge(max_cleared, after(t + 1))

                    def take_max(c):
                        n = P if c < LAST else LAST_ROWS
                        v = dve.snap(n_max, min_val=0, max_val=total)
                        dve.wait_ge(chunk_maxed, after(v))
                        for b in range(TB):
                            cols = slice(b * SEQ, (b + 1) * SEQ)
                            last = dve.scalar_tensor_tensor(
                                out=col_max[0:n, cols], in0=ps_s[c][0:n, cols],
                                scalar=mask_bias[0:n, c, bass.ds(t * TB + b, 1)], in1=col_max[0:n, cols],
                                op0=ALU.add, op1=ALU.max)
                        last.then_inc(chunk_maxed, 1)
                        dve.reg_add(n_max, n_max, 1)

                    dve.wait_ge(scored, after(t + 1))
                    waited(dve)
                    take_max(LAST)
                    for c in range(LAST):
                        with dve.If(active(dve, c, t) > 0):
                            take_max(c)
                    dve.wait_ge(max_turned, after(t + 1))
                    dve.tensor_reduce(q_max[:], ps_max, AX.X, ALU.max).then_inc(q_maxed, 1)
                    dve.wait_ge(q_maxed, after(t + 1))
                    dve.tensor_scalar(max_diag[:], ident[:], q_max[:, 0:1], None, ALU.mult).then_inc(diag_ready, 1)
                    dve.tensor_scalar(valid[:], q_max[:], -0.5 * MASKED, None, ALU.is_gt)
                    dve.wait_ge(rows_copied, after(t + 1))

                    def shift(c):
                        n = P if c < LAST else LAST_ROWS
                        for b in range(TB):
                            cols = slice(b * SEQ, (b + 1) * SEQ)
                            last = dve.scalar_tensor_tensor(
                                out=probs[0:n, c, cols], in0=ps_s[c][0:n, cols],
                                scalar=mask_bias[0:n, c, bass.ds(t * TB + b, 1)], in1=max_rows[0:n, cols],
                                op0=ALU.add, op1=ALU.subtract)
                        last.then_inc(shifted, 1)

                    shift(LAST)
                    for c in range(LAST):
                        with dve.If(active(dve, c, t) > 0):
                            shift(c)
                    dve.wait_ge(gathered, after(t + 2))
                    dve.reciprocal(denom[:], ps_o[:, D:D + 1]).then_inc(denom_ready, 1)
                    dve.wait_ge(denom_ready, after(t + 1))
                    dve.tensor_tensor(weight[:], denom[:], valid[:], ALU.mult).then_inc(weight_ready, 1)
                    dve.wait_ge(weight_ready, after(t + 1))
                    dve.scalar_tensor_tensor(out=x_all[:, t, :], in0=ps_o[:, 0:D], scalar=weight[:, 0:1],
                                             in1=x_all[:, t, :], op0=ALU.mult, op1=ALU.add).then_inc(x2_ready, 1)
                    dve.wait_ge(x2_ready, after(t + 1))
                    waited(dve)
                    dve.bn_stats(stats[:], x_all[:, t, :]).then_inc(ln2_stats, 1)
                    dve.wait_ge(ln2_stats, after(t + 1))
                    waited(dve)
                    dve.bn_aggr(moments[:], stats[:]).then_inc(ln2_moments, 1)
                    dve.wait_ge(ln2_moments, after(t + 1))
                    dve.tensor_scalar(var_eps[:], moments[:, 1:2], EPS, None, ALU.add).then_inc(ln2_var, 1)
                    dve.wait_ge(ln2_rstd, after(t + 1))
                    dve.tensor_scalar(xn[:], x_all[:, t, :], moments[:, 0:1], rstd[:, 0:1],
                                      ALU.subtract, ALU.mult).then_inc(ln2_normed, 1)
                    dve.wait_ge(dt_projected, after(t + 1))
                    dve.tensor_tensor(dt_all[:, t, :], ps_dt, dt_bias_sb[:], ALU.add).then_inc(dt_biased, 1)

            @block.scalar
            def _(act):
                act.dma_start(ident[:], c_ident).then_inc(const_loaded, 16)
                act.dma_start(level_sum[:], c_sum).then_inc(const_loaded, 16)
                act.dma_start(level_mask[:], c_mask).then_inc(const_loaded, 16)
                act.dma_start(expert_no[:], c_expert).then_inc(const_loaded, 16)
                act.dma_start(w_in_sb[:], w_in.rearrange("(k p) n -> p k n", p=P)).then_inc(const_loaded, 16)
                act.dma_start(w_out_sb[:], w_out.rearrange("(k p) n -> p k n", p=P)).then_inc(const_loaded, 16)
                act.dma_start(w_router_sb[:], w_router.rearrange("(k p) n -> p k n", p=P)).then_inc(const_loaded, 16)
                act.dma_start(conv_w_sb[:], conv_w.rearrange("(k p) n -> p k n", p=P)).then_inc(const_loaded, 16)
                act.dma_start(conv_b_sb[:], conv_b).then_inc(const_loaded, 16)
                act.dma_start(dt_bias_sb[:], dt_bias).then_inc(const_loaded, 16)
                act.dma_start(neg_a[:], a_log).then_inc(const_loaded, 16)
                act.dma_start(half_d[:], skip_d).then_inc(const_loaded, 16)
                act.dma_start(norm_sb[:], norm_w).then_inc(const_loaded, 16)
                n_exp = act.alloc_register("act_chunks_exped")
                act.reg_mov(n_exp, 0)
                total = TILES * CHUNKS
                act.wait_ge(flags_ready, 1)
                with act.Fori(0, TILES) as t:
                    act.wait_ge(q_turned, after(t + 1))
                    act.wait_ge(xt_kept, after(t))
                    act.copy(xt[:], ps_qt).then_inc(q_ready, 1)
                    act.wait_ge(rows_ready, after(t + 1))
                    act.copy(max_rows[:], ps_rows).then_inc(rows_copied, 1)

                    def exponent(c):
                        n = P if c < LAST else LAST_ROWS
                        v = act.snap(n_exp, min_val=0, max_val=total)
                        act.wait_ge(shifted, after(v + 1))
                        act.activation(probs[0:n, c, :], probs[0:n, c, :], ACT.Exp, scale=D ** -0.5
                                       ).then_inc(exped, 1)
                        act.reg_add(n_exp, n_exp, 1)

                    exponent(LAST)
                    for c in range(LAST):
                        with act.If(active(act, c, t) > 0):
                            exponent(c)
                    act.wait_ge(ln2_turned, after(t + 1))
                    act.copy(xt[:], ps_xt).then_inc(ln2_ready, 1)

            @block.tensor
            def _(pe):
                pe.wait_ge(mask_ready, 1)
                pe.wait_ge(ones_set, 1)
                pe.matmul(ps_count, ones[:, 0:1], mask_f[:], start=True, stop=True).then_inc(counted, 1)
                pe.matmul(ps_fence, ones[:], ones[:, 0:2], start=True, stop=True).then_inc(gathered, 1)
                pe.wait_ge(const_loaded, 13 * 16)
                n_s = pe.alloc_register("pe_chunks_scored")
                n_pv = pe.alloc_register("pe_chunks_summed")
                n_ld = [pe.alloc_register(f"pe_chunks_loaded{p}") for p in range(2)]
                for r in (n_s, n_pv, *n_ld):
                    pe.reg_mov(r, 0)
                total = TILES * CHUNKS
                pe.wait_ge(flags_ready, 1)
                with pe.Fori(0, TILES // 2) as j:
                    for p in range(2):
                        t = j * 2 + p
                        pe.wait_ge(q_normed, after(t + 1))
                        for k in range(KD):
                            last = pe.transpose(ps_qt[:, k, :], xn[:, k * P:(k + 1) * P], ident[:])
                        last.then_inc(q_turned, 1)
                        pe.reg_add(n_ld[p], n_ld[p], 1)
                        for c in range(LAST):
                            f = active(pe, c, t)
                            pe.reg_add(n_ld[p], n_ld[p], f)
                        pe.wait_ge(ctx_loaded[p], pe.snap(n_ld[p], min_val=0, max_val=total) * 32)
                        pe.wait_ge(q_ready, after(t + 1))

                        def score(c):
                            n = P if c < LAST else LAST_ROWS
                            for b in range(TB):
                                for k in range(KD):
                                    pe.matmul(ps_s[c][0:n, b * SEQ:(b + 1) * SEQ],
                                                     ctx_t_sb[p][c][:, b, k, 0:n],
                                                     xt[:, k, b * SEQ:(b + 1) * SEQ],
                                                     start=(k == 0), stop=(k == KD - 1))
                            pe.reg_add(n_s, n_s, 1)

                        score(LAST)
                        for c in range(LAST):
                            with pe.If(active(pe, c, t) > 0):
                                score(c)
                        pe.matmul(ps_fence, ones[:], ones[:, 0:2], start=True, stop=True).then_inc(scored, 1)
                        pe.wait_ge(chunk_maxed, after(pe.snap(n_s, min_val=0, max_val=total)))
                        pe.transpose(ps_max, col_max[:], ident[:]).then_inc(max_turned, 1)
                        pe.wait_ge(diag_ready, after(t + 1))
                        pe.matmul(ps_rows, ones[:], max_diag[:], start=True, stop=True).then_inc(rows_ready, 1)

                        def gather(c):
                            n = P if c < LAST else LAST_ROWS
                            v = pe.snap(n_pv, min_val=0, max_val=total)
                            pe.wait_ge(exped, after(v + 1))
                            for b in range(TB):
                                last = pe.matmul(ps_o[b * SEQ:(b + 1) * SEQ, 0:D + 1],
                                                 probs[0:n, c, b * SEQ:(b + 1) * SEQ],
                                                 ctx_sb[p][c][0:n, b, :], start=(c == LAST), stop=(c == LAST),
                                                 skip_group_check=True)
                            pe.reg_add(n_pv, n_pv, 1)
                            return last

                        gather(LAST)
                        for c in range(LAST):
                            with pe.If(active(pe, c, t) > 0):
                                gather(c)
                        pe.matmul(ps_fence, ones[:], ones[:, 0:2], start=True, stop=True).then_inc(gathered, 1)
                        pe.wait_ge(ln2_normed, after(t + 1))
                        for k in range(KD):
                            last = pe.transpose(ps_xt[:, k, :], xn[:, k * P:(k + 1) * P], ident[:])
                        last.then_inc(ln2_turned, 1)
                        pe.wait_ge(ln2_ready, after(t + 1))
                        for k in range(KD):
                            last = pe.matmul(ps_dt, xt[:, k, :], w_in_sb[:, k, PROJ - HEADS:PROJ],
                                             start=(k == 0), stop=(k == KD - 1))
                        last.then_inc(dt_projected, 1)

        phase.close()
        w_gu_sb = sb("w_gu_sb", [P, KD, EXPERTS, 2 * EI])
        w_down_sb = sb("w_down_sb", [P, GROUPS * HB, D])
        phase = stack.enter_context(ExitStack())
        step_abs = tmp("step_abs", [P, TILES * HEADS])
        step_exp = tmp("step_exp", [P, TILES * HEADS])
        step_log = tmp("step_log", [P, TILES * HEADS])
        z_abs = sem("z_abs")
        z_exp = sem("z_exp")
        z_log = sem("z_log")
        a_exp = sem("a_exp")
        step_done = sem("step_done")
        gu_loaded = sem("gu_loaded")
        down_loaded = sem("down_loaded")
        dt_flat = dt_all[:].rearrange("p t h -> p (t h)")

        conv = tmp("conv", [P, CB, P])
        conv_tanh = tmp("conv_tanh", [P, CB, P])
        act2 = tmp("act2", [P, CB, P])
        decay = tmp("decay", [P, NL, HEADS])
        g_masked = tmp("g_masked", [P, NL, P])
        g_scrap = tmp("g_scrap", [P, P])
        g_diag = tmp("g_diag", [P, 1])
        own = tmp("own", [P, HEADS])
        xdt = tmp("xdt", [P, INTER])
        xdec = tmp("xdec", [P, NL - 1, INTER])
        flow = tmp("flow", [P, 2, INTER])
        y = tmp("y", [P, INTER])
        gate_tanh = tmp("gate_tanh", [P, INTER])
        gate2 = tmp("gate2", [P, INTER])
        y_gated = tmp("y_gated", [P, INTER])
        y_square = tmp("y_square", [P, INTER])
        y_sum = tmp("y_sum", [P, 1])
        y_var = tmp("y_var", [P, 1])
        y_pow = tmp("y_pow", [P, 1])
        y_rstd = tmp("y_rstd", [P, 1])
        yt = tmp("yt", [P, IB, P])
        xs = tmp("xs", [P, KD, P])
        xr = tmp("xr", [P, KD, P])
        r_max = tmp("r_max", [P, 1])
        r_exp = tmp("r_exp", [P, EXPERTS])
        r_sum = tmp("r_sum", [P, 1])
        r_inv = tmp("r_inv", [P, 1])
        r_prob = tmp("r_prob", [P, EXPERTS])
        top = tmp("top", [P, TOP])
        top_no = tmp("top_no", [P, TOP], U32)
        top_sum = tmp("top_sum", [P, 1])
        top_inv = tmp("top_inv", [P, 1])
        renorm = tmp("renorm", [P, TOP])
        cum = tmp("cum", [P, TOP])
        kept = tmp("kept", [P, TOP])
        kept_sum = tmp("kept_sum", [P, 1])
        kept_inv = tmp("kept_inv", [P, 1])
        kept_w = tmp("kept_w", [P, TOP])
        is_expert = tmp("is_expert", [P, EXPERTS, TOP])
        w_expert = tmp("w_expert", [P, EXPERTS, TOP])

        ps_conv = [bank[0][:, 0:4 * P].rearrange("p (m t) -> p m t", t=P),
                   bank[1][:, 0:2 * P].rearrange("p (m t) -> p m t", t=P)]
        ps_g = bank[1][:, 2 * P:3 * P]
        ps_logit = bank[1][:, 3 * P:3 * P + EXPERTS]
        ps_gate = bank[2]
        ps_x = bank[3]
        ps_decay = bank[4][:, 0:NL * HEADS].rearrange("p (j h) -> p j h", h=HEADS)
        ps_flow = [bank[5], bank[6]]
        ps_yt = bank[4][:, :].rearrange("p (m t) -> p m t", t=P)
        ps_mix = bank[7][:, 0:D]
        ps_x3 = bank[7][:, D:2 * D].rearrange("p (k m) -> p k m", k=KD)

        def ps_conv_block(m):
            return ps_conv[m // 4][:, m % 4, :]

        def by_head(a):
            return a.rearrange("p (h e) -> p h e", e=HD)

        def spread(a):
            return a.unsqueeze(2).broadcast_to([P, HEADS, HD])

        xs_ready = loop_sem("xs_ready")
        conv_projected = loop_sem("conv_projected")
        gate_projected = loop_sem("gate_projected")
        conv_first = loop_sem("conv_first")
        conv_step = loop_sem("conv_step")
        conv_tanhed = loop_sem("conv_tanhed")
        conv_acted = loop_sem("conv_acted")
        decay_summed = loop_sem("decay_summed")
        decay_ready = loop_sem("decay_ready")
        g_ready = loop_sem("g_ready")
        x_turned = loop_sem("x_turned")
        g_split = loop_sem("g_split")
        g_diaged = loop_sem("g_diaged")
        own_ready = loop_sem("own_ready")
        xdt_ready = loop_sem("xdt_ready")
        xdec_ready = loop_sem("xdec_ready")
        flowed = loop_sem("flowed")
        flow_scaled = loop_sem("flow_scaled")
        y_added = loop_sem("y_added")
        gate_tanhed = loop_sem("gate_tanhed")
        gate_acted = loop_sem("gate_acted")
        y_gated_ready = loop_sem("y_gated_ready")
        y_summed = loop_sem("y_summed")
        y_var_ready = loop_sem("y_var_ready")
        y_pow_ready = loop_sem("y_pow_ready")
        y_rstd_ready = loop_sem("y_rstd_ready")
        y_turned = loop_sem("y_turned")
        yt_ready = loop_sem("yt_ready")
        mixed = loop_sem("mixed")
        x3_ready = loop_sem("x3_ready")
        ln3_stats = loop_sem("ln3_stats")
        ln3_moments = loop_sem("ln3_moments")
        ln3_var = loop_sem("ln3_var")
        ln3_rstd = loop_sem("ln3_rstd")
        ln3_normed = loop_sem("ln3_normed")
        ln3_turned = loop_sem("ln3_turned")
        xr_ready = loop_sem("xr_ready")
        xr_kept = sem("xr_kept")
        routed = loop_sem("routed")
        router_step = loop_sem("router_step")
        r_exped = loop_sem("r_exped")

        with nc.Block() as block:
            @block.sync
            def _(sp):
                start_loop_sems(sp)

        with nc.Block() as block:
            @block.sync
            def _(sp):
                for n, e in enumerate(range(0, EXPERTS, 8)):
                    sp.dma_start(w_gu_sb[:, :, e:e + 8, :],
                                 w_gu.rearrange("(k p) e f -> p k e f", p=P)[:, :, e:e + 8, :]).then_inc(gu_loaded, 16)
                sp.dma_start(w_down_sb[:], w_down.rearrange("(n p) d -> p n d", p=P)).then_inc(down_loaded, 16)

            @block.scalar
            def _(act):
                act.activation(neg_a[:], neg_a[:], ACT.Exp).then_inc(a_exp, 1)
                act.activation(step_abs[:], dt_flat, ACT.Abs).then_inc(z_abs, 1)
                act.wait_ge(z_abs, 1)
                act.activation(step_exp[:], step_abs[:], ACT.Exp, scale=-1.0).then_inc(z_exp, 1)
                act.wait_ge(z_exp, 1)
                act.activation(step_log[:], step_exp[:], ACT.Ln, bias=1.0).then_inc(z_log, 1)
                with act.Fori(0, TILES) as t:
                    act.wait_ge(gate_projected, after(t))
                    waited(act)
                    act.copy(xs[:].rearrange("p k m -> p (k m)"), xt_all[:, t, :]).then_inc(xs_ready, 1)
                    act.wait_ge(conv_projected, after(t + 1))
                    act.wait_ge(conv_acted, after(t))
                    for m in CONV_ORDER:
                        act.activation(conv[:, m, :], ps_conv_block(m), ACT.Identity, bias=conv_b_sb[:, m:m + 1],
                                       scale=conv_w_sb[:, m, TAPS - 1:TAPS]).then_inc(conv_first, 1)
                    act.wait_ge(decay_summed, after(t + 1))
                    act.activation(decay[:], ps_decay, ACT.Exp).then_inc(decay_ready, 1)
                    act.wait_ge(conv_step, after((t + 1) * (TAPS - 1) * CB))
                    act.activation(conv_tanh[:], conv[:], ACT.Tanh, scale=0.5).then_inc(conv_tanhed, 1)
                    act.wait_ge(gate_projected, after(t + 1))
                    act.activation(gate_tanh[:], ps_gate[:], ACT.Tanh, scale=0.5).then_inc(gate_tanhed, 1)
                    act.wait_ge(y_gated_ready, after(t + 1))
                    act.activation(y_square[:], y_gated[:], ACT.Square, accum_out=y_sum[:]).then_inc(y_summed, 1)
                    act.wait_ge(y_turned, after(t + 1))
                    act.copy(yt[:], ps_yt).then_inc(yt_ready, 1)
                    act.wait_ge(ln3_turned, after(t + 1))
                    act.copy(xr[:], ps_x3).then_inc(xr_ready, 1)
                    act.wait_ge(xr_ready, after(t + 1))
                    waited(act)
                    act.copy(xt_all[:, t, :], xr[:].rearrange("p k m -> p (k m)")).then_inc(xr_kept, 1)
                    act.wait_ge(router_step, after(t * ROUTER_STEPS + 1))
                    act.activation(r_exp[:], ps_logit, ACT.Exp, bias=r_max[:, 0:1], accum_out=r_sum[:]
                                   ).then_inc(r_exped, 1)

            @block.gpsimd
            def _(pool):
                with pool.Fori(0, TILES) as t:
                    pool.wait_ge(decay_ready, after(t + 1))
                    pool.wait_ge(xdt_ready, after(t + 1))
                    for j in range(NL - 1):
                        pool.tensor_tensor(by_head(xdec[:, j, :]), by_head(xdt[:]), spread(decay[:, j, :]),
                                           ALU.mult).then_inc(xdec_ready, 1)
                    pool.wait_ge(y_var_ready, after(t + 1))
                    pool.tensor_tensor(y_pow[:], y_var[:], minus_half[:, 0:1], ALU.pow).then_inc(y_pow_ready, 1)
                    pool.wait_ge(ln3_var, after(t + 1))
                    pool.tensor_tensor(rstd[:], var_eps[:], minus_half[:, 0:1], ALU.pow).then_inc(ln3_rstd, 1)

            @block.vector
            def _(dve):
                dve.wait_ge(z_log, 1)
                dve.scalar_tensor_tensor(out=dt_flat, in0=dt_flat, scalar=0.0, in1=step_log[:],
                                         op0=ALU.max, op1=ALU.add).then_inc(step_done, 1)
                dve.wait_ge(step_done, 1)
                dve.tensor_scalar(dt_flat, dt_flat, 0.0, 100.0, ALU.max, ALU.min).then_inc(step_done, 1)
                dve.wait_ge(a_exp, 1)
                dve.tensor_scalar(neg_a[:], neg_a[:], -1.0, None, ALU.mult).then_inc(step_done, 1)
                dve.wait_ge(step_done, 3)
                dve.tensor_tensor(adt_all[:], dt_all[:], neg_a[:].unsqueeze(1).broadcast_to([P, TILES, HEADS]),
                                  ALU.mult).then_inc(step_done, 1)
                dve.wait_ge(step_done, 4)
                dve.tensor_scalar(dt_flat, dt_flat, 0.5, None, ALU.mult).then_inc(step_done, 1)
                dve.tensor_scalar(half_d[:], half_d[:], 0.5, None, ALU.mult).then_inc(step_done, 1)
                for m in range(IB):
                    dve.tensor_scalar(w_out_sb[:, m, :], w_out_sb[:, m, :], norm_sb[:, m:m + 1], None, ALU.mult
                                      ).then_inc(step_done, 1)
                dve.wait_ge(step_done, 6 + IB)
                with dve.Fori(0, TILES) as t:
                    for n, (k, m) in enumerate(CONV_STEPS):
                            if k == 1:
                                dve.wait_ge(conv_first, after(t * CB + (2 if m in CONV_ORDER[:2] else CB)))
                            else:
                                dve.wait_ge(conv_step, after(t * len(CONV_STEPS) + CONV_STEPS.index((k - 1, m)) + 1))
                            now = conv[:, m, :].rearrange("p (b s) -> p b s", b=TB)[:, :, k:]
                            dve.scalar_tensor_tensor(
                                out=now, in0=ps_conv_block(m).rearrange("p (b s) -> p b s", b=TB)[:, :, 0:SEQ - k],
                                scalar=conv_w_sb[:, m, TAPS - 1 - k:TAPS - k], in1=now,
                                op0=ALU.mult, op1=ALU.add).then_inc(conv_step, 1)
                    dve.wait_ge(conv_tanhed, after(t + 1))
                    dve.scalar_tensor_tensor(out=act2[:].rearrange("p m t -> p (m t)"),
                                             in0=conv_tanh[:].rearrange("p m t -> p (m t)"), scalar=1.0,
                                             in1=conv[:].rearrange("p m t -> p (m t)"), op0=ALU.add, op1=ALU.mult
                                             ).then_inc(conv_acted, 1)
                    dve.wait_ge(gate_tanhed, after(t + 1))
                    dve.scalar_tensor_tensor(out=gate2[:], in0=gate_tanh[:], scalar=1.0, in1=ps_gate[:],
                                             op0=ALU.add, op1=ALU.mult).then_inc(gate_acted, 1)
                    dve.wait_ge(x_turned, after(t + 1))
                    dve.wait_ge(xdec_ready, after(t * (NL - 1)))
                    dve.tensor_tensor(by_head(xdt[:]), by_head(ps_x[:]), spread(dt_all[:, t, :]), ALU.mult
                                      ).then_inc(xdt_ready, 1)
                    dve.wait_ge(g_ready, after(t + 1))
                    dve.tensor_tensor(g_masked[:], ps_g.unsqueeze(1).broadcast_to([P, NL, P]), level_mask[:],
                                      ALU.mult).then_inc(g_split, 1)
                    dve.tensor_tensor_reduce(out=g_scrap[:], in0=ps_g, in1=ident[:], scale=0.25, scalar=0.0,
                                             op0=ALU.mult, op1=ALU.add, accum_out=g_diag[:]).then_inc(g_diaged, 1)
                    dve.wait_ge(g_diaged, after(t + 1))
                    dve.scalar_tensor_tensor(out=own[:], in0=dt_all[:, t, :], scalar=g_diag[:, 0:1], in1=half_d[:],
                                             op0=ALU.mult, op1=ALU.add).then_inc(own_ready, 1)
                    dve.wait_ge(own_ready, after(t + 1))
                    dve.tensor_tensor(by_head(y[:]), by_head(ps_x[:]), spread(own[:]), ALU.mult
                                      ).then_inc(y_added, 1)
                    for n in range(NL):
                        j = NL - 1 - n
                        dve.wait_ge(flowed, after(t * NL + n + 1))
                        if n == 0:
                            dve.wait_ge(decay_ready, after(t + 1))
                        dve.tensor_tensor(by_head(flow[:, n % 2, :]), by_head(ps_flow[n % 2][:]),
                                          spread(decay[:, j, :]), ALU.mult).then_inc(flow_scaled, 1)
                        dve.wait_ge(flow_scaled, after(t * NL + n + 1))
                        dve.wait_ge(y_added, after(t * (NL + 1) + n + 1))
                        dve.tensor_tensor(y[:], y[:], flow[:, n % 2, :], ALU.add).then_inc(y_added, 1)
                    dve.wait_ge(gate_acted, after(t + 1))
                    dve.wait_ge(y_added, after((t + 1) * (NL + 1)))
                    dve.tensor_tensor(y_gated[:], y[:], gate2[:], ALU.mult).then_inc(y_gated_ready, 1)
                    dve.wait_ge(y_summed, after(t + 1))
                    dve.tensor_scalar(y_var[:], y_sum[:], 0.25 / INTER, EPS, ALU.mult, ALU.add
                                      ).then_inc(y_var_ready, 1)
                    dve.wait_ge(y_pow_ready, after(t + 1))
                    dve.tensor_scalar(y_rstd[:], y_pow[:], 0.5, None, ALU.mult).then_inc(y_rstd_ready, 1)
                    dve.wait_ge(y_rstd_ready, after(t + 1))
                    dve.wait_ge(mixed, after(t + 1))
                    dve.scalar_tensor_tensor(out=x_all[:, t, :], in0=ps_mix, scalar=y_rstd[:, 0:1],
                                             in1=x_all[:, t, :], op0=ALU.mult, op1=ALU.add).then_inc(x3_ready, 1)
                    dve.wait_ge(x3_ready, after(t + 1))
                    waited(dve)
                    dve.bn_stats(stats[:], x_all[:, t, :]).then_inc(ln3_stats, 1)
                    dve.wait_ge(ln3_stats, after(t + 1))
                    waited(dve)
                    dve.bn_aggr(moments[:], stats[:]).then_inc(ln3_moments, 1)
                    dve.wait_ge(ln3_moments, after(t + 1))
                    dve.tensor_scalar(var_eps[:], moments[:, 1:2], EPS, None, ALU.add).then_inc(ln3_var, 1)
                    dve.wait_ge(ln3_rstd, after(t + 1))
                    dve.tensor_scalar(xn[:], x_all[:, t, :], moments[:, 0:1], rstd[:, 0:1],
                                      ALU.subtract, ALU.mult).then_inc(ln3_normed, 1)

                    steps = [0]

                    def then(instruction):
                        steps[0] += 1
                        instruction.then_inc(router_step, 1)
                        dve.wait_ge(router_step, after(t * ROUTER_STEPS + steps[0]))

                    dve.wait_ge(routed, after(t + 1))
                    then(dve.tensor_reduce(r_max[:], ps_logit, AX.X, ALU.max, negate=True))
                    dve.wait_ge(r_exped, after(t + 1))
                    then(dve.reciprocal(r_inv[:], r_sum[:]))
                    then(dve.tensor_scalar(r_prob[:], r_exp[:], r_inv[:, 0:1], None, ALU.mult))
                    waited(dve)
                    then(dve.max(top[:], r_prob[:]))
                    waited(dve)
                    then(dve.max_index(top_no[:], top[:], r_prob[:]))
                    then(dve.tensor_reduce(top_sum[:], top[:], AX.X, ALU.add))
                    then(dve.tensor_scalar(top_sum[:], top_sum[:], 1e-12, None, ALU.max))
                    then(dve.reciprocal(top_inv[:], top_sum[:]))
                    then(dve.tensor_scalar(renorm[:], top[:], top_inv[:, 0:1], None, ALU.mult))
                    then(dve.tensor_tensor_scan(cum[:], renorm[:], renorm[:], 0.0, ALU.add, ALU.bypass))
                    then(dve.tensor_copy(kept[:, 0:1], top[:, 0:1]))
                    then(dve.scalar_tensor_tensor(out=kept[:, 1:TOP], in0=cum[:, 0:TOP - 1], scalar=KEEP,
                                                  in1=top[:, 1:TOP], op0=ALU.is_lt, op1=ALU.mult))
                    then(dve.tensor_reduce(kept_sum[:], kept[:], AX.X, ALU.add))
                    then(dve.tensor_scalar(kept_sum[:], kept_sum[:], 1e-12, None, ALU.max))
                    then(dve.reciprocal(kept_inv[:], kept_sum[:]))
                    then(dve.tensor_scalar(kept_w[:], kept[:], kept_inv[:, 0:1], None, ALU.mult))
                    then(dve.tensor_tensor(is_expert[:], expert_no[:],
                                           top_no[:].unsqueeze(1).broadcast_to([P, EXPERTS, TOP]), ALU.is_equal))
                    then(dve.tensor_tensor(w_expert[:], is_expert[:],
                                           kept_w[:].unsqueeze(1).broadcast_to([P, EXPERTS, TOP]), ALU.mult))
                    then(dve.tensor_reduce(comb_all[:, t, :], w_expert[:], AX.X, ALU.add))
                    assert steps[0] == ROUTER_STEPS

            @block.tensor
            def _(pe):
                pe.wait_ge(step_done, 6 + IB)
                with pe.Fori(0, TILES) as t:
                    pe.wait_ge(xs_ready, after(t + 1))
                    pe.wait_ge(conv_step, after(t * (TAPS - 1) * CB))
                    pe.wait_ge(r_exped, after(t))
                    for m in range(CB):
                        for k in range(KD):
                            last = pe.matmul(ps_conv_block(m), w_in_sb[:, k, INTER + m * P:INTER + (m + 1) * P],
                                             xs[:, k, :], start=(k == 0), stop=(k == KD - 1))
                    last.then_inc(conv_projected, 1)
                    pe.wait_ge(gate_acted, after(t))
                    for k in range(KD):
                        last = pe.matmul(ps_gate[:], xs[:, k, :], w_in_sb[:, k, 0:INTER],
                                         start=(k == 0), stop=(k == KD - 1))
                    last.then_inc(gate_projected, 1)
                    pe.wait_ge(yt_ready, after(t))
                    for j in range(NL):
                        last = pe.matmul(ps_decay[:, j, :], level_sum[:, j, :], adt_all[:, t, :],
                                         start=True, stop=True)
                    last.then_inc(decay_summed, 1)
                    pe.wait_ge(conv_acted, after(t + 1))
                    pe.wait_ge(y_added, after(t * (NL + 1)))
                    for m in range(IB):
                        last = pe.transpose(ps_x[:, m * P:(m + 1) * P], act2[:, m, :], ident[:])
                    last.then_inc(x_turned, 1)
                    pe.matmul(ps_g, act2[:, IB, :], act2[:, IB + 1, :], start=True, stop=True).then_inc(g_ready, 1)
                    pe.wait_ge(g_split, after(t + 1))
                    for n in range(NL):
                        j = NL - 1 - n
                        if n == 0:
                            pe.wait_ge(xdt_ready, after(t + 1))
                        else:
                            pe.wait_ge(xdec_ready, after(t * (NL - 1) + j + 1))
                        if n >= 2:
                            pe.wait_ge(flow_scaled, after(t * NL + n - 1))
                        pe.matmul(ps_flow[n % 2][:], g_masked[:, j, :], xdt[:] if n == 0 else xdec[:, j, :],
                                  start=True, stop=True).then_inc(flowed, 1)
                    pe.wait_ge(y_gated_ready, after(t + 1))
                    for m in range(IB):
                        last = pe.transpose(ps_yt[:, m, :], y_gated[:, m * P:(m + 1) * P], ident[:])
                    last.then_inc(y_turned, 1)
                    pe.wait_ge(yt_ready, after(t + 1))
                    for m in range(IB):
                        last = pe.matmul(ps_mix, yt[:, m, :], w_out_sb[:, m, :], start=(m == 0), stop=(m == IB - 1))
                    last.then_inc(mixed, 1)
                    pe.wait_ge(ln3_normed, after(t + 1))
                    for k in range(KD):
                        last = pe.transpose(ps_x3[:, k, :], xn[:, k * P:(k + 1) * P], ident[:])
                    last.then_inc(ln3_turned, 1)
                    pe.wait_ge(xr_ready, after(t + 1))
                    for k in range(KD):
                        last = pe.matmul(ps_logit, xr[:, k, :], w_router_sb[:, k, :], start=(k == 0), stop=(k == KD - 1))
                    last.then_inc(routed, 1)

        phase.close()
        phase = stack.enter_context(ExitStack())
        xe = tmp("xe", [P, KD, P])
        gate = tmp("gate", [P, 2, GW])
        up_gate = tmp("up_gate", [P, 2, GW])
        hidden = tmp("hidden", [P, 2, GW])
        ht = tmp("ht", [P, 2, GW])
        ps_gate_e = [bank[0][:, 0:GW], bank[1][:, 0:GW]]
        ps_up_e = [bank[2][:, 0:GW], bank[3][:, 0:GW]]
        ps_ht = [bank[4][:, 0:GW], bank[5][:, 0:GW]]
        ps_y = bank[6][:, 0:D]

        xe_ready = loop_sem("xe_ready")
        gu_projected = loop_sem("gu_projected")
        gate_silued = loop_sem("gate_silued")
        up_gated = loop_sem("up_gated")
        weighted = loop_sem("weighted")
        h_turned = loop_sem("h_turned")
        ht_ready = loop_sem("ht_ready")
        downed = sem("downed")
        summed = loop_sem("summed")
        added = loop_sem("added")
        stored = sem("stored")

        with nc.Block() as block:
            @block.sync
            def _(sp):
                start_loop_sems(sp)

        with nc.Block() as block:
            @block.sync
            def _(sp):
                out_v = out.rearrange("(t p) d -> t p d", p=P)
                with sp.Fori(0, TILES) as t:
                    sp.wait_ge(added, after(t + 1))
                    sp.dma_start(out_v[t], x_all[:, t, :]).then_inc(stored, 16)
                sp.wait_ge(stored, TILES * 16)

            @block.scalar
            def _(act):
                with act.Fori(0, TILES) as t:
                    act.wait_ge(gu_projected, after(t * GROUPS))
                    waited(act)
                    act.copy(xe[:].rearrange("p k m -> p (k m)"), xt_all[:, t, :]).then_inc(xe_ready, 1)
                    for g in range(GROUPS + 1):
                        if g < GROUPS:
                            act.wait_ge(gu_projected, after(t * GROUPS + g + 1))
                            act.activation(gate[:, g % 2, :], ps_gate_e[g % 2], ACT.Silu).then_inc(gate_silued, 1)
                        if g >= 1:
                            act.wait_ge(h_turned, after(t * GROUPS + g))
                            act.copy(ht[:, (g - 1) % 2, :], ps_ht[(g - 1) % 2]).then_inc(ht_ready, 1)

            @block.gpsimd
            def _(pool):
                with pool.Fori(0, TILES) as t:
                    for g in range(GROUPS):
                        pool.wait_ge(up_gated, after(t * GROUPS + g + 1))
                        pool.tensor_tensor(hidden[:, g % 2, :].rearrange("p (e f) -> p e f", e=GE),
                                           up_gate[:, g % 2, :].rearrange("p (e f) -> p e f", e=GE),
                                           comb_all[:, t, g * GE:(g + 1) * GE].unsqueeze(2).broadcast_to([P, GE, EI]),
                                           ALU.mult).then_inc(weighted, 1)

            @block.vector
            def _(dve):
                with dve.Fori(0, TILES) as t:
                    for g in range(GROUPS):
                        dve.wait_ge(gate_silued, after(t * GROUPS + g + 1))
                        if g >= 2:
                            dve.wait_ge(weighted, after(t * GROUPS + g - 1))
                        dve.tensor_tensor(up_gate[:, g % 2, :], gate[:, g % 2, :], ps_up_e[g % 2], ALU.mult
                                          ).then_inc(up_gated, 1)
                    dve.wait_ge(summed, after(t + 1))
                    dve.tensor_tensor(x_all[:, t, :], ps_y, x_all[:, t, :], ALU.add).then_inc(added, 1)

            @block.tensor
            def _(pe):
                pe.wait_ge(gu_loaded, 64)
                pe.wait_ge(down_loaded, 16)
                with pe.Fori(0, TILES) as t:
                    def project(g):
                        if g == 0:
                            pe.wait_ge(xe_ready, after(t + 1))
                        if g >= 2:
                            pe.wait_ge(up_gated, after(t * GROUPS + g - 1))
                        for ps, f in ((ps_gate_e, 0), (ps_up_e, EI)):
                            for k in range(KD):
                                last = pe.matmul(ps[g % 2].rearrange("p (e f) -> p e f", e=GE), xe[:, k, :],
                                                 w_gu_sb[:, k, g * GE:(g + 1) * GE, f:f + EI],
                                                 start=(k == 0), stop=(k == KD - 1))
                        last.then_inc(gu_projected, 1)

                    def turn(g):
                        pe.wait_ge(weighted, after(t * GROUPS + g + 1))
                        for m in range(HB):
                            last = pe.transpose(ps_ht[g % 2][:, m * P:(m + 1) * P],
                                                hidden[:, g % 2, m * P:(m + 1) * P], ident[:])
                        last.then_inc(h_turned, 1)

                    def down(g):
                        if g == 0:
                            pe.wait_ge(added, after(t))
                        pe.wait_ge(ht_ready, after(t * GROUPS + g + 1))
                        for m in range(HB):
                            last = pe.matmul(ps_y, ht[:, g % 2, m * P:(m + 1) * P], w_down_sb[:, g * HB + m, :],
                                             start=(g == 0 and m == 0), stop=(g == GROUPS - 1 and m == HB - 1))
                        last.then_inc(summed if g == GROUPS - 1 else downed, 1)

                    for g in range(GROUPS + 2):
                        if g < GROUPS:
                            project(g)
                        if g >= 2:
                            down(g - 2)
                        if 1 <= g <= GROUPS:
                            turn(g - 1)


def after(n):
    return n + 1


ROUTER_STEPS = 19
CONV_ORDER = (4, 5, 0, 1, 2, 3)
CONV_STEPS = [(k, m) for part in (CONV_ORDER[:2], CONV_ORDER[2:]) for k in range(1, TAPS) for m in part]


def level_constants():
    import numpy as np

    at = np.arange(P)
    total = np.zeros((P, NL, P), np.float32)
    mask = np.zeros((P, NL, P), np.float32)
    for j, half in enumerate(LEVELS):
        block = at // (2 * half)
        second = at % (2 * half) >= half
        middle = block * 2 * half + half - 1
        k, tok = at[:, None], at[None, :]
        same = block[:, None] == block[None, :]
        after = same & second[None, :] & (k > middle[None, :]) & (k <= tok)
        before = same & ~second[None, :] & (k > tok) & (k <= middle[None, :])
        total[:, j, :] = after | before
        mask[:, j, :] = 0.25 * (same & ~second[:, None] & second[None, :])
    return total, mask


def kernel(x, ctx_2048, mask_BxS2_bk0, L0_attn_in_proj_w, L0_attn_conv_w, L0_attn_conv_b, L0_attn_dt_bias,
           L0_attn_A_log, L0_attn_D, L0_attn_norm_w, L0_attn_out_proj_w, L0_ffn_gate_weight,
           L0_ffn_gate_up_proj, L0_ffn_down_proj):
    import numpy as np
    import concourse.bacc as bacc
    from concourse.bass_utils import run_bass_kernel_spmd

    a = np.asarray
    total, mask = level_constants()
    ctx = a(ctx_2048).reshape(TILES, TB, CTX, D)
    arrays = {
        "x": a(x).reshape(TOK, D),
        "ctx": ctx,
        "ctx_t": ctx.transpose(0, 1, 3, 2),
        "mask_t": a(mask_BxS2_bk0).T,
        "w_in": a(L0_attn_in_proj_w).T,
        "conv_w": a(L0_attn_conv_w).reshape(CONV, TAPS),
        "conv_b": a(L0_attn_conv_b).reshape(CB, P).T,
        "dt_bias": np.broadcast_to(a(L0_attn_dt_bias), (P, HEADS)),
        "a_log": np.broadcast_to(a(L0_attn_A_log), (P, HEADS)),
        "skip_d": np.broadcast_to(a(L0_attn_D), (P, HEADS)),
        "norm_w": a(L0_attn_norm_w).reshape(IB, P).T,
        "w_out": a(L0_attn_out_proj_w).T,
        "w_router": a(L0_ffn_gate_weight).T,
        "w_gu": a(L0_ffn_gate_up_proj).transpose(2, 0, 1),
        "w_down": a(L0_ffn_down_proj).transpose(0, 2, 1).reshape(EXPERTS * EI, D),
        "c_ident": np.eye(P, dtype=np.float32),
        "c_sum": total,
        "c_mask": mask,
        "c_expert": np.broadcast_to(np.arange(EXPERTS, dtype=np.float32)[None, :, None], (P, EXPERTS, TOP)),
    }
    arrays = {f"in_{k}": np.ascontiguousarray(v) for k, v in arrays.items()}
    nc = bacc.Bacc("TRN2", target_bir_lowering=False, num_devices=1)
    args = [nc.dram_tensor(k, v.shape, mybir.dt.from_np(v.dtype), kind="ExternalInput").ap()
            for k, v in arrays.items()]
    out = nc.dram_tensor("out_dram", (TOK, D), F32, kind="ExternalOutput").ap()
    build(nc, *args, out)
    r = run_bass_kernel_spmd(nc, [arrays], core_ids=[0])
    return r.results[0]["out_dram"].reshape(B, SEQ, D)
```

```python
from contextlib import ExitStack

import concourse.bass as bass
from concourse import mybir

F32 = mybir.dt.float32
I32 = mybir.dt.int32
U32 = mybir.dt.uint32
U8 = mybir.dt.uint8
ALU = mybir.AluOpType
ACT = mybir.ActivationFunctionType
AX = mybir.AxisListType

P = 128
D = 256
KD = D // P
B, SEQ, CTX = 32, 64, 1601
TOK = B * SEQ
TILES = TOK // P
TB = P // SEQ
CHUNKS = -(-CTX // P)
LAST = CHUNKS - 1
LAST_ROWS = CTX - LAST * P
INTER, STATE, HEADS, HD, TAPS = 512, 128, 64, 8, 4
CONV = INTER + 2 * STATE
CB = CONV // P
IB = INTER // P
PROJ = INTER + CONV + HEADS
LEVELS = (32, 16, 8, 4, 2, 1)
NL = len(LEVELS)
EXPERTS, TOP, EI, KEEP = 32, 8, 96, 0.8
GE = 4
GROUPS = EXPERTS // GE
GW = GE * EI
HB = GW // P
EPS = 1e-5
MASKED = 1e30


def build(nc, x, ctx, ctx_t, mask_t, w_in, conv_w, conv_b, dt_bias, a_log, skip_d, norm_w, w_out,
          w_router, w_gu, w_down, c_before, c_ident, c_sum, c_mask, c_expert, out):
    with ExitStack() as stack:
        def sb(name, shape, dt=F32):
            return stack.enter_context(nc.sbuf_tensor(name, shape, dt))

        def sem(name):
            return stack.enter_context(nc.semaphore(name))

        fresh = []

        def loop_sem(name):
            fresh.append(sem(name))
            return fresh[-1]

        def start_loop_sems(eng):
            for s in fresh:
                eng.sem_inc(s, 1)
            fresh.clear()

        bank = [stack.enter_context(nc.psum_tensor(f"bank{n}", [P, 512], F32)) for n in range(8)]

        ident = sb("ident", [P, P])
        ones = sb("ones", [P, P])
        level_sum = sb("level_sum", [P, NL, P])
        level_mask = sb("level_mask", [P, NL, P])
        expert_no = sb("expert_no", [P, EXPERTS, TOP])
        minus_half = sb("minus_half", [P, TILES])
        w_in_sb = sb("w_in_sb", [P, KD, PROJ])
        w_out_sb = sb("w_out_sb", [P, IB, D])
        w_router_sb = sb("w_router_sb", [P, KD, EXPERTS])
        conv_w_sb = sb("conv_w_sb", [P, CB, TAPS])
        conv_b_sb = sb("conv_b_sb", [P, CB])
        dt_bias_sb = sb("dt_bias_sb", [P, HEADS])
        neg_a = sb("neg_a", [P, HEADS])
        half_d = sb("half_d", [P, HEADS])
        norm_sb = sb("norm_sb", [P, IB])

        x_all = sb("x_all", [P, TILES, D])
        xt_all = sb("xt_all", [P, TILES, D])
        dt_all = sb("dt_all", [P, TILES, HEADS])
        adt_all = sb("adt_all", [P, TILES, HEADS])
        comb_all = sb("comb_all", [P, TILES, EXPERTS])
        xn = sb("xn", [P, D])
        xt = sb("xt", [P, KD, P])
        stats = sb("stats", [P, 6])
        moments = sb("moments", [P, 2])
        var_eps = sb("var_eps", [P, 1])
        rstd = sb("rstd", [P, 1])

        phase = stack.enter_context(ExitStack())

        def tmp(name, shape, dt=F32):
            return phase.enter_context(nc.sbuf_tensor(name, shape, dt))

        CW = TB * D + TB * (D + 1)
        chunks = tmp("chunks", [P, 2, CHUNKS, CW])
        ctx_t_sb = [[chunks[:, p, c, 0:TB * D].rearrange("p (b k m) -> p b k m", b=TB, k=KD)
                     for c in range(CHUNKS)] for p in range(2)]
        ctx_sb = [[chunks[:, p, c, TB * D:CW].rearrange("p (b d) -> p b d", b=TB)
                   for c in range(CHUNKS)] for p in range(2)]
        mask_u8 = tmp("mask_u8", [P, CHUNKS, B], U8)
        mask_f = tmp("mask_f", [P, CHUNKS * B])
        mask_bias = tmp("mask_bias", [P, CHUNKS, B])
        count = tmp("count", [1, CHUNKS * TILES])
        before_last = tmp("before_last", [1, CHUNKS, TILES])
        any_active = tmp("any_active", [1, CHUNKS * TILES])
        first_f = tmp("first_f", [1, TILES])
        first_chunk = tmp("first_chunk", [1, TILES], I32)
        n_active = tmp("n_active", [1, TILES], I32)
        stats1 = tmp("stats1", [P, TILES, 6])
        moments1 = tmp("moments1", [P, TILES, 2])
        var1 = tmp("var1", [P, TILES])
        rstd1 = tmp("rstd1", [P, TILES])
        qn = tmp("qn", [P, D])
        qt = tmp("qt", [P, KD, P])
        col_max = tmp("col_max", [P, P])
        q_max = tmp("q_max", [P, 1])
        max_diag = tmp("max_diag", [P, P])
        max_rows = tmp("max_rows", [P, P])
        masked = [tmp(f"masked{p}", [P, CHUNKS, P]) for p in range(2)]
        valid = tmp("valid", [P, 1])
        denom = tmp("denom", [P, 1])
        weight = tmp("weight", [P, 1])
        scrap = tmp("scrap", [P, 2])

        ps_qt = bank[0][:, 0:D].rearrange("p (k m) -> p k m", k=KD)
        ps_fence_s = bank[0][:, 510:512]
        ps_s = [bank[1 + c // 4][:, (c % 4) * P:(c % 4 + 1) * P] for c in range(CHUNKS)]
        ps_o = bank[5]
        ps_fence_o = bank[5][:, 510:512]
        ps_max = bank[6][:, 0:P]
        ps_rows = bank[6][:, P:2 * P]
        ps_xt = bank[7][:, 0:D].rearrange("p (k m) -> p k m", k=KD)
        ps_dt = bank[7][:, D:D + HEADS]
        ps_count = bank[7][0:1, 0:CHUNKS * B]

        x_loaded = sem("x_loaded")
        mask_cleared = sem("mask_cleared")
        mask_loaded = sem("mask_loaded")
        const_loaded = sem("const_loaded")
        weights_loaded = sem("weights_loaded")
        ones_set = sem("ones_set")
        half_set = sem("half_set")
        mask_step = sem("mask_step")
        counted = sem("counted")
        first_ready = sem("first_ready")
        ln1_step = sem("ln1_step")
        ln1_rstd = sem("ln1_rstd")
        ones_col = sem("ones_col")
        ctx_loaded = [sem("ctx_loaded0"), sem("ctx_loaded1")]
        wait_taken = sem("wait_taken")
        q_normed = loop_sem("q_normed")
        q_turned = loop_sem("q_turned")
        q_ready = loop_sem("q_ready")
        scored = loop_sem("scored")
        max_cleared = loop_sem("max_cleared")
        chunk_masked = loop_sem("chunk_masked")
        chunk_maxed = loop_sem("chunk_maxed")
        maxed = loop_sem("maxed")
        max_turned = loop_sem("max_turned")
        q_maxed = loop_sem("q_maxed")
        diag_ready = loop_sem("diag_ready")
        rows_ready = loop_sem("rows_ready")
        rows_copied = loop_sem("rows_copied")
        shifted = loop_sem("shifted")
        exped = loop_sem("exped")
        gathered = loop_sem("gathered")
        denom_ready = loop_sem("denom_ready")
        weight_ready = loop_sem("weight_ready")
        x2_ready = loop_sem("x2_ready")
        ln2_stats = loop_sem("ln2_stats")
        ln2_moments = loop_sem("ln2_moments")
        ln2_var = loop_sem("ln2_var")
        ln2_rstd = loop_sem("ln2_rstd")
        ln2_normed = loop_sem("ln2_normed")
        ln2_turned = loop_sem("ln2_turned")
        ln2_ready = loop_sem("ln2_ready")
        xt_kept = loop_sem("xt_kept")
        dt_projected = loop_sem("dt_projected")
        dt_biased = loop_sem("dt_biased")

        def waited(eng):
            eng.sem_inc(wait_taken, 1)

        def first_of(eng, t):
            return eng.value_load(first_chunk[0:1, bass.ds(t, 1)], min_val=0, max_val=LAST)

        def active_chunks(eng, first, work):
            work(LAST)

            def back(c):
                if c >= 0:
                    with eng.If(first <= c):
                        work(c)
                        back(c - 1)

            back(LAST - 1)

        def rows(c):
            return P if c < LAST else LAST_ROWS

        def in_step(eng, step, lead=0):
            for i in range(-lead, 1):
                step(i, i % 2)
            with eng.Fori(0, (TILES - 2) // 2) as j:
                for n in (1, 2):
                    step(j * 2 + n, n % 2)
            for i in (TILES - 1, TILES):
                step(i, i % 2)

        def exists(i, ahead):
            return not isinstance(i, int) or 0 <= i + ahead < TILES

        with nc.Block() as block:
            @block.sync
            def _(sp):
                start_loop_sems(sp)

        with nc.Block() as block:
            @block.sync
            def _(sp):
                sp.wait_ge(mask_cleared, 1)
                sp.dma_start(mask_u8[:, 0:LAST, :],
                             mask_t[0:LAST * P, :].rearrange("(c p) b -> p c b", p=P)).then_inc(mask_loaded, 16)
                sp.dma_start(mask_u8[0:LAST_ROWS, LAST, :], mask_t[LAST * P:CTX, :]).then_inc(mask_loaded, 16)
                sp.wait_ge(first_ready, 1)
                sp.wait_ge(ones_col, 1)

                def load_tile(t, p):
                    def load(c):
                        n = rows(c)
                        sp.dma_start(ctx_t_sb[p][c][:, :, :, 0:n],
                                     ctx_t[t].rearrange("b (k p) m -> p b k m", p=P)[:, :, :, c * P:c * P + n]
                                     ).then_inc(ctx_loaded[p], 16)
                        sp.dma_start(ctx_sb[p][c][0:n, :, 0:D],
                                     ctx[t, :, c * P:c * P + n, :].rearrange("b m d -> m b d")
                                     ).then_inc(ctx_loaded[p], 16)

                    active_chunks(sp, first_of(sp, t), load)

                load_tile(0, 0)
                load_tile(1, 1)
                with sp.Fori(1, TILES // 2) as j:
                    for p in range(2):
                        sp.wait_ge(gathered, after(j * 2 + p - 1))
                        load_tile(j * 2 + p, p)

            @block.gpsimd
            def _(pool):
                pool.memset(mask_u8[:], 0).then_inc(mask_cleared, 1)
                pool.memset(ones[:], 1.0).then_inc(ones_set, 1)
                pool.memset(minus_half[:], -0.5).then_inc(half_set, 1)
                for p in range(2):
                    for c in range(CHUNKS):
                        last = pool.memset(ctx_sb[p][c][:, :, D:D + 1], 1.0)
                last.then_inc(ones_col, 1)
                pool.wait_ge(half_set, 1)
                pool.wait_ge(ln1_step, 3)
                pool.tensor_tensor(rstd1[:], var1[:], minus_half[:], ALU.pow).then_inc(ln1_rstd, 1)
                with pool.Fori(0, TILES) as t:
                    pool.wait_ge(ln2_var, after(t + 1))
                    pool.tensor_tensor(rstd[:], var_eps[:], minus_half[:, 0:1], ALU.pow).then_inc(ln2_rstd, 1)
                    pool.wait_ge(ln2_ready, after(t + 1))
                    pool.tensor_copy(xt_all[:, t, :], xt[:].rearrange("p k m -> p (k m)")).then_inc(xt_kept, 1)

            @block.vector
            def _(dve):
                dve.wait_ge(mask_loaded, 32)
                dve.tensor_copy(mask_f[:], mask_u8[:].rearrange("p c b -> p (c b)")).then_inc(mask_step, 1)
                dve.wait_ge(mask_step, 1)
                dve.tensor_scalar(mask_bias[:].rearrange("p c b -> p (c b)"), mask_f[:], MASKED, MASKED,
                                  ALU.mult, ALU.subtract).then_inc(mask_step, 1)
                dve.wait_ge(counted, 1)
                dve.tensor_reduce(count[:], ps_count.rearrange("p (n b) -> p n b", b=TB), AX.X, ALU.add
                                  ).then_inc(mask_step, 1)
                dve.wait_ge(mask_step, 3)
                dve.tensor_scalar(any_active[:], count[:], 1.0, None, ALU.min).then_inc(mask_step, 1)
                dve.wait_ge(mask_step, 4)
                dve.wait_ge(const_loaded, 32)
                dve.tensor_tensor(any_active[:], any_active[:], before_last[:].rearrange("p c t -> p (c t)"), ALU.mult
                                  ).then_inc(mask_step, 1)
                dve.wait_ge(mask_step, 5)
                dve.tensor_reduce(first_f[:], any_active[:].rearrange("p (c t) -> p t c", t=TILES), AX.X, ALU.min
                                  ).then_inc(mask_step, 1)
                dve.wait_ge(mask_step, 6)
                dve.tensor_scalar(n_active[:], first_f[:], -1.0, 1.0, ALU.mult, ALU.add)
                dve.tensor_scalar(first_chunk[:], first_f[:], float(LAST), None, ALU.add).then_inc(first_ready, 1)
                dve.wait_ge(x_loaded, 16)
                for t in range(TILES):
                    last = dve.bn_stats(stats1[:, t, :], x_all[:, t, :])
                last.then_inc(ln1_step, 1)
                dve.wait_ge(ln1_step, 1)
                for t in range(TILES):
                    last = dve.bn_aggr(moments1[:, t, :], stats1[:, t, :])
                last.then_inc(ln1_step, 1)
                dve.wait_ge(ln1_step, 2)
                dve.tensor_scalar(var1[:], moments1[:, :, 1], EPS, None, ALU.add).then_inc(ln1_step, 1)
                dve.wait_ge(ln1_rstd, 1)
                dve.wait_ge(weights_loaded, 12 * 16)
                n_max = dve.alloc_register("dve_chunks_maxed")
                dve.reg_mov(n_max, 0)

                def norm_queries(t):
                    if not (isinstance(t, int) and t == 0):
                        dve.wait_ge(q_turned, after(t))
                    dve.tensor_scalar(qn[:], x_all[:, t, :], moments1[:, t, 0:1], rstd1[:, bass.ds(t, 1)],
                                      ALU.subtract, ALU.mult).then_inc(q_normed, 1)

                def step(i, p):
                    first = first_of(dve, i) if exists(i, 0) else None
                    if exists(i, 0):
                        def take_max(c):
                            n = rows(c)
                            v = dve.snap(n_max, min_val=0, max_val=TILES * CHUNKS)
                            dve.tensor_tensor(
                                masked[p][0:n, c, :].rearrange("p (b s) -> p b s", b=TB),
                                ps_s[c][0:n, :].rearrange("p (b s) -> p b s", b=TB),
                                mask_bias[0:n, c, bass.ds(i * TB, TB)].unsqueeze(2).broadcast_to([n, TB, SEQ]),
                                ALU.add).then_inc(chunk_masked, 1)
                            dve.wait_ge(chunk_masked, after(v + 1))
                            dve.wait_ge(chunk_maxed, after(v))
                            dve.tensor_tensor(col_max[0:n, :], col_max[0:n, :], masked[p][0:n, c, :], ALU.max
                                              ).then_inc(chunk_maxed, 1)
                            dve.reg_add(n_max, n_max, 1)

                        if exists(i, -1):
                            dve.wait_ge(max_turned, after(i))
                        dve.memset(col_max[:], -MASKED).then_inc(max_cleared, 1)
                        dve.wait_ge(max_cleared, after(i + 1))
                        dve.wait_ge(scored, after(i + 1))
                        waited(dve)
                        active_chunks(dve, first, take_max)
                        dve.memset(scrap[:, 0:1], 0.0).then_inc(maxed, 1)
                    if exists(i, -1):
                        t = i - 1
                        dve.wait_ge(gathered, after(t + 1))
                        dve.reciprocal(denom[:], ps_o[:, D:D + 1]).then_inc(denom_ready, 1)
                        dve.wait_ge(denom_ready, after(t + 1))
                        dve.tensor_tensor(weight[:], denom[:], valid[:], ALU.mult).then_inc(weight_ready, 1)
                    if exists(i, 0):
                        dve.wait_ge(max_turned, after(i + 1))
                        dve.tensor_reduce(q_max[:], ps_max, AX.X, ALU.max).then_inc(q_maxed, 1)
                        dve.wait_ge(q_maxed, after(i + 1))
                        dve.tensor_scalar(max_diag[:], ident[:], q_max[:, 0:1], None, ALU.mult).then_inc(diag_ready, 1)
                        dve.tensor_scalar(valid[:], q_max[:], -0.5 * MASKED, None, ALU.is_gt)
                    if exists(i, -1):
                        t = i - 1
                        dve.wait_ge(weight_ready, after(t + 1))
                        dve.scalar_tensor_tensor(out=x_all[:, t, :], in0=ps_o[:, 0:D], scalar=weight[:, 0:1],
                                                 in1=x_all[:, t, :], op0=ALU.mult, op1=ALU.add).then_inc(x2_ready, 1)
                        dve.wait_ge(x2_ready, after(t + 1))
                        waited(dve)
                        dve.bn_stats(stats[:], x_all[:, t, :]).then_inc(ln2_stats, 1)
                        dve.wait_ge(ln2_stats, after(t + 1))
                        waited(dve)
                        dve.bn_aggr(moments[:], stats[:]).then_inc(ln2_moments, 1)
                        dve.wait_ge(ln2_moments, after(t + 1))
                        dve.tensor_scalar(var_eps[:], moments[:, 1:2], EPS, None, ALU.add).then_inc(ln2_var, 1)
                    if exists(i, 1):
                        norm_queries(i + 1)
                    if exists(i, -1):
                        dve.wait_ge(ln2_rstd, after(t + 1))
                        dve.tensor_scalar(xn[:], x_all[:, t, :], moments[:, 0:1], rstd[:, 0:1],
                                          ALU.subtract, ALU.mult).then_inc(ln2_normed, 1)
                    if exists(i, 0):
                        def shift(c):
                            n = rows(c)
                            dve.tensor_tensor(masked[p][0:n, c, :], masked[p][0:n, c, :], max_rows[0:n, :],
                                              ALU.subtract)

                        dve.wait_ge(rows_copied, after(i + 1))
                        waited(dve)
                        active_chunks(dve, first, shift)
                        dve.memset(scrap[:, 0:1], 0.0).then_inc(shifted, 1)
                    if exists(i, -1):
                        dve.wait_ge(dt_projected, after(t + 1))
                        dve.tensor_tensor(dt_all[:, t, :], ps_dt, dt_bias_sb[:], ALU.add).then_inc(dt_biased, 1)

                in_step(dve, step, lead=1)

            @block.scalar
            def _(act):
                act.dma_start(x_all[:], x.rearrange("(t p) d -> p t d", p=P)).then_inc(x_loaded, 16)
                act.dma_start(before_last[:], c_before).then_inc(const_loaded, 16)
                act.dma_start(ident[:], c_ident).then_inc(const_loaded, 16)
                act.dma_start(level_sum[:], c_sum).then_inc(weights_loaded, 16)
                act.dma_start(level_mask[:], c_mask).then_inc(weights_loaded, 16)
                act.dma_start(expert_no[:], c_expert).then_inc(weights_loaded, 16)
                act.dma_start(w_in_sb[:], w_in.rearrange("(k p) n -> p k n", p=P)).then_inc(weights_loaded, 16)
                act.dma_start(w_out_sb[:], w_out.rearrange("(k p) n -> p k n", p=P)).then_inc(weights_loaded, 16)
                act.dma_start(w_router_sb[:], w_router.rearrange("(k p) n -> p k n", p=P)).then_inc(weights_loaded, 16)
                act.dma_start(conv_w_sb[:], conv_w.rearrange("(k p) n -> p k n", p=P)).then_inc(weights_loaded, 16)
                act.dma_start(conv_b_sb[:], conv_b).then_inc(weights_loaded, 16)
                act.dma_start(dt_bias_sb[:], dt_bias).then_inc(weights_loaded, 16)
                act.dma_start(neg_a[:], a_log).then_inc(weights_loaded, 16)
                act.dma_start(half_d[:], skip_d).then_inc(weights_loaded, 16)
                act.dma_start(norm_sb[:], norm_w).then_inc(weights_loaded, 16)
                act.wait_ge(ones_set, 1)
                act.activation(scrap[:, 1:2], ones[:, 0:1], ACT.Exp)
                act.wait_ge(first_ready, 1)

                def step(i, p):
                    if exists(i, 0):
                        act.wait_ge(rows_ready, after(i + 1))
                        act.copy(max_rows[:], ps_rows).then_inc(rows_copied, 1)
                    if exists(i, 1):
                        act.wait_ge(q_turned, after(i + 2))
                        act.copy(qt[:], ps_qt).then_inc(q_ready, 1)
                    if exists(i, -1):
                        act.wait_ge(ln2_turned, after(i))
                        if exists(i, -2):
                            act.wait_ge(xt_kept, after(i - 1))
                        act.copy(xt[:], ps_xt).then_inc(ln2_ready, 1)
                    if exists(i, 0):
                        def exponent(c):
                            n = rows(c)
                            act.activation(masked[p][0:n, c, :], masked[p][0:n, c, :], ACT.Exp, scale=D ** -0.5)

                        first = first_of(act, i)
                        act.wait_ge(shifted, after(i + 1))
                        waited(act)
                        active_chunks(act, first, exponent)
                        act.activation(scrap[:, 1:2], ones[:, 0:1], ACT.Exp).then_inc(exped, 1)

                in_step(act, step, lead=1)

            @block.tensor
            def _(pe):
                pe.wait_ge(mask_step, 1)
                pe.wait_ge(ones_set, 1)
                pe.matmul(ps_count, ones[:, 0:1], mask_f[:], start=True, stop=True).then_inc(counted, 1)
                pe.wait_ge(const_loaded, 32)
                pe.wait_ge(weights_loaded, 12 * 16)
                n_ld = [pe.alloc_register(f"pe_chunks_loaded{p}") for p in range(2)]
                for r in n_ld:
                    pe.reg_mov(r, 0)
                pe.wait_ge(first_ready, 1)

                def turn_queries(t):
                    pe.wait_ge(q_normed, after(t + 1))
                    for k in range(KD):
                        last = pe.transpose(ps_qt[:, k, :], qn[:, k * P:(k + 1) * P], ident[:])
                    last.then_inc(q_turned, 1)

                def scores(t, p):
                    def score(c):
                        n = rows(c)
                        for b in range(TB):
                            for k in range(KD):
                                pe.matmul(ps_s[c][0:n, b * SEQ:(b + 1) * SEQ], ctx_t_sb[p][c][:, b, k, 0:n],
                                          qt[:, k, b * SEQ:(b + 1) * SEQ], start=(k == 0), stop=(k == KD - 1))

                    first = first_of(pe, t)
                    pe.reg_add(n_ld[p], n_ld[p],
                               pe.value_load(n_active[0:1, bass.ds(t, 1)], min_val=1, max_val=CHUNKS))
                    pe.wait_ge(ctx_loaded[p], pe.snap(n_ld[p], min_val=1, max_val=TILES * CHUNKS) * 32)
                    pe.wait_ge(q_ready, after(t + 1))
                    active_chunks(pe, first, score)
                    pe.matmul(ps_fence_s, ones[:], ones[:, 0:2], start=True, stop=True).then_inc(scored, 1)

                def step(i, p):
                    t = i - 1
                    if exists(i, 0):
                        pe.wait_ge(maxed, after(i + 1))
                        pe.transpose(ps_max, col_max[:], ident[:]).then_inc(max_turned, 1)
                        pe.wait_ge(diag_ready, after(i + 1))
                        pe.matmul(ps_rows, ones[:], max_diag[:], start=True, stop=True).then_inc(rows_ready, 1)
                    if exists(i, 1):
                        turn_queries(i + 1)
                    if exists(i, -1):
                        pe.wait_ge(ln2_normed, after(t + 1))
                        if exists(i, -2):
                            pe.wait_ge(dt_biased, after(t))
                        for k in range(KD):
                            last = pe.transpose(ps_xt[:, k, :], xn[:, k * P:(k + 1) * P], ident[:])
                        last.then_inc(ln2_turned, 1)
                    if exists(i, 1):
                        scores(i + 1, 1 - p)
                    if exists(i, -1):
                        pe.wait_ge(ln2_ready, after(t + 1))
                        for k in range(KD):
                            last = pe.matmul(ps_dt, xt[:, k, :], w_in_sb[:, k, PROJ - HEADS:PROJ],
                                             start=(k == 0), stop=(k == KD - 1))
                        last.then_inc(dt_projected, 1)
                    if exists(i, 0):
                        def gather(c):
                            n = rows(c)
                            for b in range(TB):
                                pe.matmul(ps_o[b * SEQ:(b + 1) * SEQ, 0:D + 1],
                                          masked[p][0:n, c, b * SEQ:(b + 1) * SEQ],
                                          ctx_sb[p][c][0:n, b, :], start=(c == LAST), stop=(c == LAST),
                                          skip_group_check=True)

                        first = first_of(pe, i)
                        pe.wait_ge(exped, after(i + 1))
                        if exists(i, -1):
                            pe.wait_ge(x2_ready, after(i))
                        waited(pe)
                        active_chunks(pe, first, gather)
                        pe.matmul(ps_fence_o, ones[:], ones[:, 0:2], start=True, stop=True).then_inc(gathered, 1)

                in_step(pe, step, lead=1)

        phase.close()
        w_gu_sb = sb("w_gu_sb", [P, KD, EXPERTS, 2 * EI])
        w_down_sb = sb("w_down_sb", [P, GROUPS * HB, D])
        phase = stack.enter_context(ExitStack())
        step_abs = tmp("step_abs", [P, TILES * HEADS])
        step_exp = tmp("step_exp", [P, TILES * HEADS])
        step_log = tmp("step_log", [P, TILES * HEADS])
        z_abs = sem("z_abs")
        z_exp = sem("z_exp")
        z_log = sem("z_log")
        a_exp = sem("a_exp")
        step_done = sem("step_done")
        gu_loaded = sem("gu_loaded")
        down_loaded = sem("down_loaded")
        dt_flat = dt_all[:].rearrange("p t h -> p (t h)")

        conv = tmp("conv", [P, CB, P])
        conv_tanh = tmp("conv_tanh", [P, CB, P])
        act2 = tmp("act2", [P, CB, P])
        decay = tmp("decay", [P, NL, HEADS])
        g_masked = tmp("g_masked", [P, NL, P])
        g_scrap = tmp("g_scrap", [P, P])
        g_diag = tmp("g_diag", [P, 1])
        own = tmp("own", [P, HEADS])
        xdt = tmp("xdt", [P, INTER])
        xdec = tmp("xdec", [P, NL - 1, INTER])
        flow = tmp("flow", [P, 2, INTER])
        y = tmp("y", [P, INTER])
        gate_tanh = tmp("gate_tanh", [P, INTER])
        gate2 = tmp("gate2", [P, INTER])
        y_gated = tmp("y_gated", [P, INTER])
        y_square = tmp("y_square", [P, INTER])
        y_sum = tmp("y_sum", [P, 1])
        y_var = tmp("y_var", [P, 1])
        y_pow = tmp("y_pow", [P, 1])
        y_rstd = tmp("y_rstd", [P, 1])
        yt = tmp("yt", [P, IB, P])
        xs = tmp("xs", [P, KD, P])
        xr = tmp("xr", [P, KD, P])
        r_max = tmp("r_max", [P, 1])
        r_exp = tmp("r_exp", [P, EXPERTS])
        r_sum = tmp("r_sum", [P, 1])
        r_inv = tmp("r_inv", [P, 1])
        r_prob = tmp("r_prob", [P, EXPERTS])
        top = tmp("top", [P, TOP])
        top_no = tmp("top_no", [P, TOP], U32)
        top_sum = tmp("top_sum", [P, 1])
        top_inv = tmp("top_inv", [P, 1])
        renorm = tmp("renorm", [P, TOP])
        cum = tmp("cum", [P, TOP])
        kept = tmp("kept", [P, TOP])
        kept_sum = tmp("kept_sum", [P, 1])
        kept_inv = tmp("kept_inv", [P, 1])
        kept_w = tmp("kept_w", [P, TOP])
        is_expert = tmp("is_expert", [P, EXPERTS, TOP])
        w_expert = tmp("w_expert", [P, EXPERTS, TOP])

        ps_conv = [bank[0][:, 0:4 * P].rearrange("p (m t) -> p m t", t=P),
                   bank[1][:, 0:2 * P].rearrange("p (m t) -> p m t", t=P)]
        ps_g = bank[1][:, 2 * P:3 * P]
        ps_logit = bank[1][:, 3 * P:3 * P + EXPERTS]
        ps_gate = bank[2]
        ps_x = bank[3]
        ps_decay = bank[4][:, 0:NL * HEADS].rearrange("p (j h) -> p j h", h=HEADS)
        ps_flow = [bank[5], bank[6]]
        ps_yt = bank[4][:, :].rearrange("p (m t) -> p m t", t=P)
        ps_mix = bank[7][:, 0:D]
        ps_x3 = bank[7][:, D:2 * D].rearrange("p (k m) -> p k m", k=KD)

        def ps_conv_block(m):
            return ps_conv[m // 4][:, m % 4, :]

        def by_head(a):
            return a.rearrange("p (h e) -> p h e", e=HD)

        def spread(a):
            return a.unsqueeze(2).broadcast_to([P, HEADS, HD])

        xs_ready = loop_sem("xs_ready")
        conv_projected = loop_sem("conv_projected")
        gate_projected = loop_sem("gate_projected")
        conv_first = loop_sem("conv_first")
        conv_step = loop_sem("conv_step")
        conv_tanhed = loop_sem("conv_tanhed")
        conv_acted = loop_sem("conv_acted")
        decay_summed = loop_sem("decay_summed")
        decay_ready = loop_sem("decay_ready")
        g_ready = loop_sem("g_ready")
        x_turned = loop_sem("x_turned")
        g_split = loop_sem("g_split")
        g_diaged = loop_sem("g_diaged")
        own_ready = loop_sem("own_ready")
        xdt_ready = loop_sem("xdt_ready")
        xdec_ready = loop_sem("xdec_ready")
        flowed = loop_sem("flowed")
        flow_scaled = loop_sem("flow_scaled")
        y_added = loop_sem("y_added")
        gate_tanhed = loop_sem("gate_tanhed")
        gate_acted = loop_sem("gate_acted")
        y_gated_ready = loop_sem("y_gated_ready")
        y_summed = loop_sem("y_summed")
        y_var_ready = loop_sem("y_var_ready")
        y_pow_ready = loop_sem("y_pow_ready")
        y_rstd_ready = loop_sem("y_rstd_ready")
        y_turned = loop_sem("y_turned")
        yt_ready = loop_sem("yt_ready")
        mixed = loop_sem("mixed")
        x3_ready = loop_sem("x3_ready")
        ln3_stats = loop_sem("ln3_stats")
        ln3_moments = loop_sem("ln3_moments")
        ln3_var = loop_sem("ln3_var")
        ln3_rstd = loop_sem("ln3_rstd")
        ln3_normed = loop_sem("ln3_normed")
        ln3_turned = loop_sem("ln3_turned")
        xr_ready = loop_sem("xr_ready")
        xr_kept = sem("xr_kept")
        routed = loop_sem("routed")
        router_step = loop_sem("router_step")
        r_exped = loop_sem("r_exped")

        with nc.Block() as block:
            @block.sync
            def _(sp):
                start_loop_sems(sp)

        with nc.Block() as block:
            @block.sync
            def _(sp):
                for n, e in enumerate(range(0, EXPERTS, 8)):
                    sp.dma_start(w_gu_sb[:, :, e:e + 8, :],
                                 w_gu.rearrange("(k p) e f -> p k e f", p=P)[:, :, e:e + 8, :]).then_inc(gu_loaded, 16)
                sp.dma_start(w_down_sb[:], w_down.rearrange("(n p) d -> p n d", p=P)).then_inc(down_loaded, 16)

            @block.scalar
            def _(act):
                act.activation(neg_a[:], neg_a[:], ACT.Exp).then_inc(a_exp, 1)
                act.activation(step_abs[:], dt_flat, ACT.Abs).then_inc(z_abs, 1)
                act.wait_ge(z_abs, 1)
                act.activation(step_exp[:], step_abs[:], ACT.Exp, scale=-1.0).then_inc(z_exp, 1)
                act.wait_ge(z_exp, 1)
                act.activation(step_log[:], step_exp[:], ACT.Ln, bias=1.0).then_inc(z_log, 1)
                act.activation(y_sum[:], ones[:, 0:1], ACT.Exp)
                with act.Fori(0, TILES) as t:
                    act.wait_ge(gate_projected, after(t))
                    waited(act)
                    act.copy(xs[:].rearrange("p k m -> p (k m)"), xt_all[:, t, :]).then_inc(xs_ready, 1)
                    act.wait_ge(conv_projected, after(t + 1))
                    act.wait_ge(conv_acted, after(t))
                    for m in CONV_ORDER:
                        act.activation(conv[:, m, :], ps_conv_block(m), ACT.Identity, bias=conv_b_sb[:, m:m + 1],
                                       scale=conv_w_sb[:, m, TAPS - 1:TAPS]).then_inc(conv_first, 1)
                    act.wait_ge(decay_summed, after(t + 1))
                    act.activation(decay[:], ps_decay, ACT.Exp).then_inc(decay_ready, 1)
                    act.wait_ge(conv_step, after((t + 1) * (TAPS - 1) * CB))
                    act.activation(conv_tanh[:], conv[:], ACT.Tanh, scale=0.5).then_inc(conv_tanhed, 1)
                    act.wait_ge(gate_projected, after(t + 1))
                    act.activation(gate_tanh[:], ps_gate[:], ACT.Tanh, scale=0.5).then_inc(gate_tanhed, 1)
                    act.wait_ge(y_gated_ready, after(t + 1))
                    act.activation(y_square[:], y_gated[:], ACT.Square, accum_out=y_sum[:]).then_inc(y_summed, 1)
                    act.wait_ge(y_turned, after(t + 1))
                    act.copy(yt[:], ps_yt).then_inc(yt_ready, 1)
                    act.wait_ge(ln3_turned, after(t + 1))
                    act.copy(xr[:], ps_x3).then_inc(xr_ready, 1)
                    act.wait_ge(xr_ready, after(t + 1))
                    waited(act)
                    act.copy(xt_all[:, t, :], xr[:].rearrange("p k m -> p (k m)")).then_inc(xr_kept, 1)
                    act.wait_ge(router_step, after(t * ROUTER_STEPS + 1))
                    act.activation(r_exp[:], ps_logit, ACT.Exp, bias=r_max[:, 0:1], accum_out=r_sum[:]
                                   ).then_inc(r_exped, 1)

            @block.gpsimd
            def _(pool):
                with pool.Fori(0, TILES) as t:
                    pool.wait_ge(decay_ready, after(t + 1))
                    pool.wait_ge(xdt_ready, after(t + 1))
                    for j in range(NL - 1):
                        pool.tensor_tensor(by_head(xdec[:, j, :]), by_head(xdt[:]), spread(decay[:, j, :]),
                                           ALU.mult).then_inc(xdec_ready, 1)
                    pool.wait_ge(y_var_ready, after(t + 1))
                    pool.tensor_tensor(y_pow[:], y_var[:], minus_half[:, 0:1], ALU.pow).then_inc(y_pow_ready, 1)
                    pool.wait_ge(ln3_var, after(t + 1))
                    pool.tensor_tensor(rstd[:], var_eps[:], minus_half[:, 0:1], ALU.pow).then_inc(ln3_rstd, 1)

            @block.vector
            def _(dve):
                dve.wait_ge(z_log, 1)
                dve.scalar_tensor_tensor(out=dt_flat, in0=dt_flat, scalar=0.0, in1=step_log[:],
                                         op0=ALU.max, op1=ALU.add).then_inc(step_done, 1)
                dve.wait_ge(step_done, 1)
                dve.tensor_scalar(dt_flat, dt_flat, 0.0, 100.0, ALU.max, ALU.min).then_inc(step_done, 1)
                dve.wait_ge(a_exp, 1)
                dve.tensor_scalar(neg_a[:], neg_a[:], -1.0, None, ALU.mult).then_inc(step_done, 1)
                dve.wait_ge(step_done, 3)
                dve.tensor_tensor(adt_all[:], dt_all[:], neg_a[:].unsqueeze(1).broadcast_to([P, TILES, HEADS]),
                                  ALU.mult).then_inc(step_done, 1)
                dve.wait_ge(step_done, 4)
                dve.tensor_scalar(dt_flat, dt_flat, 0.5, None, ALU.mult).then_inc(step_done, 1)
                dve.tensor_scalar(half_d[:], half_d[:], 0.5, None, ALU.mult).then_inc(step_done, 1)
                for m in range(IB):
                    dve.tensor_scalar(w_out_sb[:, m, :], w_out_sb[:, m, :], norm_sb[:, m:m + 1], None, ALU.mult
                                      ).then_inc(step_done, 1)
                dve.wait_ge(step_done, 6 + IB)
                with dve.Fori(0, TILES) as t:
                    for n, (k, m) in enumerate(CONV_STEPS):
                            if k == 1:
                                dve.wait_ge(conv_first, after(t * CB + (2 if m in CONV_ORDER[:2] else CB)))
                            else:
                                dve.wait_ge(conv_step, after(t * len(CONV_STEPS) + CONV_STEPS.index((k - 1, m)) + 1))
                            now = conv[:, m, :].rearrange("p (b s) -> p b s", b=TB)[:, :, k:]
                            dve.scalar_tensor_tensor(
                                out=now, in0=ps_conv_block(m).rearrange("p (b s) -> p b s", b=TB)[:, :, 0:SEQ - k],
                                scalar=conv_w_sb[:, m, TAPS - 1 - k:TAPS - k], in1=now,
                                op0=ALU.mult, op1=ALU.add).then_inc(conv_step, 1)
                    dve.wait_ge(conv_tanhed, after(t + 1))
                    dve.scalar_tensor_tensor(out=act2[:].rearrange("p m t -> p (m t)"),
                                             in0=conv_tanh[:].rearrange("p m t -> p (m t)"), scalar=1.0,
                                             in1=conv[:].rearrange("p m t -> p (m t)"), op0=ALU.add, op1=ALU.mult
                                             ).then_inc(conv_acted, 1)
                    dve.wait_ge(gate_tanhed, after(t + 1))
                    dve.scalar_tensor_tensor(out=gate2[:], in0=gate_tanh[:], scalar=1.0, in1=ps_gate[:],
                                             op0=ALU.add, op1=ALU.mult).then_inc(gate_acted, 1)
                    dve.wait_ge(x_turned, after(t + 1))
                    dve.wait_ge(xdec_ready, after(t * (NL - 1)))
                    dve.tensor_tensor(by_head(xdt[:]), by_head(ps_x[:]), spread(dt_all[:, t, :]), ALU.mult
                                      ).then_inc(xdt_ready, 1)
                    dve.wait_ge(g_ready, after(t + 1))
                    dve.tensor_tensor(g_masked[:], ps_g.unsqueeze(1).broadcast_to([P, NL, P]), level_mask[:],
                                      ALU.mult).then_inc(g_split, 1)
                    dve.tensor_tensor_reduce(out=g_scrap[:], in0=ps_g, in1=ident[:], scale=0.25, scalar=0.0,
                                             op0=ALU.mult, op1=ALU.add, accum_out=g_diag[:]).then_inc(g_diaged, 1)
                    dve.wait_ge(g_diaged, after(t + 1))
                    dve.scalar_tensor_tensor(out=own[:], in0=dt_all[:, t, :], scalar=g_diag[:, 0:1], in1=half_d[:],
                                             op0=ALU.mult, op1=ALU.add).then_inc(own_ready, 1)
                    dve.wait_ge(own_ready, after(t + 1))
                    dve.tensor_tensor(by_head(y[:]), by_head(ps_x[:]), spread(own[:]), ALU.mult
                                      ).then_inc(y_added, 1)
                    for n in range(NL):
                        j = NL - 1 - n
                        dve.wait_ge(flowed, after(t * NL + n + 1))
                        if n == 0:
                            dve.wait_ge(decay_ready, after(t + 1))
                        dve.tensor_tensor(by_head(flow[:, n % 2, :]), by_head(ps_flow[n % 2][:]),
                                          spread(decay[:, j, :]), ALU.mult).then_inc(flow_scaled, 1)
                        dve.wait_ge(flow_scaled, after(t * NL + n + 1))
                        dve.wait_ge(y_added, after(t * (NL + 1) + n + 1))
                        dve.tensor_tensor(y[:], y[:], flow[:, n % 2, :], ALU.add).then_inc(y_added, 1)
                    dve.wait_ge(gate_acted, after(t + 1))
                    dve.wait_ge(y_added, after((t + 1) * (NL + 1)))
                    dve.tensor_tensor(y_gated[:], y[:], gate2[:], ALU.mult).then_inc(y_gated_ready, 1)
                    dve.wait_ge(y_summed, after(t + 1))
                    dve.tensor_scalar(y_var[:], y_sum[:], 0.25 / INTER, EPS, ALU.mult, ALU.add
                                      ).then_inc(y_var_ready, 1)
                    dve.wait_ge(y_pow_ready, after(t + 1))
                    dve.tensor_scalar(y_rstd[:], y_pow[:], 0.5, None, ALU.mult).then_inc(y_rstd_ready, 1)
                    dve.wait_ge(y_rstd_ready, after(t + 1))
                    dve.wait_ge(mixed, after(t + 1))
                    dve.scalar_tensor_tensor(out=x_all[:, t, :], in0=ps_mix, scalar=y_rstd[:, 0:1],
                                             in1=x_all[:, t, :], op0=ALU.mult, op1=ALU.add).then_inc(x3_ready, 1)
                    dve.wait_ge(x3_ready, after(t + 1))
                    waited(dve)
                    dve.bn_stats(stats[:], x_all[:, t, :]).then_inc(ln3_stats, 1)
                    dve.wait_ge(ln3_stats, after(t + 1))
                    waited(dve)
                    dve.bn_aggr(moments[:], stats[:]).then_inc(ln3_moments, 1)
                    dve.wait_ge(ln3_moments, after(t + 1))
                    dve.tensor_scalar(var_eps[:], moments[:, 1:2], EPS, None, ALU.add).then_inc(ln3_var, 1)
                    dve.wait_ge(ln3_rstd, after(t + 1))
                    dve.tensor_scalar(xn[:], x_all[:, t, :], moments[:, 0:1], rstd[:, 0:1],
                                      ALU.subtract, ALU.mult).then_inc(ln3_normed, 1)

                    steps = [0]

                    def then(instruction):
                        steps[0] += 1
                        instruction.then_inc(router_step, 1)
                        dve.wait_ge(router_step, after(t * ROUTER_STEPS + steps[0]))

                    dve.wait_ge(routed, after(t + 1))
                    then(dve.tensor_reduce(r_max[:], ps_logit, AX.X, ALU.max, negate=True))
                    dve.wait_ge(r_exped, after(t + 1))
                    then(dve.reciprocal(r_inv[:], r_sum[:]))
                    then(dve.tensor_scalar(r_prob[:], r_exp[:], r_inv[:, 0:1], None, ALU.mult))
                    waited(dve)
                    then(dve.max(top[:], r_prob[:]))
                    waited(dve)
                    then(dve.max_index(top_no[:], top[:], r_prob[:]))
                    then(dve.tensor_reduce(top_sum[:], top[:], AX.X, ALU.add))
                    then(dve.tensor_scalar(top_sum[:], top_sum[:], 1e-12, None, ALU.max))
                    then(dve.reciprocal(top_inv[:], top_sum[:]))
                    then(dve.tensor_scalar(renorm[:], top[:], top_inv[:, 0:1], None, ALU.mult))
                    then(dve.tensor_tensor_scan(cum[:], renorm[:], renorm[:], 0.0, ALU.add, ALU.bypass))
                    then(dve.tensor_copy(kept[:, 0:1], top[:, 0:1]))
                    then(dve.scalar_tensor_tensor(out=kept[:, 1:TOP], in0=cum[:, 0:TOP - 1], scalar=KEEP,
                                                  in1=top[:, 1:TOP], op0=ALU.is_lt, op1=ALU.mult))
                    then(dve.tensor_reduce(kept_sum[:], kept[:], AX.X, ALU.add))
                    then(dve.tensor_scalar(kept_sum[:], kept_sum[:], 1e-12, None, ALU.max))
                    then(dve.reciprocal(kept_inv[:], kept_sum[:]))
                    then(dve.tensor_scalar(kept_w[:], kept[:], kept_inv[:, 0:1], None, ALU.mult))
                    then(dve.tensor_tensor(is_expert[:], expert_no[:],
                                           top_no[:].unsqueeze(1).broadcast_to([P, EXPERTS, TOP]), ALU.is_equal))
                    then(dve.tensor_tensor(w_expert[:], is_expert[:],
                                           kept_w[:].unsqueeze(1).broadcast_to([P, EXPERTS, TOP]), ALU.mult))
                    then(dve.tensor_reduce(comb_all[:, t, :], w_expert[:], AX.X, ALU.add))
                    assert steps[0] == ROUTER_STEPS

            @block.tensor
            def _(pe):
                pe.wait_ge(step_done, 6 + IB)
                with pe.Fori(0, TILES) as t:
                    pe.wait_ge(xs_ready, after(t + 1))
                    pe.wait_ge(conv_step, after(t * (TAPS - 1) * CB))
                    pe.wait_ge(r_exped, after(t))
                    for m in range(CB):
                        for k in range(KD):
                            last = pe.matmul(ps_conv_block(m), w_in_sb[:, k, INTER + m * P:INTER + (m + 1) * P],
                                             xs[:, k, :], start=(k == 0), stop=(k == KD - 1))
                    last.then_inc(conv_projected, 1)
                    pe.wait_ge(gate_acted, after(t))
                    for k in range(KD):
                        last = pe.matmul(ps_gate[:], xs[:, k, :], w_in_sb[:, k, 0:INTER],
                                         start=(k == 0), stop=(k == KD - 1))
                    last.then_inc(gate_projected, 1)
                    pe.wait_ge(yt_ready, after(t))
                    for j in range(NL):
                        last = pe.matmul(ps_decay[:, j, :], level_sum[:, j, :], adt_all[:, t, :],
                                         start=True, stop=True)
                    last.then_inc(decay_summed, 1)
                    pe.wait_ge(conv_acted, after(t + 1))
                    pe.wait_ge(y_added, after(t * (NL + 1)))
                    for m in range(IB):
                        last = pe.transpose(ps_x[:, m * P:(m + 1) * P], act2[:, m, :], ident[:])
                    last.then_inc(x_turned, 1)
                    pe.matmul(ps_g, act2[:, IB, :], act2[:, IB + 1, :], start=True, stop=True).then_inc(g_ready, 1)
                    pe.wait_ge(g_split, after(t + 1))
                    for n in range(NL):
                        j = NL - 1 - n
                        if n == 0:
                            pe.wait_ge(xdt_ready, after(t + 1))
                        else:
                            pe.wait_ge(xdec_ready, after(t * (NL - 1) + j + 1))
                        if n >= 2:
                            pe.wait_ge(flow_scaled, after(t * NL + n - 1))
                        pe.matmul(ps_flow[n % 2][:], g_masked[:, j, :], xdt[:] if n == 0 else xdec[:, j, :],
                                  start=True, stop=True).then_inc(flowed, 1)
                    pe.wait_ge(y_gated_ready, after(t + 1))
                    for m in range(IB):
                        last = pe.transpose(ps_yt[:, m, :], y_gated[:, m * P:(m + 1) * P], ident[:])
                    last.then_inc(y_turned, 1)
                    pe.wait_ge(yt_ready, after(t + 1))
                    for m in range(IB):
                        last = pe.matmul(ps_mix, yt[:, m, :], w_out_sb[:, m, :], start=(m == 0), stop=(m == IB - 1))
                    last.then_inc(mixed, 1)
                    pe.wait_ge(ln3_normed, after(t + 1))
                    for k in range(KD):
                        last = pe.transpose(ps_x3[:, k, :], xn[:, k * P:(k + 1) * P], ident[:])
                    last.then_inc(ln3_turned, 1)
                    pe.wait_ge(xr_ready, after(t + 1))
                    for k in range(KD):
                        last = pe.matmul(ps_logit, xr[:, k, :], w_router_sb[:, k, :], start=(k == 0), stop=(k == KD - 1))
                    last.then_inc(routed, 1)

        phase.close()
        phase = stack.enter_context(ExitStack())
        xe = tmp("xe", [P, KD, P])
        gate = tmp("gate", [P, 2, GW])
        up_gate = tmp("up_gate", [P, 2, GW])
        hidden = tmp("hidden", [P, 2, GW])
        ht = tmp("ht", [P, 2, GW])
        ps_gate_e = [bank[0][:, 0:GW], bank[1][:, 0:GW]]
        ps_up_e = [bank[2][:, 0:GW], bank[3][:, 0:GW]]
        ps_ht = [bank[4][:, 0:GW], bank[5][:, 0:GW]]
        ps_y = bank[6][:, 0:D]

        xe_ready = loop_sem("xe_ready")
        gu_projected = loop_sem("gu_projected")
        gate_silued = loop_sem("gate_silued")
        up_gated = loop_sem("up_gated")
        weighted = loop_sem("weighted")
        h_turned = loop_sem("h_turned")
        ht_ready = loop_sem("ht_ready")
        downed = sem("downed")
        summed = loop_sem("summed")
        added = loop_sem("added")
        stored = sem("stored")

        with nc.Block() as block:
            @block.sync
            def _(sp):
                start_loop_sems(sp)

        with nc.Block() as block:
            @block.sync
            def _(sp):
                out_v = out.rearrange("(t p) d -> t p d", p=P)
                with sp.Fori(0, TILES) as t:
                    sp.wait_ge(added, after(t + 1))
                    sp.dma_start(out_v[t], x_all[:, t, :]).then_inc(stored, 16)
                sp.wait_ge(stored, TILES * 16)

            @block.scalar
            def _(act):
                act.activation(gate[:, 0, 0:1], ones[:, 0:1], ACT.Silu)
                with act.Fori(0, TILES) as t:
                    act.wait_ge(gu_projected, after(t * GROUPS))
                    waited(act)
                    act.copy(xe[:].rearrange("p k m -> p (k m)"), xt_all[:, t, :]).then_inc(xe_ready, 1)
                    for g in range(GROUPS + 1):
                        if g < GROUPS:
                            act.wait_ge(gu_projected, after(t * GROUPS + g + 1))
                            act.activation(gate[:, g % 2, :], ps_gate_e[g % 2], ACT.Silu).then_inc(gate_silued, 1)
                        if g >= 1:
                            act.wait_ge(h_turned, after(t * GROUPS + g))
                            act.copy(ht[:, (g - 1) % 2, :], ps_ht[(g - 1) % 2]).then_inc(ht_ready, 1)

            @block.gpsimd
            def _(pool):
                with pool.Fori(0, TILES) as t:
                    for g in range(GROUPS):
                        pool.wait_ge(up_gated, after(t * GROUPS + g + 1))
                        pool.tensor_tensor(hidden[:, g % 2, :].rearrange("p (e f) -> p e f", e=GE),
                                           up_gate[:, g % 2, :].rearrange("p (e f) -> p e f", e=GE),
                                           comb_all[:, t, g * GE:(g + 1) * GE].unsqueeze(2).broadcast_to([P, GE, EI]),
                                           ALU.mult).then_inc(weighted, 1)

            @block.vector
            def _(dve):
                with dve.Fori(0, TILES) as t:
                    for g in range(GROUPS):
                        dve.wait_ge(gate_silued, after(t * GROUPS + g + 1))
                        if g >= 2:
                            dve.wait_ge(weighted, after(t * GROUPS + g - 1))
                        dve.tensor_tensor(up_gate[:, g % 2, :], gate[:, g % 2, :], ps_up_e[g % 2], ALU.mult
                                          ).then_inc(up_gated, 1)
                    dve.wait_ge(summed, after(t + 1))
                    dve.tensor_tensor(x_all[:, t, :], ps_y, x_all[:, t, :], ALU.add).then_inc(added, 1)

            @block.tensor
            def _(pe):
                pe.wait_ge(gu_loaded, 64)
                pe.wait_ge(down_loaded, 16)
                with pe.Fori(0, TILES) as t:
                    def project(g):
                        if g == 0:
                            pe.wait_ge(xe_ready, after(t + 1))
                        if g >= 2:
                            pe.wait_ge(up_gated, after(t * GROUPS + g - 1))
                        for ps, f in ((ps_gate_e, 0), (ps_up_e, EI)):
                            for k in range(KD):
                                last = pe.matmul(ps[g % 2].rearrange("p (e f) -> p e f", e=GE), xe[:, k, :],
                                                 w_gu_sb[:, k, g * GE:(g + 1) * GE, f:f + EI],
                                                 start=(k == 0), stop=(k == KD - 1))
                        last.then_inc(gu_projected, 1)

                    def turn(g):
                        pe.wait_ge(weighted, after(t * GROUPS + g + 1))
                        for m in range(HB):
                            last = pe.transpose(ps_ht[g % 2][:, m * P:(m + 1) * P],
                                                hidden[:, g % 2, m * P:(m + 1) * P], ident[:])
                        last.then_inc(h_turned, 1)

                    def down(g):
                        if g == 0:
                            pe.wait_ge(added, after(t))
                        pe.wait_ge(ht_ready, after(t * GROUPS + g + 1))
                        for m in range(HB):
                            last = pe.matmul(ps_y, ht[:, g % 2, m * P:(m + 1) * P], w_down_sb[:, g * HB + m, :],
                                             start=(g == 0 and m == 0), stop=(g == GROUPS - 1 and m == HB - 1))
                        last.then_inc(summed if g == GROUPS - 1 else downed, 1)

                    for g in range(GROUPS + 2):
                        if g < GROUPS:
                            project(g)
                        if g >= 2:
                            down(g - 2)
                        if 1 <= g <= GROUPS:
                            turn(g - 1)


def after(n):
    return n + 1


ROUTER_STEPS = 19
CONV_ORDER = (4, 5, 0, 1, 2, 3)
CONV_STEPS = [(k, m) for part in (CONV_ORDER[:2], CONV_ORDER[2:]) for k in range(1, TAPS) for m in part]


def level_constants():
    import numpy as np

    at = np.arange(P)
    total = np.zeros((P, NL, P), np.float32)
    mask = np.zeros((P, NL, P), np.float32)
    for j, half in enumerate(LEVELS):
        block = at // (2 * half)
        second = at % (2 * half) >= half
        middle = block * 2 * half + half - 1
        k, tok = at[:, None], at[None, :]
        same = block[:, None] == block[None, :]
        after = same & second[None, :] & (k > middle[None, :]) & (k <= tok)
        before = same & ~second[None, :] & (k > tok) & (k <= middle[None, :])
        total[:, j, :] = after | before
        mask[:, j, :] = 0.25 * (same & ~second[:, None] & second[None, :])
    return total, mask


def kernel(x, ctx_2048, mask_BxS2_bk0, L0_attn_in_proj_w, L0_attn_conv_w, L0_attn_conv_b, L0_attn_dt_bias,
           L0_attn_A_log, L0_attn_D, L0_attn_norm_w, L0_attn_out_proj_w, L0_ffn_gate_weight,
           L0_ffn_gate_up_proj, L0_ffn_down_proj):
    import numpy as np
    import concourse.bacc as bacc
    from concourse.bass_utils import run_bass_kernel_spmd

    a = np.asarray
    total, mask = level_constants()
    ctx = a(ctx_2048).reshape(TILES, TB, CTX, D)
    arrays = {
        "x": a(x).reshape(TOK, D),
        "ctx": ctx,
        "ctx_t": ctx.transpose(0, 1, 3, 2),
        "mask_t": a(mask_BxS2_bk0).T,
        "w_in": a(L0_attn_in_proj_w).T,
        "conv_w": a(L0_attn_conv_w).reshape(CONV, TAPS),
        "conv_b": a(L0_attn_conv_b).reshape(CB, P).T,
        "dt_bias": np.broadcast_to(a(L0_attn_dt_bias), (P, HEADS)),
        "a_log": np.broadcast_to(a(L0_attn_A_log), (P, HEADS)),
        "skip_d": np.broadcast_to(a(L0_attn_D), (P, HEADS)),
        "norm_w": a(L0_attn_norm_w).reshape(IB, P).T,
        "w_out": a(L0_attn_out_proj_w).T,
        "w_router": a(L0_ffn_gate_weight).T,
        "w_gu": a(L0_ffn_gate_up_proj).transpose(2, 0, 1),
        "w_down": a(L0_ffn_down_proj).transpose(0, 2, 1).reshape(EXPERTS * EI, D),
        "c_before": np.broadcast_to(np.arange(-LAST, 1, dtype=np.float32)[None, :, None], (1, CHUNKS, TILES)),
        "c_ident": np.eye(P, dtype=np.float32),
        "c_sum": total,
        "c_mask": mask,
        "c_expert": np.broadcast_to(np.arange(EXPERTS, dtype=np.float32)[None, :, None], (P, EXPERTS, TOP)),
    }
    arrays = {f"in_{k}": np.ascontiguousarray(v) for k, v in arrays.items()}
    nc = bacc.Bacc("TRN2", target_bir_lowering=False, num_devices=1)
    args = [nc.dram_tensor(k, v.shape, mybir.dt.from_np(v.dtype), kind="ExternalInput").ap()
            for k, v in arrays.items()]
    out = nc.dram_tensor("out_dram", (TOK, D), F32, kind="ExternalOutput").ap()
    build(nc, *args, out)
    r = run_bass_kernel_spmd(nc, [arrays], core_ids=[0])
    return r.results[0]["out_dram"].reshape(B, SEQ, D)
```

```python
from contextlib import ExitStack

import concourse.bass as bass
from concourse import mybir

F32 = mybir.dt.float32
F32R = mybir.dt.float32r
I32 = mybir.dt.int32
U32 = mybir.dt.uint32
U8 = mybir.dt.uint8
ALU = mybir.AluOpType
ACT = mybir.ActivationFunctionType
AX = mybir.AxisListType

P = 128
D = 256
KD = D // P
B, SEQ, CTX = 32, 64, 1601
TOK = B * SEQ
TILES = TOK // P
TB = P // SEQ
CHUNKS = -(-CTX // P)
LAST = CHUNKS - 1
LAST_ROWS = CTX - LAST * P
INTER, STATE, HEADS, HD, TAPS = 512, 128, 64, 8, 4
CONV = INTER + 2 * STATE
CB = CONV // P
IB = INTER // P
PROJ = INTER + CONV + HEADS
LEVELS = (32, 16, 8, 4, 2, 1)
NL = len(LEVELS)
EXPERTS, TOP, EI, KEEP = 32, 8, 96, 0.8
FEATURES = EXPERTS * EI
FB = FEATURES // P
TG = 4
GROUPS = TILES // TG
GT = TG * P
EPS = 1e-5
MASKED = 1e30
EARLY = 2
FIRST = 2
STAGES = 4
RT = 4
ROUTER_PARTS = ((0, TILES - RT), (TILES - RT, TILES))


def build(nc, x, ctx, ctx_t, mask_t, w_in, conv_w, conv_b, dt_bias, a_log, skip_d, norm_w, w_out,
          w_router, w_experts, c_before, c_ident, c_sum, c_mask, c_expert, c_select, out):
    with ExitStack() as stack:
        def sb(name, shape, dt=F32):
            return stack.enter_context(nc.sbuf_tensor(name, shape, dt))

        def sem(name):
            return stack.enter_context(nc.semaphore(name))

        fresh = []

        def loop_sem(name):
            fresh.append(sem(name))
            return fresh[-1]

        def start_loop_sems(eng):
            for s in fresh:
                eng.sem_inc(s, 1)
            fresh.clear()

        bank = [stack.enter_context(nc.psum_tensor(f"bank{n}", [P, 512], F32)) for n in range(8)]

        ident = sb("ident", [P, P])
        x_all = sb("x_all", [P, TILES, D])
        xt_all = sb("xt_all", [P, TILES, D])
        comb_all = sb("comb_all", [P, TILES, EXPERTS])

        before_experts = stack.enter_context(ExitStack())

        def kept_until_experts(name, shape, dt=F32):
            return before_experts.enter_context(nc.sbuf_tensor(name, shape, dt))

        ones = kept_until_experts("ones", [P, P])
        level_sum = kept_until_experts("level_sum", [P, NL, P])
        level_mask = kept_until_experts("level_mask", [P, NL, P])
        expert_no = kept_until_experts("expert_no", [P, EXPERTS, TOP])
        minus_half = kept_until_experts("minus_half", [P, TILES])
        w_in_sb = kept_until_experts("w_in_sb", [P, KD, PROJ])
        w_out_sb = kept_until_experts("w_out_sb", [P, IB, D])
        w_router_sb = kept_until_experts("w_router_sb", [P, KD, EXPERTS])
        conv_w_sb = kept_until_experts("conv_w_sb", [P, CB, TAPS])
        conv_b_sb = kept_until_experts("conv_b_sb", [P, CB])
        dt_bias_sb = kept_until_experts("dt_bias_sb", [P, HEADS])
        neg_a = kept_until_experts("neg_a", [P, HEADS])
        half_d = kept_until_experts("half_d", [P, HEADS])
        norm_sb = kept_until_experts("norm_sb", [P, IB])
        dt_all = kept_until_experts("dt_all", [P, TILES, HEADS])
        adt_all = kept_until_experts("adt_all", [P, TILES, HEADS])
        logits = kept_until_experts("logits", [P, TILES, EXPERTS])
        xn = kept_until_experts("xn", [P, D])
        xt = kept_until_experts("xt", [P, KD, P])
        stats = kept_until_experts("stats", [P, 6])
        moments = kept_until_experts("moments", [P, 2])
        var_eps = kept_until_experts("var_eps", [P, 1])
        rstd = kept_until_experts("rstd", [P, 1])

        phase = before_experts.enter_context(ExitStack())

        def tmp(name, shape, dt=F32):
            return phase.enter_context(nc.sbuf_tensor(name, shape, dt))

        CW = TB * D + TB * (D + 1)
        chunks = tmp("chunks", [P, 2, CHUNKS, CW])
        ctx_t_sb = [[chunks[:, p, c, 0:TB * D].rearrange("p (b k m) -> p b k m", b=TB, k=KD)
                     for c in range(CHUNKS)] for p in range(2)]
        ctx_sb = [[chunks[:, p, c, TB * D:CW].rearrange("p (b d) -> p b d", b=TB)
                   for c in range(CHUNKS)] for p in range(2)]
        mask_u8 = tmp("mask_u8", [P, CHUNKS, B], U8)
        mask_f = tmp("mask_f", [P, CHUNKS * B])
        mask_bias = tmp("mask_bias", [P, CHUNKS, B])
        count = tmp("count", [1, CHUNKS * TILES])
        before_last = tmp("before_last", [1, CHUNKS, TILES])
        any_active = tmp("any_active", [1, CHUNKS * TILES])
        first_f = tmp("first_f", [1, TILES])
        first_chunk = tmp("first_chunk", [1, TILES], I32)
        n_active = tmp("n_active", [1, TILES], I32)
        stats1 = tmp("stats1", [P, TILES, 6])
        moments1 = tmp("moments1", [P, TILES, 2])
        var1 = tmp("var1", [P, TILES])
        rstd1 = tmp("rstd1", [P, TILES])
        qn = tmp("qn", [P, D])
        qt = tmp("qt", [P, KD, P])
        col_max = tmp("col_max", [P, P])
        q_max = tmp("q_max", [P, 1])
        max_diag = tmp("max_diag", [P, P])
        max_rows = tmp("max_rows", [P, P])
        masked = [tmp(f"masked{p}", [P, CHUNKS, P]) for p in range(2)]
        valid = [tmp(f"valid{p}", [P, 1]) for p in range(2)]
        denom = tmp("denom", [P, 1])
        weight = tmp("weight", [P, 1])
        scrap = tmp("scrap", [P, 2])

        ps_qt = bank[0][:, 0:D].rearrange("p (k m) -> p k m", k=KD)
        ps_fence_s = bank[0][:, 510:512]
        ps_s = [bank[1 + c // 4][:, (c % 4) * P:(c % 4 + 1) * P] for c in range(CHUNKS)]
        ps_o = bank[5]
        ps_fence_o = bank[5][:, 510:512]
        ps_max = bank[6][:, 0:P]
        ps_rows = bank[6][:, P:2 * P]
        ps_xt = bank[7][:, 0:D].rearrange("p (k m) -> p k m", k=KD)
        ps_dt = bank[7][:, D:D + HEADS]
        ps_count = bank[7][0:1, 0:CHUNKS * B]

        ln1_parts = (slice(0, FIRST), slice(FIRST, TILES))
        x_loaded = sem("x_loaded")
        mask_cleared = sem("mask_cleared")
        mask_loaded = sem("mask_loaded")
        const_loaded = sem("const_loaded")
        weights_loaded = sem("weights_loaded")
        ones_set = sem("ones_set")
        half_set = sem("half_set")
        mask_step = sem("mask_step")
        counted = sem("counted")
        first_ready = sem("first_ready")
        ln1_step = sem("ln1_step")
        ln1_rstd = sem("ln1_rstd")
        ones_col = sem("ones_col")
        ctx_t_loaded = [sem("ctx_t_loaded0"), sem("ctx_t_loaded1")]
        ctx_loaded = [sem("ctx_loaded0"), sem("ctx_loaded1")]
        wait_taken = sem("wait_taken")
        q_normed = loop_sem("q_normed")
        q_turned = loop_sem("q_turned")
        q_ready = loop_sem("q_ready")
        scored = loop_sem("scored")
        max_cleared = loop_sem("max_cleared")
        chunk_masked = loop_sem("chunk_masked")
        chunk_maxed = loop_sem("chunk_maxed")
        maxed = loop_sem("maxed")
        max_turned = loop_sem("max_turned")
        q_maxed = loop_sem("q_maxed")
        diag_ready = loop_sem("diag_ready")
        rows_ready = loop_sem("rows_ready")
        rows_copied = loop_sem("rows_copied")
        shifted = loop_sem("shifted")
        exped = loop_sem("exped")
        gathered = loop_sem("gathered")
        denom_ready = loop_sem("denom_ready")
        weight_ready = loop_sem("weight_ready")
        x2_ready = loop_sem("x2_ready")
        ln2_stats = loop_sem("ln2_stats")
        ln2_moments = loop_sem("ln2_moments")
        ln2_var = loop_sem("ln2_var")
        ln2_rstd = loop_sem("ln2_rstd")
        ln2_normed = loop_sem("ln2_normed")
        ln2_turned = loop_sem("ln2_turned")
        ln2_ready = loop_sem("ln2_ready")
        xt_kept = loop_sem("xt_kept")
        dt_projected = loop_sem("dt_projected")
        dt_biased = loop_sem("dt_biased")

        def waited(eng):
            eng.sem_inc(wait_taken, 1)

        def first_of(eng, t):
            return eng.value_load(first_chunk[0:1, bass.ds(t, 1)], min_val=0, max_val=LAST)

        def active_chunks(eng, first, work):
            work(LAST)

            def back(c):
                if c >= 0:
                    with eng.If(first <= c):
                        work(c)
                        back(c - 1)

            back(LAST - 1)

        def rows(c):
            return P if c < LAST else LAST_ROWS

        def in_steps(eng, step, lead, lag):
            pairs = (TILES - lead - lag) // 2
            for i in range(-lead, lag):
                step(i, i % 2)
            with eng.Fori(0, pairs) as j:
                for n in (0, 1):
                    step(j * 2 + (lag + n), (lag + n) % 2)
            for i in range(lag + 2 * pairs, TILES + lag):
                step(i, i % 2)

        def exists(i, ahead):
            return not isinstance(i, int) or 0 <= i + ahead < TILES

        with nc.Block() as block:
            @block.sync
            def _(sp):
                start_loop_sems(sp)

        xs_ready = loop_sem("xs_ready")
        conv_projected = loop_sem("conv_projected")
        gate_projected = loop_sem("gate_projected")
        conv_first = loop_sem("conv_first")
        conv_step = loop_sem("conv_step")
        conv_tanhed = loop_sem("conv_tanhed")
        conv_acted = loop_sem("conv_acted")
        decay_summed = loop_sem("decay_summed")
        decay_ready = loop_sem("decay_ready")
        g_ready = loop_sem("g_ready")
        x_turned = loop_sem("x_turned")
        g_split = loop_sem("g_split")
        y_started = loop_sem("y_started")
        g_diaged = loop_sem("g_diaged")
        own_ready = loop_sem("own_ready")
        xdt_ready = loop_sem("xdt_ready")
        xdec_ready = loop_sem("xdec_ready")
        flowed = loop_sem("flowed")
        flow_scaled = loop_sem("flow_scaled")
        y_added = loop_sem("y_added")
        gate_tanhed = loop_sem("gate_tanhed")
        gate_acted = loop_sem("gate_acted")
        y_gated_ready = loop_sem("y_gated_ready")
        y_summed = loop_sem("y_summed")
        y_var_ready = loop_sem("y_var_ready")
        y_pow_ready = loop_sem("y_pow_ready")
        y_rstd_ready = loop_sem("y_rstd_ready")
        y_turned = loop_sem("y_turned")
        yt_ready = loop_sem("yt_ready")
        mixed = loop_sem("mixed")
        x3_ready = loop_sem("x3_ready")
        ln3_stats = loop_sem("ln3_stats")
        ln3_moments = loop_sem("ln3_moments")
        ln3_var = loop_sem("ln3_var")
        ln3_rstd = loop_sem("ln3_rstd")
        ln3_normed = loop_sem("ln3_normed")
        ln3_turned = loop_sem("ln3_turned")
        xr_ready = loop_sem("xr_ready")
        xr_kept = sem("xr_kept")
        routed = loop_sem("routed")
        logit_kept = loop_sem("logit_kept")
        router_step = sem("router_step")
        r_shifted = sem("r_shifted")
        r_exped = sem("r_exped")
        one_set = sem("one_set")
        staged_in = [sem(f"staged_in{n}") for n in range(STAGES)]
        staged_out = sem("staged_out")
        w_main_ready = sem("w_main_ready")
        xe_main_ready = loop_sem("xe_main_ready")
        xe_ready = loop_sem("xe_ready")
        comb_main_ready = loop_sem("comb_main_ready")
        comb_ready = loop_sem("comb_ready")
        comb_transposed = loop_sem("comb_transposed")
        comb_turned_ready = loop_sem("comb_turned_ready")
        projected = loop_sem("projected")
        comb_spread = loop_sem("comb_spread")
        gate_silued = loop_sem("gate_silued")
        up_gated = loop_sem("up_gated")
        weighted = loop_sem("weighted")
        h_main_ready = loop_sem("h_main_ready")
        h_ready = loop_sem("h_ready")
        downed = loop_sem("downed")
        added = loop_sem("added")
        stored = sem("stored")

        x_v = x.rearrange("(t p) d -> p t d", p=P)

        with nc.Block() as block:
            @block.sync
            def _(sp):
                sp.wait_ge(mask_cleared, 1)
                sp.dma_start(mask_u8[:, 0:LAST, :],
                             mask_t[0:LAST * P, :].rearrange("(c p) b -> p c b", p=P)).then_inc(mask_loaded, 16)
                sp.dma_start(mask_u8[0:LAST_ROWS, LAST, :], mask_t[LAST * P:CTX, :]).then_inc(mask_loaded, 16)
                sp.wait_ge(first_ready, 1)
                sp.wait_ge(ones_col, 1)

                def load_turned(t, p, first):
                    def load(c):
                        n = rows(c)
                        sp.dma_start(ctx_t_sb[p][c][:, :, :, 0:n],
                                     ctx_t[t].rearrange("b (k p) m -> p b k m", p=P)[:, :, :, c * P:c * P + n]
                                     ).then_inc(ctx_t_loaded[p], 16)

                    active_chunks(sp, first, load)

                def load_natural(t, p, first):
                    def load(c):
                        n = rows(c)
                        sp.dma_start(ctx_sb[p][c][0:n, :, 0:D],
                                     ctx[t, :, c * P:c * P + n, :].rearrange("b m d -> m b d")
                                     ).then_inc(ctx_loaded[p], 16)

                    active_chunks(sp, first, load)

                first0, first1 = first_of(sp, 0), first_of(sp, 1)
                load_turned(0, 0, first0)
                load_natural(0, 0, first0)
                sp.dma_start(x_all[:, FIRST:TILES, :], x_v[:, FIRST:TILES, :]).then_inc(x_loaded, 16)
                load_turned(1, 1, first1)
                load_natural(1, 1, first1)
                sp.dma_start(w_in_sb[:], w_in.rearrange("(k p) n -> p k n", p=P)).then_inc(weights_loaded, 16)
                sp.dma_start(dt_bias_sb[:], dt_bias).then_inc(weights_loaded, 16)
                sp.dma_start(level_sum[:], c_sum).then_inc(weights_loaded, 16)
                sp.dma_start(level_mask[:], c_mask).then_inc(weights_loaded, 16)
                sp.dma_start(expert_no[:], c_expert).then_inc(weights_loaded, 16)
                sp.dma_start(w_out_sb[:], w_out.rearrange("(k p) n -> p k n", p=P)).then_inc(weights_loaded, 16)
                sp.dma_start(w_router_sb[:], w_router.rearrange("(k p) n -> p k n", p=P)).then_inc(weights_loaded, 16)
                sp.dma_start(conv_w_sb[:], conv_w.rearrange("(k p) n -> p k n", p=P)).then_inc(weights_loaded, 16)
                sp.dma_start(conv_b_sb[:], conv_b).then_inc(weights_loaded, 16)
                sp.dma_start(neg_a[:], a_log).then_inc(weights_loaded, 16)
                sp.dma_start(half_d[:], skip_d).then_inc(weights_loaded, 16)
                sp.dma_start(norm_sb[:], norm_w).then_inc(weights_loaded, 16)
                first = first_of(sp, 2)
                sp.wait_ge(scored, after(1))
                load_turned(2, 0, first)

                def load_next(t, p):
                    first, first_next = first_of(sp, t), first_of(sp, t + 1)
                    sp.wait_ge(gathered, after(t - 1))
                    waited(sp)
                    load_natural(t, p, first)
                    sp.wait_ge(scored, after(t))
                    waited(sp)
                    load_turned(t + 1, 1 - p, first_next)

                with sp.Fori(0, (TILES - 4) // 2) as j:
                    for n in (2, 3):
                        load_next(j * 2 + n, n % 2)
                load_next(TILES - 2, 0)
                first = first_of(sp, TILES - 1)
                sp.wait_ge(gathered, after(TILES - 2))
                load_natural(TILES - 1, 1, first)

            @block.gpsimd
            def _(pool):
                pool.memset(mask_u8[:, LAST, :], 0).then_inc(mask_cleared, 1)
                pool.memset(ones[:], 1.0).then_inc(ones_set, 1)
                pool.memset(minus_half[:], -0.5).then_inc(half_set, 1)
                for p in range(2):
                    for c in range(CHUNKS):
                        last = pool.memset(ctx_sb[p][c][:, :, D:D + 1], 1.0)
                last.then_inc(ones_col, 1)
                start_loop_sems(pool)
                pool.wait_ge(half_set, 1)
                for n, part in enumerate(ln1_parts):
                    pool.wait_ge(ln1_step, 3 * (n + 1))
                    pool.tensor_tensor(rstd1[:, part], var1[:, part], minus_half[:, part], ALU.pow
                                       ).then_inc(ln1_rstd, 1)
                with pool.Fori(0, TILES) as t:
                    pool.wait_ge(ln2_var, after(t + 1))
                    pool.tensor_tensor(rstd[:], var_eps[:], minus_half[:, 0:1], ALU.pow).then_inc(ln2_rstd, 1)
                    pool.wait_ge(ln2_ready, after(t + 1))
                    pool.tensor_copy(xt_all[:, t, :], xt[:].rearrange("p k m -> p (k m)")).then_inc(xt_kept, 1)

            @block.vector
            def _(dve):
                dve.wait_ge(mask_loaded, 32)
                dve.tensor_copy(mask_f[:], mask_u8[:].rearrange("p c b -> p (c b)")).then_inc(mask_step, 1)
                dve.wait_ge(mask_step, 1)
                dve.tensor_scalar(mask_bias[:].rearrange("p c b -> p (c b)"), mask_f[:], MASKED, MASKED,
                                  ALU.mult, ALU.subtract).then_inc(mask_step, 1)
                dve.wait_ge(counted, 1)
                dve.tensor_reduce(count[:], ps_count.rearrange("p (n b) -> p n b", b=TB), AX.X, ALU.add
                                  ).then_inc(mask_step, 1)
                dve.wait_ge(mask_step, 3)
                dve.tensor_scalar(any_active[:], count[:], 1.0, None, ALU.min).then_inc(mask_step, 1)
                dve.wait_ge(mask_step, 4)
                dve.wait_ge(const_loaded, 32)
                dve.tensor_tensor(any_active[:], any_active[:], before_last[:].rearrange("p c t -> p (c t)"), ALU.mult
                                  ).then_inc(mask_step, 1)
                dve.wait_ge(mask_step, 5)
                dve.tensor_reduce(first_f[:], any_active[:].rearrange("p (c t) -> p t c", t=TILES), AX.X, ALU.min
                                  ).then_inc(mask_step, 1)
                dve.wait_ge(mask_step, 6)
                dve.tensor_scalar(n_active[:], first_f[:], -1.0, 1.0, ALU.mult, ALU.add)
                dve.tensor_scalar(first_chunk[:], first_f[:], float(LAST), None, ALU.add).then_inc(first_ready, 1)
                def ln1(n):
                    part = ln1_parts[n]
                    dve.wait_ge(x_loaded, 16 * (n + 1))
                    for t in range(part.start, part.stop):
                        last = dve.bn_stats(stats1[:, t, :], x_all[:, t, :])
                    last.then_inc(ln1_step, 1)
                    dve.wait_ge(ln1_step, 3 * n + 1)
                    for t in range(part.start, part.stop):
                        last = dve.bn_aggr(moments1[:, t, :], stats1[:, t, :])
                    last.then_inc(ln1_step, 1)
                    dve.wait_ge(ln1_step, 3 * n + 2)
                    dve.tensor_scalar(var1[:, part], moments1[:, part, 1], EPS, None, ALU.add).then_inc(ln1_step, 1)

                n_max = dve.alloc_register("dve_chunks_maxed")
                dve.reg_mov(n_max, 0)

                def norm_queries(t):
                    if not (isinstance(t, int) and t == 0):
                        dve.wait_ge(q_turned, after(t))
                    dve.tensor_scalar(qn[:], x_all[:, t, :], moments1[:, t, 0:1], rstd1[:, bass.ds(t, 1)],
                                      ALU.subtract, ALU.mult).then_inc(q_normed, 1)

                def step(i, p):
                    first = first_of(dve, i) if exists(i, 0) else None
                    if isinstance(i, int) and i + 1 in (0, FIRST):
                        dve.wait_ge(ln1_rstd, 1 if i + 1 == 0 else 2)
                    if exists(i, 1):
                        norm_queries(i + 1)
                    if isinstance(i, int) and i == 1:
                        dve.wait_ge(weights_loaded, 12 * 16)
                    if exists(i, 0):
                        def take_max(c):
                            n = rows(c)
                            v = dve.snap(n_max, min_val=0, max_val=TILES * CHUNKS)
                            dve.tensor_tensor(
                                masked[p][0:n, c, :].rearrange("p (b s) -> p b s", b=TB),
                                ps_s[c][0:n, :].rearrange("p (b s) -> p b s", b=TB),
                                mask_bias[0:n, c, bass.ds(i * TB, TB)].unsqueeze(2).broadcast_to([n, TB, SEQ]),
                                ALU.add).then_inc(chunk_masked, 1)
                            dve.wait_ge(chunk_masked, after(v + 1))
                            dve.wait_ge(chunk_maxed, after(v))
                            dve.tensor_tensor(col_max[0:n, :], col_max[0:n, :], masked[p][0:n, c, :], ALU.max
                                              ).then_inc(chunk_maxed, 1)
                            dve.reg_add(n_max, n_max, 1)

                        if exists(i, -1):
                            dve.wait_ge(max_turned, after(i))
                        dve.memset(col_max[:], -MASKED).then_inc(max_cleared, 1)
                        dve.wait_ge(max_cleared, after(i + 1))
                        dve.wait_ge(scored, after(i + 1))
                        waited(dve)
                        active_chunks(dve, first, take_max)
                        dve.memset(scrap[:, 0:1], 0.0).then_inc(maxed, 1)
                    if exists(i, 0):
                        dve.wait_ge(max_turned, after(i + 1))
                        dve.tensor_reduce(q_max[:], ps_max, AX.X, ALU.max).then_inc(q_maxed, 1)
                        dve.wait_ge(q_maxed, after(i + 1))
                        dve.tensor_scalar(max_diag[:], ident[:], q_max[:, 0:1], None, ALU.mult).then_inc(diag_ready, 1)
                        dve.tensor_scalar(valid[p][:], q_max[:], -0.5 * MASKED, None, ALU.is_gt)
                    if exists(i, -2):
                        dve.wait_ge(dt_projected, after(i - 1))
                        dve.tensor_tensor(dt_all[:, i - 2, :], ps_dt, dt_bias_sb[:], ALU.add).then_inc(dt_biased, 1)
                    if exists(i, -1):
                        t = i - 1
                        dve.wait_ge(gathered, after(t + 1))
                        dve.reciprocal(denom[:], ps_o[:, D:D + 1]).then_inc(denom_ready, 1)
                        dve.wait_ge(denom_ready, after(t + 1))
                        dve.tensor_tensor(weight[:], denom[:], valid[1 - p][:], ALU.mult).then_inc(weight_ready, 1)
                    if exists(i, 0):
                        def shift(c):
                            n = rows(c)
                            dve.tensor_tensor(masked[p][0:n, c, :], masked[p][0:n, c, :], max_rows[0:n, :],
                                              ALU.subtract)

                        dve.wait_ge(rows_copied, after(i + 1))
                        waited(dve)
                        active_chunks(dve, first, shift)
                        dve.memset(scrap[:, 0:1], 0.0).then_inc(shifted, 1)
                    if isinstance(i, int) and i == 0:
                        ln1(1)
                    if exists(i, -1):
                        t = i - 1
                        dve.wait_ge(weight_ready, after(t + 1))
                        dve.scalar_tensor_tensor(out=x_all[:, t, :], in0=ps_o[:, 0:D], scalar=weight[:, 0:1],
                                                 in1=x_all[:, t, :], op0=ALU.mult, op1=ALU.add).then_inc(x2_ready, 1)
                        dve.wait_ge(x2_ready, after(t + 1))
                        waited(dve)
                        dve.bn_stats(stats[:], x_all[:, t, :]).then_inc(ln2_stats, 1)
                        dve.wait_ge(ln2_stats, after(t + 1))
                        waited(dve)
                        dve.bn_aggr(moments[:], stats[:]).then_inc(ln2_moments, 1)
                        dve.wait_ge(ln2_moments, after(t + 1))
                        dve.tensor_scalar(var_eps[:], moments[:, 1:2], EPS, None, ALU.add).then_inc(ln2_var, 1)
                        dve.wait_ge(ln2_rstd, after(t + 1))
                        if exists(i, -2):
                            dve.wait_ge(ln2_turned, after(t))
                        dve.tensor_scalar(xn[:], x_all[:, t, :], moments[:, 0:1], rstd[:, 0:1],
                                          ALU.subtract, ALU.mult).then_inc(ln2_normed, 1)

                ln1(0)
                in_steps(dve, step, lead=1, lag=2)

            @block.scalar
            def _(act):
                act.dma_start(before_last[:], c_before).then_inc(const_loaded, 16)
                act.dma_start(x_all[:, 0:FIRST, :], x_v[:, 0:FIRST, :]).then_inc(x_loaded, 16)
                act.dma_start(ident[:], c_ident).then_inc(const_loaded, 16)
                act.wait_ge(ones_set, 1)
                act.activation(scrap[:, 1:2], ones[:, 0:1], ACT.Exp)
                act.wait_ge(first_ready, 1)

                def step(i, p):
                    if exists(i, 1):
                        act.wait_ge(q_turned, after(i + 2))
                        act.copy(qt[:], ps_qt).then_inc(q_ready, 1)
                    if exists(i, 0):
                        act.wait_ge(rows_ready, after(i + 1))
                        act.copy(max_rows[:], ps_rows).then_inc(rows_copied, 1)

                        def exponent(c):
                            n = rows(c)
                            act.activation(masked[p][0:n, c, :], masked[p][0:n, c, :], ACT.Exp, scale=D ** -0.5)

                        first = first_of(act, i)
                        act.wait_ge(shifted, after(i + 1))
                        waited(act)
                        active_chunks(act, first, exponent)
                        act.activation(scrap[:, 1:2], ones[:, 0:1], ACT.Exp).then_inc(exped, 1)
                    if exists(i, -1):
                        act.wait_ge(ln2_turned, after(i))
                        if exists(i, -2):
                            act.wait_ge(xt_kept, after(i - 1))
                        act.copy(xt[:], ps_xt).then_inc(ln2_ready, 1)

                in_steps(act, step, lead=1, lag=2)

            @block.tensor
            def _(pe):
                pe.wait_ge(mask_step, 1)
                pe.wait_ge(ones_set, 1)
                pe.matmul(ps_count, ones[:, 0:1], mask_f[:], start=True, stop=True).then_inc(counted, 1)
                pe.wait_ge(const_loaded, 32)
                n_ld = [pe.alloc_register(f"pe_chunks_loaded{p}") for p in range(2)]
                for r in n_ld:
                    pe.reg_mov(r, 0)
                pe.wait_ge(first_ready, 1)

                def turn_queries(t):
                    pe.wait_ge(q_normed, after(t + 1))
                    for k in range(KD):
                        last = pe.transpose(ps_qt[:, k, :], qn[:, k * P:(k + 1) * P], ident[:])
                    last.then_inc(q_turned, 1)

                def scores(t, p):
                    def score(c):
                        n = rows(c)
                        for b in range(TB):
                            for k in range(KD):
                                pe.matmul(ps_s[c][0:n, b * SEQ:(b + 1) * SEQ], ctx_t_sb[p][c][:, b, k, 0:n],
                                          qt[:, k, b * SEQ:(b + 1) * SEQ], start=(k == 0), stop=(k == KD - 1))

                    first = first_of(pe, t)
                    pe.reg_add(n_ld[p], n_ld[p],
                               pe.value_load(n_active[0:1, bass.ds(t, 1)], min_val=1, max_val=CHUNKS))
                    pe.wait_ge(ctx_t_loaded[p], pe.snap(n_ld[p], min_val=1, max_val=TILES * CHUNKS) * 16)
                    pe.wait_ge(q_ready, after(t + 1))
                    active_chunks(pe, first, score)
                    pe.matmul(ps_fence_s, ones[:], ones[:, 0:2], start=True, stop=True).then_inc(scored, 1)

                def step(i, p):
                    t = i - 1
                    if isinstance(i, int) and i == 1:
                        pe.wait_ge(weights_loaded, 12 * 16)
                    if exists(i, 1):
                        turn_queries(i + 1)
                    if exists(i, 0):
                        pe.wait_ge(maxed, after(i + 1))
                        pe.transpose(ps_max, col_max[:], ident[:]).then_inc(max_turned, 1)
                    if exists(i, -2):
                        pe.wait_ge(ln2_ready, after(i - 1))
                        for k in range(KD):
                            last = pe.matmul(ps_dt, xt[:, k, :], w_in_sb[:, k, PROJ - HEADS:PROJ],
                                             start=(k == 0), stop=(k == KD - 1))
                        last.then_inc(dt_projected, 1)
                    if exists(i, 0):
                        pe.wait_ge(diag_ready, after(i + 1))
                        pe.matmul(ps_rows, ones[:], max_diag[:], start=True, stop=True).then_inc(rows_ready, 1)
                    if exists(i, 1):
                        scores(i + 1, 1 - p)
                    if exists(i, 0):
                        def gather(c):
                            n = rows(c)
                            for b in range(TB):
                                pe.matmul(ps_o[b * SEQ:(b + 1) * SEQ, 0:D + 1],
                                          masked[p][0:n, c, b * SEQ:(b + 1) * SEQ],
                                          ctx_sb[p][c][0:n, b, :], start=(c == LAST), stop=(c == LAST),
                                          skip_group_check=True)

                        first = first_of(pe, i)
                        pe.wait_ge(ctx_loaded[p], pe.snap(n_ld[p], min_val=1, max_val=TILES * CHUNKS) * 16)
                        pe.wait_ge(exped, after(i + 1))
                        if exists(i, -1):
                            pe.wait_ge(x2_ready, after(i))
                        waited(pe)
                        active_chunks(pe, first, gather)
                        pe.matmul(ps_fence_o, ones[:], ones[:, 0:2], start=True, stop=True).then_inc(gathered, 1)
                    if exists(i, -1):
                        pe.wait_ge(ln2_normed, after(t + 1))
                        if exists(i, -2):
                            pe.wait_ge(dt_biased, after(t))
                        for k in range(KD):
                            last = pe.transpose(ps_xt[:, k, :], xn[:, k * P:(k + 1) * P], ident[:])
                        last.then_inc(ln2_turned, 1)

                in_steps(pe, step, lead=1, lag=2)

        phase.close()
        phase = before_experts.enter_context(ExitStack())
        def far(name, shape, dt=F32):
            return stack.enter_context(nc.sbuf_tensor(name, shape, dt, side="right"))

        staged = [far(f"staged{n}", [P, D]) for n in range(STAGES)]
        one = far("one", [P, 1])
        select = far("select", [2 * EXPERTS, FB // 2, P], F32R)
        w_main = [far(f"w_main{b}", [P, 3, D], F32R) for b in range(EARLY)]
        w_rest = [far(f"w_rest{b}", [P, 3, D], F32R) for b in range(EARLY)]

        step_abs = tmp("step_abs", [P, TILES * HEADS])
        step_exp = tmp("step_exp", [P, TILES * HEADS])
        step_log = tmp("step_log", [P, TILES * HEADS])
        z_abs = sem("z_abs")
        z_exp = sem("z_exp")
        z_log = sem("z_log")
        a_exp = sem("a_exp")
        step_done = sem("step_done")
        dt_flat = dt_all[:].rearrange("p t h -> p (t h)")

        conv = [tmp(f"conv{p}", [P, CB, P]) for p in range(2)]
        conv_tanh = tmp("conv_tanh", [P, CB, P])
        act2 = tmp("act2", [P, CB, P])
        decay = [tmp(f"decay{p}", [P, NL, HEADS]) for p in range(2)]
        g_masked = tmp("g_masked", [P, NL, P])
        g_scrap = tmp("g_scrap", [P, P])
        g_diag = tmp("g_diag", [P, 1])
        own = tmp("own", [P, HEADS])
        xdt = tmp("xdt", [P, INTER])
        xdec = tmp("xdec", [P, NL - 1, INTER])
        flow = tmp("flow", [P, 2, INTER])
        y = tmp("y", [P, INTER])
        gate_tanh = tmp("gate_tanh", [P, INTER])
        gate2 = [tmp(f"gate2_{p}", [P, INTER]) for p in range(2)]
        y_gated = tmp("y_gated", [P, INTER])
        y_square = tmp("y_square", [P, INTER])
        y_sum = tmp("y_sum", [P, 1])
        y_var = tmp("y_var", [P, 1])
        y_pow = tmp("y_pow", [P, 1])
        y_rstd = tmp("y_rstd", [P, 1])
        yt = tmp("yt", [P, IB, P])
        xs = tmp("xs", [P, KD, P])
        xr = tmp("xr", [P, KD, P])
        r_max = tmp("r_max", [P, TILES])
        r_exp = tmp("r_exp", [P, TILES, EXPERTS])
        r_sum = tmp("r_sum", [P, TILES])
        r_inv = tmp("r_inv", [P, TILES])
        r_prob = tmp("r_prob", [P, TILES, EXPERTS])
        top = tmp("top", [P, TILES, TOP])
        top_no = tmp("top_no", [P, TILES, TOP], U32)
        top_f = tmp("top_f", [P, TILES, TOP])
        top_sum = tmp("top_sum", [P, TILES])
        top_inv = tmp("top_inv", [P, TILES])
        renorm = tmp("renorm", [P, TILES, TOP])
        kept = tmp("kept", [P, TILES, TOP])
        kept_sum = tmp("kept_sum", [P, TILES])
        kept_inv = tmp("kept_inv", [P, TILES])
        kept_w = tmp("kept_w", [P, TILES, TOP])
        is_expert = tmp("is_expert", [P, RT, EXPERTS, TOP])
        w_expert = tmp("w_expert", [P, RT, EXPERTS, TOP])

        ps_conv = [bank[0][:, 0:4 * P].rearrange("p (m t) -> p m t", t=P),
                   bank[1][:, 0:2 * P].rearrange("p (m t) -> p m t", t=P)]
        ps_g = bank[4][:, 3 * P:4 * P]
        ps_gate = bank[2]
        ps_x = bank[3]
        ps_decay = bank[4][:, 0:NL * HEADS].rearrange("p (j h) -> p j h", h=HEADS)
        ps_flow = [bank[5], bank[6]]
        ps_yt = bank[3][:, :].rearrange("p (m t) -> p m t", t=P)
        ps_mix = bank[7][:, 0:D]
        ps_logit = bank[7][:, 0:EXPERTS]
        ps_x3 = bank[7][:, D:2 * D].rearrange("p (k m) -> p k m", k=KD)

        def ps_conv_block(m):
            return ps_conv[m // 4][:, m % 4, :]

        def by_head(a):
            return a.rearrange("p (h e) -> p h e", e=HD)

        def spread(a):
            return a.unsqueeze(2).broadcast_to([P, HEADS, HD])

        n_select = FB // 2 * P // D
        staging = ([("w", m) for m in range(3)] + [("select", m) for m in range(n_select)]
                   + [("w", m) for m in range(3, FB * 3)])
        n_early = EARLY * 3 + n_select

        def stage(sp, part):
            for n in part:
                what, m = staging[n]
                if n >= STAGES:
                    sp.wait_ge(staged_out, n - STAGES + 1)
                if what == "w":
                    sp.dma_start(staged[n % STAGES][:], w_experts[m]).then_inc(staged_in[n % STAGES], 16)
                else:
                    sp.dma_start(staged[n % STAGES][0:2 * EXPERTS, :], c_select[:, m * D:(m + 1) * D]
                                 ).then_inc(staged_in[n % STAGES], 16)

        def split_staged(pool, part):
            for n in part:
                what, m = staging[n]
                whole = staged[n % STAGES]
                pool.wait_ge(staged_in[n % STAGES], 16 * (n // STAGES + 1))
                if what == "w":
                    main, rest = w_main[m // 3][:, m % 3, :], w_rest[m // 3][:, m % 3, :]
                    pool.tensor_tensor(main, whole[:], one[:].broadcast_to([P, D]), ALU.mult).then_inc(w_main_ready, 1)
                    pool.wait_ge(w_main_ready, m + 1)
                    pool.tensor_tensor(rest, whole[:], main.bitcast(F32), ALU.subtract).then_inc(staged_out, 1)
                else:
                    pool.tensor_tensor(select[:].rearrange("p b f -> p (b f)")[:, m * D:(m + 1) * D],
                                       whole[0:2 * EXPERTS, :], one[0:2 * EXPERTS, :].broadcast_to([2 * EXPERTS, D]),
                                       ALU.mult).then_inc(staged_out, 1)

        with nc.Block() as block:
            @block.sync
            def _(sp):
                stage(sp, range(n_early))

            @block.scalar
            def _(act):
                def step_logs():
                    act.activation(neg_a[:], neg_a[:], ACT.Exp).then_inc(a_exp, 1)
                    act.activation(step_abs[:], dt_flat, ACT.Abs).then_inc(z_abs, 1)
                    act.wait_ge(z_abs, 1)
                    act.activation(step_exp[:], step_abs[:], ACT.Exp, scale=-1.0).then_inc(z_exp, 1)
                    act.wait_ge(z_exp, 1)
                    act.activation(step_log[:], step_exp[:], ACT.Ln, bias=1.0).then_inc(z_log, 1)
                    act.activation(y_sum[:], ones[:, 0:1], ACT.Exp)

                def exp_logits(n):
                    lo, hi = ROUTER_PARTS[n]
                    act.wait_ge(r_shifted, n + 1)
                    act.activation(r_exp[:, lo:hi, :], r_exp[:, lo:hi, :], ACT.Exp).then_inc(r_exped, 1)

                def step(i, p):
                    e, f, c, u = i - 3, i - 2, i, i + 1
                    if exists(i, -3):
                        act.wait_ge(ln3_turned, after(e + 1))
                        act.copy(xr[:], ps_x3).then_inc(xr_ready, 1)
                    if exists(i, -2):
                        act.wait_ge(y_gated_ready, after(f + 1))
                        act.activation(y_square[:], y_gated[:], ACT.Square, accum_out=y_sum[:]).then_inc(y_summed, 1)
                    if exists(i, 0):
                        act.wait_ge(gate_projected, after(c + 1))
                        act.activation(gate_tanh[:], ps_gate[:], ACT.Tanh, scale=0.5).then_inc(gate_tanhed, 1)
                    if exists(i, 1):
                        if exists(i, 0):
                            act.wait_ge(gate_projected, after(u))
                        waited(act)
                        act.copy(xs[:].rearrange("p k m -> p (k m)"), xt_all[:, u, :]).then_inc(xs_ready, 1)
                        if isinstance(i, int) and i == -1:
                            step_logs()
                    if exists(i, 0):
                        act.wait_ge(decay_summed, after(c + 1))
                        if exists(i, -2):
                            act.wait_ge(flow_scaled, after((i - 1) * NL))
                        act.activation(decay[p][:], ps_decay, ACT.Exp).then_inc(decay_ready, 1)
                    if exists(i, -3):
                        act.wait_ge(routed, after(e + 1))
                        waited(act)
                        act.copy(logits[:, e, :], ps_logit).then_inc(logit_kept, 1)
                        waited(act)
                        act.copy(xt_all[:, e, :], xr[:].rearrange("p k m -> p (k m)")).then_inc(xr_kept, 1)
                    if exists(i, -2):
                        act.wait_ge(y_turned, after(f + 1))
                        act.copy(yt[:], ps_yt).then_inc(yt_ready, 1)
                    if isinstance(i, int) and i == TILES:
                        exp_logits(0)
                    if exists(i, 0):
                        act.wait_ge(conv_step, after((c + 1) * len(CONV_STEPS)))
                        act.activation(conv_tanh[:], conv[p][:], ACT.Tanh, scale=0.5).then_inc(conv_tanhed, 1)
                    if exists(i, 1):
                        act.wait_ge(conv_projected, after(u + 1))
                        for m in CONV_ORDER:
                            act.activation(conv[1 - p][:, m, :], ps_conv_block(m), ACT.Identity,
                                           bias=conv_b_sb[:, m:m + 1],
                                           scale=conv_w_sb[:, m, TAPS - 1:TAPS]).then_inc(conv_first, 1)

                in_steps(act, step, lead=1, lag=3)
                exp_logits(1)

            @block.gpsimd
            def _(pool):
                def step(i, p):
                    f, s = i - 2, i - 1

                    def decay_half(n):
                        if n == 1:
                            pool.wait_ge(decay_ready, after(s + 1))
                            pool.wait_ge(xdt_ready, after(s + 1))
                            if exists(i, -2):
                                pool.wait_ge(flowed, after(s * NL))
                        j = NL - 1 - n
                        pool.tensor_tensor(by_head(xdec[:, j, :]), by_head(xdt[:]), spread(decay[1 - p][:, j, :]),
                                           ALU.mult).then_inc(xdec_ready, 1)

                    def add(n):
                        pool.wait_ge(flow_scaled, after(s * NL + n + 1))
                        if n == 0:
                            pool.wait_ge(y_started, after(s + 1))
                        else:
                            pool.wait_ge(y_added, after(s * NL + n))
                        pool.tensor_tensor(y[:], y[:], flow[:, n % 2, :], ALU.add).then_inc(y_added, 1)

                    if exists(i, -2):
                        pool.wait_ge(y_added, after((f + 1) * NL))
                        pool.wait_ge(gate_acted, after(f + 1))
                        if exists(i, -3):
                            pool.wait_ge(y_turned, after(f))
                            pool.wait_ge(y_summed, after(f))
                        pool.tensor_tensor(y_gated[:], y[:], gate2[p][:], ALU.mult).then_inc(y_gated_ready, 1)
                    if exists(i, -1):
                        decay_half(1)
                        decay_half(2)
                        decay_half(3)
                        add(0)
                    if exists(i, -2):
                        pool.wait_ge(y_var_ready, after(f + 1))
                        pool.tensor_tensor(y_pow[:], y_var[:], minus_half[:, 0:1], ALU.pow).then_inc(y_pow_ready, 1)
                    if exists(i, -1):
                        add(1)
                        decay_half(4)
                        add(2)
                        decay_half(5)
                        add(3)
                        add(4)
                    if exists(i, -2):
                        pool.wait_ge(ln3_var, after(f + 1))
                        pool.tensor_tensor(rstd[:], var_eps[:], minus_half[:, 0:1], ALU.pow).then_inc(ln3_rstd, 1)
                    if exists(i, -1):
                        add(5)

                pool.memset(one[:], 1.0).then_inc(one_set, 1)
                in_steps(pool, step, lead=1, lag=3)
                pool.wait_ge(one_set, 1)
                split_staged(pool, range(n_early))

            @block.vector
            def _(dve):
                dve.wait_ge(z_log, 1)
                dve.scalar_tensor_tensor(out=dt_flat, in0=dt_flat, scalar=0.0, in1=step_log[:],
                                         op0=ALU.max, op1=ALU.add).then_inc(step_done, 1)
                dve.wait_ge(step_done, 1)
                dve.tensor_scalar(dt_flat, dt_flat, 0.0, 100.0, ALU.max, ALU.min).then_inc(step_done, 1)
                dve.wait_ge(a_exp, 1)
                dve.tensor_scalar(neg_a[:], neg_a[:], -1.0, None, ALU.mult).then_inc(step_done, 1)
                dve.wait_ge(step_done, 3)
                dve.tensor_tensor(adt_all[:], dt_all[:], neg_a[:].unsqueeze(1).broadcast_to([P, TILES, HEADS]),
                                  ALU.mult).then_inc(step_done, 1)
                dve.wait_ge(step_done, 4)
                dve.tensor_scalar(dt_flat, dt_flat, 0.5, None, ALU.mult).then_inc(step_done, 1)
                dve.tensor_scalar(half_d[:], half_d[:], 0.5, None, ALU.mult).then_inc(step_done, 1)
                for m in range(IB):
                    dve.tensor_scalar(w_out_sb[:, m, :], w_out_sb[:, m, :], norm_sb[:, m:m + 1], None, ALU.mult
                                      ).then_inc(step_done, 1)
                dve.wait_ge(step_done, 6 + IB)

                def step(i, p):
                    f, s, c = i - 2, i - 1, i

                    def taps(part):
                        if not exists(i, 0):
                            return
                        for n in part:
                            k, m = CONV_STEPS[n]
                            if k == 1:
                                dve.wait_ge(conv_first, after(c * CB + (2 if m in CONV_ORDER[:2] else CB)))
                            else:
                                dve.wait_ge(conv_step, after(c * len(CONV_STEPS) + CONV_STEPS.index((k - 1, m)) + 1))
                            now = conv[p][:, m, :].rearrange("p (b s) -> p b s", b=TB)[:, :, k:]
                            dve.scalar_tensor_tensor(
                                out=now, in0=ps_conv_block(m).rearrange("p (b s) -> p b s", b=TB)[:, :, 0:SEQ - k],
                                scalar=conv_w_sb[:, m, TAPS - 1 - k:TAPS - k], in1=now,
                                op0=ALU.mult, op1=ALU.add).then_inc(conv_step, 1)

                    def scale_flow(n):
                        if not exists(i, -1):
                            return
                        dve.wait_ge(flowed, after(s * NL + n + 1))
                        if n == 0:
                            dve.wait_ge(decay_ready, after(s + 1))
                        if n >= 2:
                            dve.wait_ge(y_added, after(s * NL + n - 1))
                        dve.tensor_tensor(by_head(flow[:, n % 2, :]), by_head(ps_flow[n % 2][:]),
                                          spread(decay[1 - p][:, NL - 1 - n, :]), ALU.mult).then_inc(flow_scaled, 1)

                    if exists(i, -1):
                        dve.tensor_tensor_reduce(out=g_scrap[:], in0=ps_g, in1=ident[:], scale=0.25, scalar=0.0,
                                                 op0=ALU.mult, op1=ALU.add, accum_out=g_diag[:]).then_inc(g_diaged, 1)
                        dve.wait_ge(g_diaged, after(s + 1))
                        dve.scalar_tensor_tensor(out=own[:], in0=dt_all[:, s, :], scalar=g_diag[:, 0:1], in1=half_d[:],
                                                 op0=ALU.mult, op1=ALU.add).then_inc(own_ready, 1)
                    taps(range(6))
                    if exists(i, -1):
                        dve.wait_ge(own_ready, after(s + 1))
                        if exists(i, -2):
                            dve.wait_ge(y_gated_ready, after(f + 1))
                        dve.tensor_tensor(by_head(y[:]), by_head(ps_x[:]), spread(own[:]), ALU.mult
                                          ).then_inc(y_started, 1)
                    scale_flow(0)
                    if isinstance(i, int) and i == TILES:
                        shift_logits(0)
                    if exists(i, -2):
                        dve.wait_ge(y_summed, after(f + 1))
                        dve.tensor_scalar(y_var[:], y_sum[:], 0.25 / INTER, EPS, ALU.mult, ALU.add
                                          ).then_inc(y_var_ready, 1)
                    scale_flow(1)
                    if isinstance(i, int) and i == TILES:
                        pick_top(0)
                    if exists(i, 0):
                        dve.wait_ge(gate_tanhed, after(c + 1))
                        if exists(i, -2):
                            dve.wait_ge(y_gated_ready, after(f + 1))
                        dve.scalar_tensor_tensor(out=gate2[p][:], in0=gate_tanh[:], scalar=1.0, in1=ps_gate[:],
                                                 op0=ALU.add, op1=ALU.mult).then_inc(gate_acted, 1)
                    taps(range(6, 12))
                    if exists(i, -2):
                        dve.wait_ge(y_pow_ready, after(f + 1))
                        dve.tensor_scalar(y_rstd[:], y_pow[:], 0.5, None, ALU.mult).then_inc(y_rstd_ready, 1)
                    scale_flow(2)
                    taps(range(12, 18))
                    if isinstance(i, int) and i == TILES + 1:
                        spread_weights(2 * RT)
                    if exists(i, -2):
                        dve.wait_ge(y_rstd_ready, after(f + 1))
                        dve.wait_ge(mixed, after(f + 1))
                        dve.scalar_tensor_tensor(out=x_all[:, f, :], in0=ps_mix, scalar=y_rstd[:, 0:1],
                                                 in1=x_all[:, f, :], op0=ALU.mult, op1=ALU.add).then_inc(x3_ready, 1)
                    scale_flow(3)
                    if isinstance(i, int) and i == TILES:
                        weigh_top(0)
                    if exists(i, -2):
                        dve.wait_ge(x3_ready, after(f + 1))
                        waited(dve)
                        dve.bn_stats(stats[:], x_all[:, f, :]).then_inc(ln3_stats, 1)
                    if exists(i, 0):
                        dve.wait_ge(conv_tanhed, after(c + 1))
                        if exists(i, -1):
                            dve.wait_ge(x_turned, after(s + 1))
                            dve.wait_ge(g_ready, after(s + 1))
                        dve.scalar_tensor_tensor(out=act2[:].rearrange("p m t -> p (m t)"),
                                                 in0=conv_tanh[:].rearrange("p m t -> p (m t)"), scalar=1.0,
                                                 in1=conv[p][:].rearrange("p m t -> p (m t)"), op0=ALU.add,
                                                 op1=ALU.mult).then_inc(conv_acted, 1)
                    if exists(i, -2):
                        dve.wait_ge(ln3_stats, after(f + 1))
                        waited(dve)
                        dve.bn_aggr(moments[:], stats[:]).then_inc(ln3_moments, 1)
                    scale_flow(4)
                    if exists(i, -2):
                        dve.wait_ge(ln3_moments, after(f + 1))
                        dve.tensor_scalar(var_eps[:], moments[:, 1:2], EPS, None, ALU.add).then_inc(ln3_var, 1)
                    if isinstance(i, int) and i == TILES:
                        spread_weights(0)
                    scale_flow(5)
                    if isinstance(i, int) and i == TILES:
                        spread_weights(RT)
                    if exists(i, 0):
                        dve.wait_ge(x_turned, after(c + 1))
                        if exists(i, -1):
                            dve.wait_ge(xdec_ready, after(c * (NL - 1)))
                            dve.wait_ge(flowed, after(c * NL))
                        dve.tensor_tensor(by_head(xdt[:]), by_head(ps_x[:]), spread(dt_all[:, c, :]), ALU.mult
                                          ).then_inc(xdt_ready, 1)
                        dve.wait_ge(g_ready, after(c + 1))
                        dve.tensor_tensor(g_masked[:], ps_g.unsqueeze(1).broadcast_to([P, NL, P]), level_mask[:],
                                          ALU.mult).then_inc(g_split, 1)
                    if exists(i, -2):
                        dve.wait_ge(ln3_rstd, after(f + 1))
                        if exists(i, -3):
                            dve.wait_ge(ln3_turned, after(f))
                        dve.tensor_scalar(xn[:], x_all[:, f, :], moments[:, 0:1], rstd[:, 0:1],
                                          ALU.subtract, ALU.mult).then_inc(ln3_normed, 1)

                steps = [0]

                def then(instruction):
                    steps[0] += 1
                    instruction.then_inc(router_step, 1)
                    dve.wait_ge(router_step, steps[0])

                def per_tile(a, lo, hi, n):
                    return a[:, lo:hi].unsqueeze(2).broadcast_to([P, hi - lo, n])

                def shift_logits(part):
                    lo, hi = ROUTER_PARTS[part]
                    dve.wait_ge(logit_kept, after(hi))
                    then(dve.tensor_reduce(r_max[:, lo:hi], logits[:, lo:hi, :], AX.X, ALU.max))
                    dve.tensor_tensor(r_exp[:, lo:hi, :], logits[:, lo:hi, :], per_tile(r_max, lo, hi, EXPERTS),
                                      ALU.subtract).then_inc(r_shifted, 1)

                def pick_top(part):
                    lo, hi = ROUTER_PARTS[part]
                    dve.wait_ge(r_exped, part + 1)
                    then(dve.tensor_reduce(r_sum[:, lo:hi], r_exp[:, lo:hi, :], AX.X, ALU.add))
                    then(dve.reciprocal(r_inv[:, lo:hi], r_sum[:, lo:hi]))
                    then(dve.tensor_tensor(r_prob[:, lo:hi, :], r_exp[:, lo:hi, :], per_tile(r_inv, lo, hi, EXPERTS),
                                           ALU.mult))
                    for t in range(lo, hi):
                        last = dve.max(top[:, t, :], r_prob[:, t, :])
                    then(last)
                    for t in range(lo, hi):
                        last = dve.max_index(top_no[:, t, :], top[:, t, :], r_prob[:, t, :])
                    then(last)
                    then(dve.tensor_copy(top_f[:, lo:hi, :], top_no[:, lo:hi, :]))

                def weigh_top(part):
                    lo, hi = ROUTER_PARTS[part]
                    now = slice(lo, hi)
                    then(dve.tensor_reduce(top_sum[:, now], top[:, now, :], AX.X, ALU.add))
                    then(dve.tensor_scalar(top_sum[:, now], top_sum[:, now], 1e-12, None, ALU.max))
                    then(dve.reciprocal(top_inv[:, now], top_sum[:, now]))
                    then(dve.tensor_tensor(renorm[:, now, :], top[:, now, :], per_tile(top_inv, lo, hi, TOP), ALU.mult))
                    for k in range(1, TOP - 1):
                        then(dve.tensor_tensor(renorm[:, now, k:k + 1], renorm[:, now, k:k + 1],
                                               renorm[:, now, k - 1:k], ALU.add))
                    then(dve.tensor_copy(kept[:, now, 0:1], top[:, now, 0:1]))
                    then(dve.scalar_tensor_tensor(out=kept[:, now, 1:TOP], in0=renorm[:, now, 0:TOP - 1], scalar=KEEP,
                                                  in1=top[:, now, 1:TOP], op0=ALU.is_lt, op1=ALU.mult))
                    then(dve.tensor_reduce(kept_sum[:, now], kept[:, now, :], AX.X, ALU.add))
                    then(dve.tensor_scalar(kept_sum[:, now], kept_sum[:, now], 1e-12, None, ALU.max))
                    then(dve.reciprocal(kept_inv[:, now], kept_sum[:, now]))
                    then(dve.tensor_tensor(kept_w[:, now, :], kept[:, now, :], per_tile(kept_inv, lo, hi, TOP),
                                           ALU.mult))

                def spread_weights(t):
                    now = slice(t, t + RT)
                    for a, b, op, result in ((expert_no[:].unsqueeze(1).broadcast_to([P, RT, EXPERTS, TOP]), top_f,
                                              ALU.is_equal, is_expert),
                                             (is_expert[:], kept_w, ALU.mult, w_expert)):
                        then(dve.tensor_tensor(
                            result[:], a, b[:, now, :].unsqueeze(2).broadcast_to([P, RT, EXPERTS, TOP]), op))
                    then(dve.tensor_reduce(comb_all[:, now, :], w_expert[:], AX.X, ALU.add))

                in_steps(dve, step, lead=1, lag=3)
                shift_logits(1)
                pick_top(1)
                weigh_top(1)
                spread_weights(ROUTER_PARTS[1][0])


            @block.tensor
            def _(pe):
                def step(i, p):
                    e, f, s, c, u = i - 3, i - 2, i - 1, i, i + 1

                    def flow_between(n):
                        if not exists(i, -1):
                            return
                        j = NL - 1 - n
                        if n == 0:
                            pe.wait_ge(xdt_ready, after(s + 1))
                            pe.wait_ge(g_split, after(s + 1))
                        else:
                            pe.wait_ge(xdec_ready, after(s * (NL - 1) + n))
                        if n >= 2 or exists(i, -2):
                            pe.wait_ge(flow_scaled, after(s * NL + n - 1))
                        pe.matmul(ps_flow[n % 2][:], g_masked[:, j, :], xdt[:] if n == 0 else xdec[:, j, :],
                                  start=True, stop=True).then_inc(flowed, 1)

                    flow_between(0)
                    if exists(i, -3):
                        pe.wait_ge(ln3_normed, after(e + 1))
                        for k in range(KD):
                            last = pe.transpose(ps_x3[:, k, :], xn[:, k * P:(k + 1) * P], ident[:])
                        last.then_inc(ln3_turned, 1)
                    if exists(i, -2):
                        pe.wait_ge(y_gated_ready, after(f + 1))
                        if exists(i, -1):
                            pe.wait_ge(y_started, after(s + 1))
                        for m in range(IB):
                            last = pe.transpose(ps_yt[:, m, :], y_gated[:, m * P:(m + 1) * P], ident[:])
                        last.then_inc(y_turned, 1)
                    flow_between(1)
                    if exists(i, 0):
                        if exists(i, -1):
                            pe.wait_ge(g_diaged, after(s + 1))
                        if isinstance(i, int) and i == 0:
                            pe.wait_ge(step_done, 4)
                        for j in range(NL):
                            last = pe.matmul(ps_decay[:, j, :], level_sum[:, j, :], adt_all[:, c, :],
                                             start=True, stop=True)
                        last.then_inc(decay_summed, 1)
                    if exists(i, -3):
                        pe.wait_ge(xr_ready, after(e + 1))
                        for k in range(KD):
                            last = pe.matmul(ps_logit, xr[:, k, :], w_router_sb[:, k, :],
                                             start=(k == 0), stop=(k == KD - 1))
                        last.then_inc(routed, 1)
                    flow_between(2)
                    if exists(i, -2):
                        pe.wait_ge(yt_ready, after(f + 1))
                        if exists(i, -3):
                            pe.wait_ge(logit_kept, after(e + 1))
                        if isinstance(i, int) and i == 2:
                            pe.wait_ge(step_done, 6 + IB)
                        for m in range(IB):
                            last = pe.matmul(ps_mix, yt[:, m, :], w_out_sb[:, m, :], start=(m == 0), stop=(m == IB - 1))
                        last.then_inc(mixed, 1)
                    flow_between(3)
                    flow_between(4)
                    flow_between(5)
                    if exists(i, 0):
                        pe.wait_ge(conv_acted, after(c + 1))
                        if exists(i, -1):
                            pe.wait_ge(y_started, after(s + 1))
                        if exists(i, -2):
                            pe.wait_ge(yt_ready, after(f + 1))
                        for m in range(IB):
                            last = pe.transpose(ps_x[:, m * P:(m + 1) * P], act2[:, m, :], ident[:])
                        last.then_inc(x_turned, 1)
                        pe.wait_ge(decay_ready, after(c + 1))
                        pe.matmul(ps_g, act2[:, IB, :], act2[:, IB + 1, :], start=True, stop=True).then_inc(g_ready, 1)
                    if exists(i, 1):
                        pe.wait_ge(xs_ready, after(u + 1))
                        if exists(i, 0):
                            pe.wait_ge(conv_step, after(u * len(CONV_STEPS)))
                        for m in CONV_ORDER:
                            for k in range(KD):
                                last = pe.matmul(ps_conv_block(m), w_in_sb[:, k, INTER + m * P:INTER + (m + 1) * P],
                                                 xs[:, k, :], start=(k == 0), stop=(k == KD - 1))
                        last.then_inc(conv_projected, 1)
                    if exists(i, 1):
                        if exists(i, 0):
                            pe.wait_ge(gate_acted, after(u))
                        for k in range(KD):
                            last = pe.matmul(ps_gate[:], xs[:, k, :], w_in_sb[:, k, 0:INTER],
                                             start=(k == 0), stop=(k == KD - 1))
                        last.then_inc(gate_projected, 1)
                in_steps(pe, step, lead=1, lag=3)

        phase.close()
        before_experts.close()
        phase = stack.enter_context(ExitStack())

        def by_half(q):
            return xt_all[:, bass.ds(q * TG, TG), :].rearrange("p t (k m) -> p k t m", k=KD)

        w_main += [tmp(f"w_main{b}", [P, 3, D], F32R) for b in range(EARLY, FB)]
        w_rest += [tmp(f"w_rest{b}", [P, 3, D], F32R) for b in range(EARLY, FB)]
        xe_main = tmp("xe_main", [P, KD, GT], F32R)
        xe_rest = tmp("xe_rest", [P, KD, GT], F32R)
        comb_split = tmp("comb_split", [P, TG, 2, 2, EXPERTS // 2], F32R)
        comb_turned = tmp("comb_turned", [2 * EXPERTS, GT], F32R)
        hidden = [tmp(f"hidden{n}", [P, GT]) for n in range(2)]
        h_main = tmp("h_main", [P, GT], F32R)
        h_rest = tmp("h_rest", [P, GT], F32R)
        ps_gate_e = [bank[0], bank[1]]
        ps_up_e = [bank[2], bank[3]]
        ps_comb = [bank[4], bank[5]]
        ps_y = [bank[6][:, 0:D], bank[6][:, D:2 * D], bank[7][:, 0:D], bank[7][:, D:2 * D]]

        with nc.Block() as block:
            @block.sync
            def _(sp):
                stage(sp, range(n_early, len(staging)))
                out_v = out.rearrange("(g t p) d -> g p t d", p=P, t=TG)
                with sp.Fori(0, GROUPS) as q:
                    sp.wait_ge(added, after((q + 1) * 2))
                    sp.dma_start(out_v[q], x_all[:, bass.ds(q * TG, TG), :]).then_inc(stored, 16)
                sp.wait_ge(stored, GROUPS * 16)

            @block.gpsimd
            def _(pool):
                split_staged(pool, range(n_early, len(staging)))

            @block.scalar
            def _(act):
                act.activation(hidden[0][:, 0:1], ident[:, 0:1], ACT.Silu)
                def split_tokens(q):
                    act.copy(xe_main[:].rearrange("p k (t m) -> p k t m", t=TG), by_half(q)).then_inc(xe_main_ready, 1)

                def split_hidden(n, p):
                    act.wait_ge(weighted, after(n + 1))
                    act.wait_ge(downed, after(n))
                    act.copy(h_main[:], hidden[p][:]).then_inc(h_main_ready, 1)

                split_tokens(0)
                with act.Fori(0, GROUPS) as q:
                    for b in range(FB):
                        if b == 0:
                            with act.If(q > 0):
                                act.wait_ge(h_ready, after(q * FB - 1))
                                waited(act)
                        act.wait_ge(projected, after(q * FB + b + 1))
                        if b == FB - 1:
                            waited(act)
                            with act.If(q < GROUPS - 1):
                                split_tokens(nc.s_assert_within(
                                    q + 1, 1, GROUPS - 1, skip_runtime_bounds_check_because="within the If"))
                        if b > 0:
                            act.wait_ge(h_ready, after(q * FB + b - 1))
                        act.activation(hidden[b % 2][:], ps_gate_e[b % 2][:], ACT.Silu).then_inc(gate_silued, 1)
                        if b == 0:
                            act.wait_ge(comb_transposed, after(q + 1))
                            act.wait_ge(comb_spread, after(q * FB))
                            act.copy(comb_turned[:], ps_comb[0][0:2 * EXPERTS, :]).then_inc(comb_turned_ready, 1)
                            with act.If(q > 0):
                                split_hidden(q * FB - 1, 1)
                        else:
                            split_hidden(q * FB + b - 1, (b - 1) % 2)
                split_hidden(GROUPS * FB - 1, 1)

            @block.vector
            def _(dve):
                def split_tokens(q):
                    dve.wait_ge(xe_main_ready, after(q + 1))
                    dve.tensor_tensor(xe_rest[:].rearrange("p k (t m) -> p k t m", t=TG), by_half(q),
                                      xe_main[:].bitcast(F32).rearrange("p k (t m) -> p k t m", t=TG),
                                      ALU.subtract).then_inc(xe_ready, 1)
                    combs = comb_all[:, bass.ds(q * TG, TG), :].rearrange("p t (n e) -> p t n e", n=2)
                    dve.wait_ge(comb_transposed, after(q))
                    dve.tensor_copy(comb_split[:, :, :, 0, :], combs).then_inc(comb_main_ready, 1)
                    dve.wait_ge(comb_main_ready, after(q + 1))
                    dve.tensor_tensor(comb_split[:, :, :, 1, :], combs, comb_split[:, :, :, 0, :].bitcast(F32),
                                      ALU.subtract).then_inc(comb_ready, 1)

                def split_hidden(n, p):
                    dve.wait_ge(h_main_ready, after(n + 1))
                    dve.tensor_tensor(h_rest[:], hidden[p][:], h_main[:].bitcast(F32), ALU.subtract).then_inc(h_ready, 1)

                def add_group(q):
                    dve.wait_ge(downed, after((q + 1) * FB))
                    for n in range(2):
                        result = x_all[:, bass.ds(q * TG + n * 2, 2), :]
                        dve.tensor_tensor(result, bank[6 + n][:].rearrange("p (t d) -> p t d", t=2), result, ALU.add
                                          ).then_inc(added, 1)

                split_tokens(0)
                with dve.Fori(0, GROUPS) as q:
                    for b in range(FB):
                        if b == FB - 1:
                            with dve.If(q < GROUPS - 1):
                                split_tokens(nc.s_assert_within(
                                    q + 1, 1, GROUPS - 1, skip_runtime_bounds_check_because="within the If"))
                        dve.wait_ge(gate_silued, after(q * FB + b + 1))
                        dve.tensor_tensor(hidden[b % 2][:], hidden[b % 2][:], ps_up_e[b % 2][:], ALU.mult
                                          ).then_inc(up_gated, 1)
                        dve.wait_ge(up_gated, after(q * FB + b + 1))
                        dve.wait_ge(comb_spread, after(q * FB + b + 1))
                        dve.tensor_tensor(hidden[b % 2][:], hidden[b % 2][:], ps_comb[b % 2][:], ALU.mult
                                          ).then_inc(weighted, 1)
                        if b == 0:
                            with dve.If(q > 0):
                                split_hidden(q * FB - 1, 1)
                        else:
                            split_hidden(q * FB + b - 1, (b - 1) % 2)
                        if b == 1:
                            with dve.If(q > 0):
                                add_group(nc.s_assert_within(
                                    q - 1, 0, GROUPS - 2, skip_runtime_bounds_check_because="within the If"))
                split_hidden(GROUPS * FB - 1, 1)
                add_group(GROUPS - 1)

            @block.tensor
            def _(pe):
                with pe.Fori(0, GROUPS) as q:
                    def project(b):
                        if b == 0:
                            pe.wait_ge(xe_ready, after(q + 1))
                        if b >= 2:
                            pe.wait_ge(up_gated, after(q * FB + b - 1))
                        pe.wait_ge(staged_out, staging.index(("w", b * 3 + 2)) + 1)
                        for ps, part in ((ps_gate_e, 0), (ps_up_e, 1)):
                            for k in range(KD):
                                w = slice(k * P, (k + 1) * P)
                                pe.matmul(ps[b % 2][:], w_main[b][:, part, w], xe_main[:, k, :], start=(k == 0), stop=False)
                                pe.matmul(ps[b % 2][:], w_main[b][:, part, w], xe_rest[:, k, :], start=False, stop=False)
                                last = pe.matmul(ps[b % 2][:], w_rest[b][:, part, w], xe_main[:, k, :],
                                                 start=False, stop=(k == KD - 1))
                        last.then_inc(projected, 1)

                    def turn_combs():
                        pe.wait_ge(comb_ready, after(q + 1))
                        waited(pe)
                        for t in range(TG):
                            last = pe.transpose(ps_comb[0][0:2 * EXPERTS, t * P:(t + 1) * P],
                                                comb_split[:, t].bitcast(F32).rearrange("p n r e -> p (n r e)"),
                                                ident[:])
                        last.then_inc(comb_transposed, 1)

                    def spread_combs(b):
                        if b == 0:
                            pe.wait_ge(comb_turned_ready, after(q + 1))
                            pe.wait_ge(staged_out, staging.index(("select", n_select - 1)) + 1)
                        if b >= 2:
                            pe.wait_ge(weighted, after(q * FB + b - 1))
                        half = slice(b // (FB // 2) * EXPERTS, (b // (FB // 2) + 1) * EXPERTS)
                        pe.matmul(ps_comb[b % 2][:], select[half, b % (FB // 2), :], comb_turned[half, :],
                                  start=True, stop=True
                                  ).then_inc(comb_spread, 1)

                    def down(b, q):
                        if b == 0:
                            pe.wait_ge(added, after(q * 2))
                        pe.wait_ge(h_ready, after(q * FB + b + 1))
                        for t in range(TG):
                            at = slice(t * P, (t + 1) * P)
                            for n, (h, w) in enumerate(((h_main, w_main), (h_main, w_rest), (h_rest, w_main))):
                                last = pe.matmul(ps_y[t], h[:, at], w[b][:, 2, :],
                                                 start=(b == 0 and n == 0 and t % 2 == 0),
                                                 stop=(b == FB - 1 and n == 2),
                                                 skip_group_check=True)
                        last.then_inc(downed, 1)

                    for b in range(FB):
                        project(b)
                        if b == 0:
                            turn_combs()
                        spread_combs(b)
                        if b < 2:
                            with pe.If(q > 0):
                                down(FB - 2 + b, q - 1)
                        else:
                            down(b - 2, q)
                down(FB - 2, GROUPS - 1)
                down(FB - 1, GROUPS - 1)


def after(n):
    return n + 1


CONV_ORDER = (4, 5, 0, 1, 2, 3)
CONV_STEPS = [(k, m) for part in (CONV_ORDER[:2], CONV_ORDER[2:]) for k in range(1, TAPS) for m in part]


def level_constants():
    import numpy as np

    at = np.arange(P)
    total = np.zeros((P, NL, P), np.float32)
    mask = np.zeros((P, NL, P), np.float32)
    for j, half in enumerate(LEVELS):
        block = at // (2 * half)
        second = at % (2 * half) >= half
        middle = block * 2 * half + half - 1
        k, tok = at[:, None], at[None, :]
        same = block[:, None] == block[None, :]
        after = same & second[None, :] & (k > middle[None, :]) & (k <= tok)
        before = same & ~second[None, :] & (k > tok) & (k <= middle[None, :])
        total[:, j, :] = after | before
        mask[:, j, :] = 0.25 * (same & ~second[:, None] & second[None, :])
    return total, mask


def kernel(x, ctx_2048, mask_BxS2_bk0, L0_attn_in_proj_w, L0_attn_conv_w, L0_attn_conv_b, L0_attn_dt_bias,
           L0_attn_A_log, L0_attn_D, L0_attn_norm_w, L0_attn_out_proj_w, L0_ffn_gate_weight,
           L0_ffn_gate_up_proj, L0_ffn_down_proj):
    import numpy as np
    import concourse.bacc as bacc
    from concourse.bass_utils import run_bass_kernel_spmd

    a = np.asarray
    total, mask = level_constants()
    gate_up = a(L0_ffn_gate_up_proj).reshape(EXPERTS, 2, EI, KD, P)
    gate, up = (gate_up[:, n].reshape(FB, P, KD, P).transpose(0, 3, 2, 1).reshape(FB, P, D) for n in range(2))
    down = a(L0_ffn_down_proj).transpose(0, 2, 1).reshape(FB, P, D)
    owner = np.arange(FEATURES // 2).reshape(1, FB // 2, P) // EI
    select = (owner == np.arange(2 * EXPERTS)[:, None, None] % (EXPERTS // 2)).astype(np.float32)
    select = select.reshape(2 * EXPERTS, FB // 2 * P)
    ctx = a(ctx_2048).reshape(TILES, TB, CTX, D)
    arrays = {
        "x": a(x).reshape(TOK, D),
        "ctx": ctx,
        "ctx_t": ctx.transpose(0, 1, 3, 2),
        "mask_t": a(mask_BxS2_bk0).T,
        "w_in": a(L0_attn_in_proj_w).T,
        "conv_w": a(L0_attn_conv_w).reshape(CONV, TAPS),
        "conv_b": a(L0_attn_conv_b).reshape(CB, P).T,
        "dt_bias": np.broadcast_to(a(L0_attn_dt_bias), (P, HEADS)),
        "a_log": np.broadcast_to(a(L0_attn_A_log), (P, HEADS)),
        "skip_d": np.broadcast_to(a(L0_attn_D), (P, HEADS)),
        "norm_w": a(L0_attn_norm_w).reshape(IB, P).T,
        "w_out": a(L0_attn_out_proj_w).T,
        "w_router": a(L0_ffn_gate_weight).T,
        "w_experts": np.stack([gate, up, down], axis=1).reshape(FB * 3, P, D),
        "c_before": np.broadcast_to(np.arange(-LAST, 1, dtype=np.float32)[None, :, None], (1, CHUNKS, TILES)),
        "c_ident": np.eye(P, dtype=np.float32),
        "c_sum": total,
        "c_mask": mask,
        "c_expert": np.broadcast_to(np.arange(EXPERTS, dtype=np.float32)[None, :, None], (P, EXPERTS, TOP)),
        "c_select": select,
    }
    arrays = {f"in_{k}": np.ascontiguousarray(v) for k, v in arrays.items()}
    nc = bacc.Bacc("TRN2", target_bir_lowering=False, num_devices=1)
    args = [nc.dram_tensor(k, v.shape, mybir.dt.from_np(v.dtype), kind="ExternalInput").ap()
            for k, v in arrays.items()]
    out = nc.dram_tensor("out_dram", (TOK, D), F32, kind="ExternalOutput").ap()
    build(nc, *args, out)
    r = run_bass_kernel_spmd(nc, [arrays], core_ids=[0])
    return r.results[0]["out_dram"].reshape(B, SEQ, D)
```
